# Optimizing a Trainium2 kernel written in Bass

```python
import numpy as np
import jax
import jax.numpy as jnp

def _softmax(x, axis=-1):
    return jax.nn.softmax(x, axis=axis)

def _gelu(x):
    return jax.nn.gelu(x, approximate=True)

def _silu(x):
    return jax.nn.silu(x)

def _sigmoid(x):
    return jax.nn.sigmoid(x)

def _layernorm(x, axis=-1, eps=1e-05):
    m = jnp.mean(x, axis=axis, keepdims=True)
    v = jnp.var(x, axis=axis, keepdims=True)
    return (x - m) / jnp.sqrt(v + eps)

def _scatter_add(tgt, idx, src, axis=0):
    return tgt.at[idx].add(src)

def _segment_sum(src, seg, n):
    return jax.ops.segment_sum(src, seg, n)
kernel_name = 'mk_hybrid_d1_jaxref_r8_468520'

def setup_inputs(seed: int=0):
    np.random.seed(seed)
    _w = jnp.asarray

    def _L0_attn_a_setup():
        import jax, jax.numpy as jnp
        import numpy as np
        EPS = 1e-05
        CHUNK = 128

        def lightning_attn(q, k, v, ld, chunk=CHUNK):
            b, n, h, d = q.shape
            nc = n // chunk
            idx = jnp.arange(chunk)
            diff = idx[:, None] - idx[None, :]
            mask = diff >= 0
            D = jnp.exp(ld[:, None, None] * jnp.where(mask, diff, 0)) * mask
            q_decay = jnp.exp(ld[None, :] * (idx + 1)[:, None])
            k_decay = jnp.exp(ld[None, :] * (chunk - 1 - idx)[:, None])
            chunk_decay = jnp.exp(ld * chunk)
            qc = jnp.moveaxis(q.reshape(b, nc, chunk, h, d), 1, 0)
            kc = jnp.moveaxis(k.reshape(b, nc, chunk, h, d), 1, 0)
            vc = jnp.moveaxis(v.reshape(b, nc, chunk, h, d), 1, 0)

            def step(S, inp):
                qb, kb, vb = inp
                scores = jnp.einsum('bchd,bshd->bhcs', qb, kb) * D[None]
                o_intra = jnp.einsum('bhcs,bshd->bchd', scores, vb)
                o_inter = jnp.einsum('bchd,bhde->bche', qb, S) * q_decay[None, :, :, None]
                S_new = chunk_decay[None, :, None, None] * S + jnp.einsum('bshd,bshe->bhde', kb * k_decay[None, :, :, None], vb)
                return (S_new, o_intra + o_inter)
            S0 = jnp.zeros((b, h, d, d), dtype=q.dtype)
            S_final, oc = jax.lax.scan(step, S0, (qc, kc, vc))
            out = jnp.moveaxis(oc, 0, 1).reshape(b, n, h, d)
            return (out, S_final)

        def group_rmsnorm_fused_gate(o, gate, w, num_heads):
            b, n, d = o.shape
            hd = d // num_heads
            o = o * jax.nn.sigmoid(gate)
            og = o.reshape(b, n, num_heads, hd)
            og = og * jax.lax.rsqrt(jnp.mean(og * og, axis=-1, keepdims=True) + EPS)
            return og.reshape(b, n, d) * w
        key = jax.random.key(seed)
        ks = jax.random.split(key, 10)
        B, N, D, H = (2, 512, 256, 16)
        HD = D // H
        s = 1.0 / np.sqrt(D)
        x = jax.random.normal(ks[0], (B, N, D), dtype=jnp.float32)
        log_decay = -jax.random.uniform(ks[1], (H,), dtype=jnp.float32, minval=0.01, maxval=1.0)
        Wq = jax.random.normal(ks[2], (D, D), dtype=jnp.float32) * s
        Wk = jax.random.normal(ks[3], (D, D), dtype=jnp.float32) * s
        Wv = jax.random.normal(ks[4], (D, D), dtype=jnp.float32) * s
        Wo = jax.random.normal(ks[5], (D, D), dtype=jnp.float32) * s
        Wg1 = jax.random.normal(ks[6], (D, HD), dtype=jnp.float32) * s
        Wg2 = jax.random.normal(ks[7], (HD, D), dtype=jnp.float32) / np.sqrt(HD)
        norm_w = jnp.ones((D,), dtype=jnp.float32)
        return {'x': x, 'log_decay': log_decay, 'Wq': Wq, 'Wk': Wk, 'Wv': Wv, 'Wo': Wo, 'Wg1': Wg1, 'Wg2': Wg2, 'norm_w': norm_w}
    _L0_attn_a_in = _L0_attn_a_setup()

    def _L0_attn_b_setup():
        import jax, jax.numpy as jnp
        import numpy as np
        B, T, C = (4, 256, 256)
        N, K = (16, 4)
        G, H = (N // K, C // N)

        def _rmsnorm(x):
            var = jnp.mean(jnp.square(x.astype(jnp.float32)), axis=-1, keepdims=True)
            return (x * jax.lax.rsqrt(var + 1e-06)).astype(x.dtype)

        def _sine_table(features, length, max_timescale=10000.0):
            fraction = jnp.arange(0, features, 2, dtype=jnp.float32) / features
            timescale = max_timescale ** fraction
            sinusoid = jnp.einsum('i,j->ij', jnp.arange(length).astype(jnp.float32), 1.0 / timescale, precision=jax.lax.Precision.HIGHEST)
            sinusoid = jnp.concatenate([sinusoid, sinusoid], axis=-1)
            return (jnp.sin(sinusoid), jnp.cos(sinusoid))

        def _rotate_half(x):
            x1, x2 = jnp.split(x, 2, axis=-1)
            return jnp.concatenate([-x2, x1], axis=-1)
        key = jax.random.key(seed)
        kx, kq, kk, kv, ko = jax.random.split(key, 5)
        q_std = float(np.sqrt(2.0 / (5.0 * C)))
        o_std = 2.0 / 24 / float(np.sqrt(N * H))
        return {'x': jax.random.normal(kx, (B, T, C), dtype=jnp.float32), 'Wq': jax.random.normal(kq, (C, N * H), dtype=jnp.float32) * q_std, 'Wk': jax.random.normal(kk, (C, K * H), dtype=jnp.float32) * q_std, 'Wv': jax.random.normal(kv, (C, K * H), dtype=jnp.float32) * q_std, 'Wout': jax.random.normal(ko, (N * H, C), dtype=jnp.float32) * o_std}
    _L0_attn_b_in = _L0_attn_b_setup()

    def _L0_ffn_setup():
        import jax, jax.numpy as jnp
        import numpy as np
        NUM_EXPERTS = 32
        TOP_K = 8
        THRESHOLD = 0.8
        HIDDEN = 256
        INTER = 96
        key = jax.random.key(seed)
        k1, k2, k3, k4 = jax.random.split(key, 4)
        hidden_states = jax.random.normal(k1, (2, 128, HIDDEN), jnp.float32)
        gate_weight = jax.random.normal(k2, (NUM_EXPERTS, HIDDEN), jnp.float32) * 0.02
        gate_up_proj = jax.random.normal(k3, (NUM_EXPERTS, 2 * INTER, HIDDEN), jnp.float32) * 0.02
        down_proj = jax.random.normal(k4, (NUM_EXPERTS, HIDDEN, INTER), jnp.float32) * 0.02
        return {'hidden_states': hidden_states, 'gate_weight': gate_weight, 'gate_up_proj': gate_up_proj, 'down_proj': down_proj}
    _L0_ffn_in = _L0_ffn_setup()
    _d = {'L0_attn_a_x': _L0_attn_a_in['x'], 'L0_attn_a_log_decay': _L0_attn_a_in['log_decay'], 'L0_attn_a_Wq': _L0_attn_a_in['Wq'], 'L0_attn_a_Wk': _L0_attn_a_in['Wk'], 'L0_attn_a_Wv': _L0_attn_a_in['Wv'], 'L0_attn_a_Wo': _L0_attn_a_in['Wo'], 'L0_attn_a_Wg1': _L0_attn_a_in['Wg1'], 'L0_attn_a_Wg2': _L0_attn_a_in['Wg2'], 'L0_attn_a_norm_w': _L0_attn_a_in['norm_w'], 'L0_attn_b_Wq': _L0_attn_b_in['Wq'], 'L0_attn_b_Wk': _L0_attn_b_in['Wk'], 'L0_attn_b_Wv': _L0_attn_b_in['Wv'], 'L0_attn_b_Wout': _L0_attn_b_in['Wout'], 'L0_ffn_gate_weight': _L0_ffn_in['gate_weight'], 'L0_ffn_gate_up_proj': _L0_ffn_in['gate_up_proj'], 'L0_ffn_down_proj': _L0_ffn_in['down_proj']}
    _x0 = _d['L0_attn_a_x']
    _d['L0_attn_a_x'] = jax.random.normal(jax.random.fold_in(jax.random.key(seed), 1), (4, 512, 256), dtype=_x0.dtype)
    del _x0
    return _d

def reference(L0_attn_a_x, L0_attn_a_log_decay, L0_attn_a_Wq, L0_attn_a_Wk, L0_attn_a_Wv, L0_attn_a_Wo, L0_attn_a_Wg1, L0_attn_a_Wg2, L0_attn_a_norm_w, L0_attn_b_Wq, L0_attn_b_Wk, L0_attn_b_Wv, L0_attn_b_Wout, L0_ffn_gate_weight, L0_ffn_gate_up_proj, L0_ffn_down_proj):

    def _L0_attn_a_ref(x, log_decay, Wq, Wk, Wv, Wo, Wg1, Wg2, norm_w):
        import jax, jax.numpy as jnp
        import numpy as np
        EPS = 1e-05
        CHUNK = 128

        def lightning_attn(q, k, v, ld, chunk=CHUNK):
            b, n, h, d = q.shape
            nc = n // chunk
            idx = jnp.arange(chunk)
            diff = idx[:, None] - idx[None, :]
            mask = diff >= 0
            D = jnp.exp(ld[:, None, None] * jnp.where(mask, diff, 0)) * mask
            q_decay = jnp.exp(ld[None, :] * (idx + 1)[:, None])
            k_decay = jnp.exp(ld[None, :] * (chunk - 1 - idx)[:, None])
            chunk_decay = jnp.exp(ld * chunk)
            qc = jnp.moveaxis(q.reshape(b, nc, chunk, h, d), 1, 0)
            kc = jnp.moveaxis(k.reshape(b, nc, chunk, h, d), 1, 0)
            vc = jnp.moveaxis(v.reshape(b, nc, chunk, h, d), 1, 0)

            def step(S, inp):
                qb, kb, vb = inp
                scores = jnp.einsum('bchd,bshd->bhcs', qb, kb) * D[None]
                o_intra = jnp.einsum('bhcs,bshd->bchd', scores, vb)
                o_inter = jnp.einsum('bchd,bhde->bche', qb, S) * q_decay[None, :, :, None]
                S_new = chunk_decay[None, :, None, None] * S + jnp.einsum('bshd,bshe->bhde', kb * k_decay[None, :, :, None], vb)
                return (S_new, o_intra + o_inter)
            S0 = jnp.zeros((b, h, d, d), dtype=q.dtype)
            S_final, oc = jax.lax.scan(step, S0, (qc, kc, vc))
            out = jnp.moveaxis(oc, 0, 1).reshape(b, n, h, d)
            return (out, S_final)

        def group_rmsnorm_fused_gate(o, gate, w, num_heads):
            b, n, d = o.shape
            hd = d // num_heads
            o = o * jax.nn.sigmoid(gate)
            og = o.reshape(b, n, num_heads, hd)
            og = og * jax.lax.rsqrt(jnp.mean(og * og, axis=-1, keepdims=True) + EPS)
            return og.reshape(b, n, d) * w
        b, n, d = x.shape
        H = log_decay.shape[0]
        hd = d // H
        q = jax.nn.silu(jnp.einsum('bnd,de->bne', x, Wq).reshape(b, n, H, hd))
        k = jax.nn.silu(jnp.einsum('bnd,de->bne', x, Wk).reshape(b, n, H, hd))
        v = jax.nn.silu(jnp.einsum('bnd,de->bne', x, Wv).reshape(b, n, H, hd))
        o, _ = lightning_attn(q, k, v, log_decay)
        o = o.reshape(b, n, d)
        gate = jnp.einsum('bnk,kd->bnd', jnp.einsum('bnd,dk->bnk', x, Wg1), Wg2)
        o = group_rmsnorm_fused_gate(o, gate, norm_w, H)
        return jnp.einsum('bnd,de->bne', o, Wo)

    def _L0_attn_b_ref(x, Wq, Wk, Wv, Wout):
        import jax, jax.numpy as jnp
        import numpy as np
        B, T, C = (4, 256, 256)
        N, K = (16, 4)
        G, H = (N // K, C // N)

        def _rmsnorm(x):
            var = jnp.mean(jnp.square(x.astype(jnp.float32)), axis=-1, keepdims=True)
            return (x * jax.lax.rsqrt(var + 1e-06)).astype(x.dtype)

        def _sine_table(features, length, max_timescale=10000.0):
            fraction = jnp.arange(0, features, 2, dtype=jnp.float32) / features
            timescale = max_timescale ** fraction
            sinusoid = jnp.einsum('i,j->ij', jnp.arange(length).astype(jnp.float32), 1.0 / timescale, precision=jax.lax.Precision.HIGHEST)
            sinusoid = jnp.concatenate([sinusoid, sinusoid], axis=-1)
            return (jnp.sin(sinusoid), jnp.cos(sinusoid))

        def _rotate_half(x):
            x1, x2 = jnp.split(x, 2, axis=-1)
            return jnp.concatenate([-x2, x1], axis=-1)
        b, t, c = x.shape
        q = _rmsnorm(x @ Wq)
        k = _rmsnorm(x @ Wk)
        v = x @ Wv
        q = q.reshape(b, t, K, G, H)
        k = k.reshape(b, t, K, H)
        v = v.reshape(b, t, K, H)
        sin, cos = _sine_table(H, t)
        qcos, qsin = (cos[None, :, None, None, :], sin[None, :, None, None, :])
        kcos, ksin = (cos[None, :, None, :], sin[None, :, None, :])
        q = (q * qcos + _rotate_half(q) * qsin).astype(q.dtype)
        k = (k * kcos + _rotate_half(k) * ksin).astype(k.dtype)
        scale = jax.lax.rsqrt(jnp.array(H, dtype=jnp.float32)).astype(q.dtype)
        q = q * scale
        logits = jnp.einsum('btkgh,bskh->bkgts', q, k)
        probs = jax.nn.softmax(logits.astype(jnp.float32), axis=-1).astype(logits.dtype)
        enc = jnp.einsum('bkgts,bskh->btkgh', probs, v)
        return enc.reshape(b, t, N * H) @ Wout

    def _L0_ffn_ref(hidden_states, gate_weight, gate_up_proj, down_proj):
        import jax, jax.numpy as jnp
        import numpy as np
        NUM_EXPERTS = 32
        TOP_K = 8
        THRESHOLD = 0.8
        HIDDEN = 256
        INTER = 96
        B, S, H = hidden_states.shape
        x = hidden_states.reshape(-1, H)
        logits = x @ gate_weight.T
        probs = jax.nn.softmax(logits.astype(jnp.float32), axis=-1).astype(logits.dtype)
        top_vals, top_idx = jax.lax.top_k(probs, TOP_K)
        renorm = top_vals / jnp.clip(jnp.sum(top_vals, axis=-1, keepdims=True), 1e-12)
        cum = jnp.cumsum(renorm, axis=-1)
        num_keep = jnp.minimum(jnp.sum((cum < THRESHOLD).astype(jnp.int32), axis=-1) + 1, TOP_K)
        active = jnp.arange(TOP_K)[None, :] < num_keep[:, None]
        rw = top_vals * active.astype(top_vals.dtype)
        rw = rw / jnp.clip(jnp.sum(rw, axis=-1, keepdims=True), 1e-12)
        combine = jnp.sum(jax.nn.one_hot(top_idx, NUM_EXPERTS, dtype=rw.dtype) * rw[..., None], axis=1)

        def body(acc, params):
            w_gu, w_d, ce = params
            gu = x @ w_gu.T
            g, u = jnp.split(gu, 2, axis=-1)
            h = jax.nn.silu(g) * u
            return (acc + h @ w_d.T * ce[:, None], None)
        out, _ = jax.lax.scan(body, jnp.zeros_like(x), (gate_up_proj, down_proj, combine.T))
        return out.reshape(B, S, H)
    x = L0_attn_a_x
    x = x + _L0_attn_a_ref(_layernorm(x, axis=-1), L0_attn_a_log_decay, L0_attn_a_Wq, L0_attn_a_Wk, L0_attn_a_Wv, L0_attn_a_Wo, L0_attn_a_Wg1, L0_attn_a_Wg2, L0_attn_a_norm_w)
    x = x + _L0_ffn_ref(_layernorm(x, axis=-1), L0_ffn_gate_weight, L0_ffn_gate_up_proj, L0_ffn_down_proj)
    x = x + _L0_attn_b_ref(_layernorm(x, axis=-1), L0_attn_b_Wq, L0_attn_b_Wk, L0_attn_b_Wv, L0_attn_b_Wout)
    x = x + _L0_ffn_ref(_layernorm(x, axis=-1), L0_ffn_gate_weight, L0_ffn_gate_up_proj, L0_ffn_down_proj)
    return x

_drawn_inputs = setup_inputs


def setup_inputs(seed=0):
    import zlib

    import numpy as np

    out = dict(_drawn_inputs(seed))
    spreads = {'L0_attn_a_norm_w': (1.0, 0.2)}
    factors = {'L0_attn_b_Wq': 8.0,
     'L0_attn_b_Wk': 8.0,
     'L0_attn_b_Wv': 4.704,
     'L0_attn_b_Wout': 4.678,
     'L0_ffn_gate_weight': 8.0,
     'L0_ffn_gate_up_proj': 8.0,
     'L0_ffn_down_proj': 8.0}
    for name, (base, spread) in spreads.items():
        noise = np.random.default_rng([zlib.crc32(name.encode()), seed]).standard_normal(out[name].shape)
        drawn = base * np.exp(spread * noise) if base else spread * noise
        out[name] = jnp.asarray(drawn.astype(out[name].dtype))
    for name, factor in factors.items():
        out[name] = (out[name] * factor).astype(out[name].dtype)
    return out
```

```python
from contextlib import ExitStack, contextmanager

import concourse.bass as bass
import numpy as np
from concourse import mybir

F32 = mybir.dt.float32
F32R = mybir.dt.float32r
BF16 = mybir.dt.bfloat16
U16 = mybir.dt.uint16
ALU = mybir.AluOpType
ACT = mybir.ActivationFunctionType
AX = mybir.AxisListType

P = 128
B, N, D = 4, 512, 256
TT = N // P
NT = B * TT
KD = D // P
H, HD = 16, 16
KV = 4
G = H // KV
PAD = 32
E, TOPK, KEEP = 32, 8, 0.8
INTER = 96
HT = E * INTER // P
QKV = D + 2 * KV * HD
PASSES = (("hi", "hi"), ("hi", "lo"), ("lo", "hi"))


def chunks(n, step):
    return [(i, min(step, n - i)) for i in range(0, n, step)]


@contextmanager
def signals(nc):
    given = []

    def sem(name):
        given.append(nc.alloc_semaphore(name))
        return given[-1]

    yield sem
    nc.clear_and_free_semaphores(given)
    nc.all_engine_barrier()


class Steps:

    def __init__(self, eng, sem, base=0):
        self.eng, self.sem, self.base, self.n = eng, sem, base, 0

    def __call__(self, ins):
        ins.then_inc(self.sem, 1)
        self.n += 1

    def settle(self):
        self.eng.wait_ge(self.sem, self.base + self.n)


class Parts:

    def __init__(self, hi, lo):
        self.hi, self.lo = hi, lo

    def __getitem__(self, i):
        return Parts(self.hi[i], self.lo[i])


def product(nc, out, stationary, moving, start, stop):
    pairs = [(s, m, sp, mp) for s, m in zip(stationary, moving) for sp, mp in PASSES]
    for i, (s, m, sp, mp) in enumerate(pairs):
        last = nc.tensor.matmul(out, s.hi if sp == "hi" else s.lo, m.hi if mp == "hi" else m.lo,
                                start=start and i == 0, stop=stop and i == len(pairs) - 1,
                                skip_group_check=True)
    return last


LN_STEPS = 2 * TT + 2


class Norm:

    def __init__(self, nc, ctx, signal, name, xn):
        def sb(n, shape):
            return ctx.enter_context(nc.sbuf_tensor(f"{name}_{n}", shape, F32))

        def sem(n):
            return signal(f"{name}_{n}")

        self.nc, self.xn = nc, xn
        self.stats = sb("stats", [P, TT, 6])
        self.mean_var = sb("mean_var", [P, TT, 2])
        self.eps = sb("eps", [P, TT])
        self.var_eps = sb("var_eps", [P, TT])
        self.std = sb("std", [P, TT])
        self.rstd = sb("rstd", [P, TT])
        self.var_ready, self.std_ready = sem("var_ready"), sem("std_ready")
        self.xn_ready, self.turned = sem("xn_ready"), sem("turned")
        self.hi_ready, self.lo_ready = sem("hi_ready"), sem("lo_ready")

    def vector(self, eng, steps, b, x, xt, banks):
        nc = self.nc
        for t in range(TT):
            steps(nc.vector.bn_stats(self.stats[:, t, :], x[:, t, :]))
        steps.settle()
        steps(nc.vector.memset(self.eps[:, :], 1e-5))
        for t in range(TT):
            steps(nc.vector.bn_aggr(self.mean_var[:, t, :], self.stats[:, t, :]))
        steps.settle()
        nc.vector.tensor_tensor(self.var_eps[:, :], self.mean_var[:, :, 1], self.eps[:, :],
                                ALU.add).then_inc(self.var_ready, 1)
        eng.wait_ge(self.std_ready, b + 1)
        steps(nc.vector.reciprocal(self.rstd[:, :], self.std[:, :]))
        steps.settle()
        for t in range(TT):
            nc.vector.tensor_scalar(self.xn[:, t, :], x[:, t, :], self.mean_var[:, t, 0:1],
                                    self.rstd[:, t:t + 1], ALU.subtract, ALU.mult).then_inc(self.xn_ready, 1)
        self.low_part(eng, b, xt, banks)

    def low_part(self, eng, b, xt, banks):
        for k in range(KD):
            eng.wait_ge(self.hi_ready, KD * b + k + 1)
            self.nc.vector.tensor_tensor(xt.lo[:, k, :], banks[:, k, :], xt.hi[:, k, :].bitcast(F32),
                                         ALU.subtract).then_inc(self.lo_ready, 1)

    def scalar(self, eng, b, xt, banks):
        nc = self.nc
        eng.wait_ge(self.var_ready, b + 1)
        nc.scalar.activation(self.std[:, :], self.var_eps[:, :], ACT.Sqrt).then_inc(self.std_ready, 1)
        self.high_part(eng, b, xt, banks)

    def high_part(self, eng, b, xt, banks):
        for k in range(KD):
            eng.wait_ge(self.turned, KD * b + k + 1)
            self.nc.scalar.copy(xt.hi[:, k, :], banks[:, k, :]).then_inc(self.hi_ready, 1)

    def tensor(self, eng, b, ident, banks):
        for t in range(TT):
            eng.wait_ge(self.xn_ready, TT * b + t + 1)
            for k in range(KD):
                ins = self.nc.tensor.transpose(banks[:, k, t * P:(t + 1) * P],
                                               self.xn[:, t, k * P:(k + 1) * P], ident[:, :])
                if t == TT - 1:
                    ins.then_inc(self.turned, 1)

    def wait_parts(self, eng, b):
        eng.wait_ge(self.hi_ready, KD * (b + 1))
        eng.wait_ge(self.lo_ready, KD * (b + 1))


def split_weights(nc, name, jobs):
    STAGES, WIDTH = 4, 1024
    pieces = [(src[:, o:o + n], dst[:, o:o + n]) for src, dst in jobs for o, n in chunks(src.shape[1], WIDTH)]
    with ExitStack() as ctx:
        signal = ctx.enter_context(signals(nc))
        stage = ctx.enter_context(nc.sbuf_tensor(f"{name}_stage", [P, STAGES, WIDTH], F32))
        loaded = [signal(f"{name}_loaded{i}") for i in range(STAGES)]
        hi_done = signal(f"{name}_hi_done")
        lo_done = signal(f"{name}_lo_done")
        block = ctx.enter_context(nc.Block())

        @block.sync
        def _(sp):
            for i, (src, dst) in enumerate(pieces):
                if i >= STAGES:
                    sp.wait_ge(lo_done, i - STAGES + 1)
                sp.dma_start(stage[:, i % STAGES, 0:src.shape[1]], src).then_inc(loaded[i % STAGES], 16)

        @block.scalar
        def _(act):
            for i, (src, dst) in enumerate(pieces):
                act.wait_ge(loaded[i % STAGES], 16 * (i // STAGES + 1))
                nc.scalar.copy(dst.hi, stage[:, i % STAGES, 0:src.shape[1]]).then_inc(hi_done, 1)

        @block.vector
        def _(dve):
            for i, (src, dst) in enumerate(pieces):
                dve.wait_ge(hi_done, i + 1)
                nc.vector.tensor_tensor(dst.lo, stage[:, i % STAGES, 0:src.shape[1]], dst.hi.bitcast(F32),
                                        ALU.subtract).then_inc(lo_done, 1)


def lightning(nc, X, ident, ps, d):
    HH = H // KD
    QUADS = H // 4
    with ExitStack() as ctx:
        signal = ctx.enter_context(signals(nc))

        def sb(n, shape, dt=F32):
            return ctx.enter_context(nc.sbuf_tensor(f"a_{n}", shape, dt))

        def sem(n):
            return signal(f"a_{n}")

        def parts(n, shape):
            return Parts(sb(n + "_hi", shape, F32R), sb(n + "_lo", shape, F32R))

        w_qkv = parts("w_qkv", [P, KD * 3 * D])
        w_o = parts("w_o", [P, KD * D])
        w_g1 = parts("w_g1", [P, KD * P])
        w_g2 = sb("w_g2", [P, D])
        norm_w = sb("norm_w", [P, D])
        ld_heads = sb("ld_heads", [P, H])
        ld_rows = sb("ld_rows", [P, KD])
        gap = sb("gap", [P, P])
        causal = sb("causal", [P, P])
        ahead = sb("ahead", [P, P])
        left = sb("left", [P, 1])
        head_rows = sb("head_rows", [P, HH])
        diagonal = sb("diagonal", [P, HH * PAD])
        decay = sb("decay", [P, H, P])
        q_decay = sb("q_decay", [P, KD, P])
        k_decay = sb("k_decay", [P, H])
        k_left = sb("k_left", [P, H])
        chunk_decay = sb("chunk_decay", [P, KD])

        split_weights(nc, "a_w", [(d["Wqkv"], w_qkv), (d["Wo"], w_o), (d["Wg1"], w_g1)])

        with ExitStack() as sub:
            signal = sub.enter_context(signals(nc))
            loaded = signal("a_const_loaded")
            raw = signal("a_decay_raw")
            kl = signal("a_k_left_done")
            done = signal("a_decay_done")
            block = sub.enter_context(nc.Block())
            loads = [(w_g2, d["Wg2"]), (norm_w, d["norm_w"]), (ld_heads, d["ld_heads"]), (ld_rows, d["ld_rows"]),
                     (gap, d["gap"]), (causal, d["causal"]), (ahead, d["ahead"]), (left, d["left"]),
                     (head_rows, d["head_rows"]), (diagonal, d["diagonal"])]

            @block.sync
            def _(sp):
                for dst, src in loads:
                    sp.dma_start(dst[:, :], src).then_inc(loaded, 16)

            @block.scalar
            def _(act):
                act.wait_ge(loaded, 16 * len(loads))
                for h in range(H):
                    nc.scalar.activation(decay[:, h, :], gap[:, :], ACT.Exp,
                                         scale=ld_heads[:, h:h + 1]).then_inc(raw, 1)
                for m in range(KD):
                    nc.scalar.activation(q_decay[:, m, :], ahead[:, :], ACT.Exp, scale=ld_rows[:, m:m + 1])
                act.wait_ge(kl, 1)
                nc.scalar.activation(k_decay[:, :], k_left[:, :], ACT.Exp)
                nc.scalar.activation(chunk_decay[:, :], ld_rows[:, :], ACT.Exp, scale=float(P))

            @block.vector
            def _(dve):
                dve.wait_ge(loaded, 16 * len(loads))
                nc.vector.tensor_scalar(k_left[:, :], ld_heads[:, :], left[:, 0:1], None, ALU.mult).then_inc(kl, 1)
                for h in range(H):
                    dve.wait_ge(raw, h + 1)
                    nc.vector.tensor_tensor(decay[:, h, :], decay[:, h, :], causal[:, :],
                                            ALU.mult).then_inc(done, 1)

        xn = sb("xn", [P, TT, D])
        xt = parts("xt", [P, KD, N])
        q_t = sb("q_t", [P, KD, N])
        k_t = sb("k_t", [P, KD, N])
        k_tok = sb("k_tok", [P, TT, D])
        v_pad = sb("v_pad", [P, TT, H, PAD])
        g1 = sb("g1", [P, N])
        gate = sb("gate", [P, TT, D])
        k_dec = sb("k_dec", [P, 2, D])
        q_dec = sb("q_dec", [P, 2, KD, P])
        q_mask = sb("q_mask", [P, 2, 4, P])
        weights = sb("weights", [P, 2, 4, P])
        state = sb("state", [P, KD, HH * PAD])
        outer = sb("outer", [P, KD, HH * PAD])
        o_t = sb("o_t", [P, 2, N])
        og = sb("og", [P, TT, D])
        sq = sb("sq", [P, TT, D])
        ss = sb("ss", [P, TT * H])
        ms = sb("ms", [P, TT * H])
        rms = sb("rms", [P, TT * H])
        rrms = sb("rrms", [P, TT * H])

        norm = Norm(nc, ctx, signal, "a_ln", xn)
        again = Norm(nc, ctx, signal, "a_og", og)
        vec = sem("vec")
        batch_done = sem("batch_done")
        v_zero = sem("v_zero")
        qk_ready, qk_sb = sem("qk_ready"), sem("qk_sb")
        kv_ready, kv_sb = sem("kv_ready"), sem("kv_sb")
        g1_ready, g1_sb = sem("g1_ready"), sem("g1_sb")
        gate_ready, gate_sb = sem("gate_ready"), sem("gate_sb")
        dec_ready, mask_ready = sem("dec_ready"), sem("mask_ready")
        score_ready, weight_ready = sem("score_ready"), sem("weight_ready")
        outer_ready, outer_masked, state_ready = sem("outer_ready"), sem("outer_masked"), sem("state_ready")
        o_ready, o_sb, o_turned, og_ready = sem("o_ready"), sem("o_sb"), sem("o_turned"), sem("og_ready")
        ms_ready, rms_ready, y_ready = sem("ms_ready"), sem("rms_ready"), sem("y_ready")
        QB = H // 4 * TT
        VEC = LN_STEPS + 5

        wqkv = Parts(*(w.rearrange("p (k n) -> p k n", k=KD) for w in (w_qkv.hi[:, :], w_qkv.lo[:, :])))
        wo = Parts(*(w.rearrange("p (k n) -> p k n", k=KD) for w in (w_o.hi[:, :], w_o.lo[:, :])))
        wg1 = Parts(*(w.rearrange("p (k n) -> p k n", k=KD) for w in (w_g1.hi[:, :], w_g1.lo[:, :])))
        bank_s, bank_o, bank_kv = 4, 6, 7

        block = ctx.enter_context(nc.Block())

        @block.tensor
        def _(pe):
            with pe.Fori(0, B) as b:
                pe.wait_ge(batch_done, b)
                norm.tensor(pe, b, ident, ps[:, 4:6, :])
                norm.wait_parts(pe, b)
                for i in range(2 * KD):
                    product(nc, ps[:, i, :], [wqkv[:, k, i * P:(i + 1) * P] for k in range(KD)],
                            [xt[:, k, :] for k in range(KD)], True, True).then_inc(qk_ready, 1)
                for t in range(TT):
                    product(nc, ps[:, 4 + t, :], [xt[:, k, t * P:(t + 1) * P] for k in range(KD)],
                            [wqkv[:, k, D:3 * D] for k in range(KD)], True, True).then_inc(kv_ready, 1)
                pe.wait_ge(qk_sb, 2 * KD * b + 1)
                product(nc, ps[:, 0, :], [wg1[:, k, :] for k in range(KD)], [xt[:, k, :] for k in range(KD)],
                        True, True).then_inc(g1_ready, 1)
                pe.wait_ge(qk_sb, 2 * KD * b + 3)
                pe.wait_ge(g1_sb, b + 1)
                for t in range(TT):
                    ins = nc.tensor.matmul(ps[:, 1 + t // 2, (t % 2) * D:(t % 2 + 1) * D],
                                           g1[:, t * P:(t + 1) * P], w_g2[:, :], start=True, stop=True)
                ins.then_inc(gate_ready, 1)
                pe.wait_ge(qk_sb, 2 * KD * (b + 1))
                pe.wait_ge(kv_sb, TT * (b + 1))
                pe.wait_ge(gate_sb, b + 1)

                def turn_output(n):
                    pe.wait_ge(o_sb, TT * b + n + 1)
                    for q in range(QUADS):
                        ins = nc.tensor.transpose(ps[:, n, q * P:(q + 1) * P], o_t[:, n % 2, q * P:(q + 1) * P],
                                                  ident[:, :])
                    ins.then_inc(o_turned, 1)

                def scores(i):
                    n, q = i // QUADS, i % QUADS
                    pe.wait_ge(mask_ready, QB * b + i + 1)
                    if i >= 2:
                        pe.wait_ge(weight_ready, QB * b + i - 1)
                    nc.tensor.matmul(ps[:, bank_s + q % 2, :], k_t[:, q // 2, n * P:(n + 1) * P],
                                     q_mask[:, q % 2, :, :], start=True, stop=True).then_inc(score_ready, 1)

                def outer_product(n):
                    pe.wait_ge(dec_ready, 2 * (TT * b + n) + 1)
                    if n >= 1:
                        pe.wait_ge(outer_masked, (TT - 1) * b + n)
                    for m in range(KD):
                        ins = nc.tensor.matmul(ps[:, bank_kv, m * HH * PAD:(m + 1) * HH * PAD],
                                               k_dec[:, n % 2, m * P:(m + 1) * P],
                                               v_pad[:, n, m * HH:(m + 1) * HH, :], start=True, stop=True)
                    ins.then_inc(outer_ready, 1)

                def output(i):
                    n, q = i // QUADS, i % QUADS
                    if q == 0 and n >= 1:
                        pe.wait_ge(o_sb, TT * b + n)
                        turn_output(n - 1)
                        pe.wait_ge(state_ready, (TT - 1) * b + n)
                        pe.wait_ge(dec_ready, 2 * (TT * b + n + 1))
                    out = ps[:, bank_o, q * P:(q + 1) * P]
                    if n >= 1:
                        nc.tensor.matmul(out, state[:, q // 2, (q % 2) * P:(q % 2 + 1) * P],
                                         q_dec[:, n % 2, q // 2, :], start=(q == 0), stop=False,
                                         skip_group_check=True)
                    pe.wait_ge(weight_ready, QB * b + i + 1)
                    for j in range(4):
                        ins = nc.tensor.matmul(out[j * PAD:(j + 1) * PAD, :], v_pad[:, n, 4 * q + j, :],
                                               weights[:, q % 2, j, :], start=(q == 0 and n == 0), stop=True,
                                               skip_group_check=True)
                    if q == QUADS - 1:
                        ins.then_inc(o_ready, 1)

                for i in range(QB + 1):
                    if i < QB:
                        scores(i)
                        if i % QUADS == 1 and i // QUADS < TT - 1:
                            outer_product(i // QUADS)
                    if i >= 1:
                        output(i - 1)
                turn_output(TT - 1)
                again.tensor(pe, b, ident, ps[:, 4:6, :])
                again.wait_parts(pe, b)
                pe.wait_ge(o_sb, TT * (b + 1))
                for t in range(TT):
                    ins = product(nc, ps[:, 6 + t // 2, (t % 2) * D:(t % 2 + 1) * D],
                                  [xt[:, k, t * P:(t + 1) * P] for k in range(KD)],
                                  [wo[:, k, :] for k in range(KD)], True, True)
                ins.then_inc(y_ready, 1)

        @block.scalar
        def _(act):
            with act.Fori(0, B) as b:
                act.wait_ge(batch_done, b)
                norm.scalar(act, b, xt, ps[:, 4:6, :])
                act.wait_ge(v_zero, 1)
                for i in range(2 * KD):
                    act.wait_ge(qk_ready, 2 * KD * b + i + 1)
                    dst = q_t if i < KD else k_t
                    nc.scalar.activation(dst[:, i % KD, :], ps[:, i, :], ACT.Silu).then_inc(qk_sb, 1)
                act.wait_ge(g1_ready, b + 1)
                nc.scalar.copy(g1[:, :], ps[:, 0, :]).then_inc(g1_sb, 1)
                for t in range(TT):
                    act.wait_ge(kv_ready, TT * b + t + 1)
                    nc.scalar.activation(k_tok[:, t, :], ps[:, 4 + t, 0:D], ACT.Silu)
                    nc.scalar.activation(v_pad[:, t, :, 0:HD],
                                         ps[:, 4 + t, D:2 * D].rearrange("p (h e) -> p h e", e=HD),
                                         ACT.Silu).then_inc(kv_sb, 1)
                act.wait_ge(gate_ready, b + 1)
                nc.scalar.activation(gate[:, :, :].rearrange("p t n -> p (t n)"),
                                     ps[:, 1:3, :].rearrange("p t n -> p (t n)"), ACT.Sigmoid).then_inc(gate_sb, 1)
                for n in range(TT):
                    act.wait_ge(o_ready, TT * b + n + 1)
                    if n >= 2:
                        act.wait_ge(o_turned, TT * b + n - 1)
                    nc.scalar.copy(o_t[:, n % 2, :], ps[:, bank_o, :]).then_inc(o_sb, 1)
                act.wait_ge(ms_ready, b + 1)
                nc.scalar.activation(rms[:, :], ms[:, :], ACT.Sqrt).then_inc(rms_ready, 1)
                again.high_part(act, b, xt, ps[:, 4:6, :])

        @block.gpsimd
        def _(pool):
            with pool.Fori(0, B) as b:
                pool.wait_ge(qk_sb, 2 * KD * (b + 1))
                for i in range(QB):
                    n, q = i // QUADS, i % QUADS
                    if i >= 2:
                        pool.wait_ge(score_ready, QB * b + i - 1)
                    src = q_t[:, q // 2, n * P:(n + 1) * P][:, None, :].broadcast_to([P, 4, P])
                    rows = head_rows[:, (q % 2) * 4:(q % 2) * 4 + 4][:, :, None].broadcast_to([P, 4, P])
                    nc.gpsimd.tensor_tensor(q_mask[:, q % 2, :, :], src, rows, ALU.mult).then_inc(mask_ready, 1)

        @block.vector
        def _(dve):
            nc.vector.memset(v_pad[:, :, :, :], 0.0).then_inc(v_zero, 1)
            with dve.Fori(0, B) as b:
                steps = Steps(dve, vec, b * VEC)
                x = X[:, bass.ds(b * TT, TT), :]
                dve.wait_ge(batch_done, b)
                norm.vector(dve, steps, b, x, xt, ps[:, 4:6, :])
                dve.wait_ge(kv_sb, TT * (b + 1))
                for n in range(TT):
                    cols = slice(n * P, (n + 1) * P)
                    if n >= 2:
                        dve.wait_ge(o_ready, TT * b + n - 1)
                    nc.vector.tensor_tensor(k_dec[:, n % 2, :].rearrange("p (h e) -> p h e", e=HD),
                                            k_tok[:, n, :].rearrange("p (h e) -> p h e", e=HD),
                                            k_decay[:, :, None].broadcast_to([P, H, HD]),
                                            ALU.mult).then_inc(dec_ready, 1)
                    nc.vector.tensor_tensor(q_dec[:, n % 2, :, :], q_t[:, :, cols], q_decay[:, :, :],
                                            ALU.mult).then_inc(dec_ready, 1)
                    for q in range(QUADS):
                        i = QUADS * n + q
                        dve.wait_ge(score_ready, QB * b + i + 1)
                        nc.vector.tensor_tensor(weights[:, q % 2, :, :],
                                                ps[:, bank_s + q % 2, :].rearrange("p (j c) -> p j c", j=4),
                                                decay[:, 4 * q:4 * q + 4, :], ALU.mult).then_inc(weight_ready, 1)
                        if q == 2 and n < TT - 1:
                            dve.wait_ge(outer_ready, (TT - 1) * b + n + 1)
                            if n >= 1:
                                dve.wait_ge(state_ready, (TT - 1) * b + n)
                            nc.vector.tensor_tensor(outer[:, :, :],
                                                    ps[:, bank_kv, :].rearrange("p (m c) -> p m c", m=KD),
                                                    diagonal[:, None, :].broadcast_to([P, KD, HH * PAD]),
                                                    ALU.mult).then_inc(outer_masked, 1)
                    if n < TT - 1:
                        dve.wait_ge(outer_masked, (TT - 1) * b + n + 1)
                        if n == 0:
                            nc.vector.tensor_copy(state[:, :, :], outer[:, :, :]).then_inc(state_ready, 1)
                        else:
                            dve.wait_ge(o_ready, TT * b + n + 1)
                            for m in range(KD):
                                ins = nc.vector.scalar_tensor_tensor(out=state[:, m, :], in0=state[:, m, :],
                                                                     scalar=chunk_decay[:, m:m + 1],
                                                                     in1=outer[:, m, :], op0=ALU.mult, op1=ALU.add)
                            ins.then_inc(state_ready, 1)
                dve.wait_ge(gate_sb, b + 1)
                for n in range(TT):
                    dve.wait_ge(o_turned, TT * b + n + 1)
                    src = ps[:, n, :].rearrange("p (h e) -> p h e", e=PAD)[:, :, 0:HD]
                    nc.vector.tensor_tensor(og[:, n, :].rearrange("p (h e) -> p h e", e=HD), src,
                                            gate[:, n, :].rearrange("p (h e) -> p h e", e=HD),
                                            ALU.mult).then_inc(og_ready, 1)
                dve.wait_ge(og_ready, TT * (b + 1))
                steps(nc.vector.tensor_tensor(sq[:, :, :], og[:, :, :], og[:, :, :], ALU.mult))
                steps.settle()
                steps(nc.vector.tensor_reduce(ss[:, :], sq[:, :, :].rearrange("p t (h e) -> p (t h) e", e=HD),
                                              AX.X, ALU.add))
                steps.settle()
                nc.vector.tensor_scalar(ms[:, :], ss[:, :], 1.0 / HD, 1e-5, ALU.mult, ALU.add).then_inc(ms_ready, 1)
                dve.wait_ge(rms_ready, b + 1)
                steps(nc.vector.reciprocal(rrms[:, :], rms[:, :]))
                steps.settle()
                steps(nc.vector.tensor_tensor(sq[:, :, :].rearrange("p t (h e) -> p (t h) e", e=HD),
                                              og[:, :, :].rearrange("p t (h e) -> p (t h) e", e=HD),
                                              rrms[:, :, None].broadcast_to([P, TT * H, HD]), ALU.mult))
                steps.settle()
                for t in range(TT):
                    nc.vector.tensor_tensor(og[:, t, :], sq[:, t, :], norm_w[:, :],
                                            ALU.mult).then_inc(again.xn_ready, 1)
                again.low_part(dve, b, xt, ps[:, 4:6, :])
                dve.wait_ge(y_ready, b + 1)
                steps(nc.vector.tensor_tensor(x[:, 0:2, :], x[:, 0:2, :],
                                              ps[:, 6, :].rearrange("p (t n) -> p t n", t=2), ALU.add))
                nc.vector.tensor_tensor(x[:, 2:4, :], x[:, 2:4, :],
                                        ps[:, 7, :].rearrange("p (t n) -> p t n", t=2),
                                        ALU.add).then_inc(batch_done, 1)
                dve.wait_ge(batch_done, b + 1)
                assert steps.n == VEC


def experts(nc, X, ident, ps, d, name, w_gu):
    with ExitStack() as ctx:
        def sb(n, shape, dt=F32):
            return ctx.enter_context(nc.sbuf_tensor(f"{name}_{n}", shape, dt))

        xt = Parts(sb("xt_hi", [P, KD, B * N], F32R), sb("xt_lo", [P, KD, B * N], F32R))
        shares_t = sb("shares_t", [P, B * N], BF16)
        spread = sb("spread", [P, HT, P], BF16)
        w_d = sb("w_d", [P, HT, D])
        routing(nc, X, ident, ps, d, name, xt, shares_t, spread, w_d)
        mixture(nc, X, ps, name, xt, shares_t, spread, w_gu, w_d)


def routing(nc, X, ident, ps, d, name, xt, shares_t, spread, w_d):
    SENT = TOPK
    with ExitStack() as ctx:
        signal = ctx.enter_context(signals(nc))

        def sb(n, shape, dt=F32):
            return ctx.enter_context(nc.sbuf_tensor(f"{name}r_{n}", shape, dt))

        def sem(n):
            return signal(f"{name}r_{n}")

        w_r = Parts(sb("w_r_hi", [P, KD * P], F32R), sb("w_r_lo", [P, KD * P], F32R))
        split_weights(nc, f"{name}r_w", [(d["Wr"], w_r)])
        wr = Parts(*(w.rearrange("p (k n) -> p k n", k=KD) for w in (w_r.hi[:, :], w_r.lo[:, :])))
        ident_b = sb("ident_b", [P, P], BF16)
        xn = sb("xn", [P, TT, D])
        logit_t = sb("logit_t", [P, N])
        logit = sb("logit", [P, NT, E])
        top = sb("top", [P, NT])
        ex = sb("ex", [P, NT, E])
        den = sb("den", [P, NT])
        rden = sb("rden", [P, NT])
        prob = sb("prob", [P, NT, E + SENT])
        best = sb("best", [P, NT, TOPK])
        total = sb("total", [P, NT])
        total_c = sb("total_c", [P, NT])
        rtotal = sb("rtotal", [P, NT])
        renorm = sb("renorm", [P, NT, TOPK])
        ones = sb("ones", [P, TOPK])
        cum = sb("cum", [P, NT, TOPK])
        active = sb("active", [P, NT, TOPK])
        kept = sb("kept", [P, NT, TOPK])
        inactive = sb("inactive", [P, NT, TOPK])
        key = sb("key", [P, NT, TOPK])
        mass = sb("mass", [P, NT])
        mass_c = sb("mass_c", [P, NT])
        rmass = sb("rmass", [P, NT])
        rest = sb("rest", [P, NT, E + SENT])
        found = logit
        share = ex
        left1 = logit
        left2 = logit
        share_parts = sb("share_parts", [P, NT, P], BF16)

        norm = Norm(nc, ctx, signal, f"{name}_ln", xn)
        vec = sem("vec")
        const_loaded, down_loaded = sem("const_loaded"), sem("down_loaded")
        logit_ready, logit_sb, logit_turned, logit_tok = (sem("logit_ready"), sem("logit_sb"),
                                                          sem("logit_turned"), sem("logit_tok"))
        shifted, exp_done = sem("shifted"), sem("exp_done")
        parts_ready, parts_turned, parts_sb = sem("parts_ready"), sem("parts_turned"), sem("parts_sb")
        VEC = LN_STEPS
        HALF = NT // 2
        block = ctx.enter_context(nc.Block())

        @block.sync
        def _(sp):
            sp.dma_start(spread[:, :, :].bitcast(U16), d["spread"].rearrange("p (t n) -> p t n", n=P)).then_inc(const_loaded, 16)
            sp.dma_start(ident_b[:, :].bitcast(U16), d["ident_b"]).then_inc(const_loaded, 16)
            sp.dma_start(w_d[:, :, :], d["Wdown"].rearrange("(t p) n -> p t n", p=P)).then_inc(down_loaded, 16)
            sp.wait_ge(const_loaded, 32)
            sp.wait_ge(down_loaded, 16)

        @block.tensor
        def _(pe):
            with pe.Fori(0, B) as b:
                pe.wait_ge(norm.lo_ready, KD * b)
                norm.tensor(pe, b, ident, ps[:, 0:2, :])
                norm.wait_parts(pe, b)
                pe.wait_ge(logit_sb, b)
                cols = bass.ds(b * N, N)
                product(nc, ps[:, 2, :], [wr[:, k, :] for k in range(KD)], [xt[:, k, cols] for k in range(KD)],
                        True, True).then_inc(logit_ready, 1)
                pe.wait_ge(logit_sb, b + 1)
                pe.wait_ge(logit_tok, b)
                for t in range(TT):
                    ins = nc.tensor.transpose(ps[:, 3, t * P:(t + 1) * P], logit_t[:, t * P:(t + 1) * P],
                                              ident[:, :])
                ins.then_inc(logit_turned, 1)
            pe.wait_ge(const_loaded, 32)
            for b in range(B):
                pe.wait_ge(parts_ready, 1)
                bank = ps[:, 4 + b, 0:N // 2].bitcast(BF16)
                for t in range(TT):
                    ins = nc.tensor.transpose(bank[:, t * P:(t + 1) * P], share_parts[:, b * TT + t, :],
                                              ident_b[:, :])
                ins.then_inc(parts_turned, 1)

        @block.scalar
        def _(act):
            with act.Fori(0, B) as b:
                cols = bass.ds(b * N, N)
                norm.scalar(act, b, xt[:, :, cols], ps[:, 0:2, :])
                act.wait_ge(logit_ready, b + 1)
                nc.scalar.copy(logit_t[:, :], ps[:, 2, :]).then_inc(logit_sb, 1)
                act.wait_ge(logit_turned, b + 1)
                nc.scalar.copy(logit[:, bass.ds(b * TT, TT), :],
                               ps[:, 3, :].rearrange("p (t e) -> p t e", e=P)[:, :, 0:E]).then_inc(logit_tok, 1)
            act.wait_ge(shifted, 1)
            nc.scalar.activation(ex[:, :, :], logit[:, :, :], ACT.Exp).then_inc(exp_done, 1)
            for b in range(B):
                act.wait_ge(parts_turned, b + 1)
                nc.scalar.copy(shares_t[:, b * N:(b + 1) * N],
                               ps[:, 4 + b, 0:N // 2].bitcast(BF16)).then_inc(parts_sb, 1)

        @block.vector
        def _(dve):
            with dve.Fori(0, B) as b:
                steps = Steps(dve, vec, b * VEC)
                dve.wait_ge(norm.turned, KD * b)
                norm.vector(dve, steps, b, X[:, bass.ds(b * TT, TT), :], xt[:, :, bass.ds(b * N, N)], ps[:, 0:2, :])
                assert steps.n == VEC
            steps = Steps(dve, vec, B * VEC)

            def each(v, n):
                return v[:, :, None].broadcast_to([P, NT, n])

            steps(nc.vector.memset(ones[:, :], 1.0))
            steps(nc.vector.memset(prob[:, :, E:], -1.0))
            steps(nc.vector.memset(active[:, :, 0:1], 1.0))
            steps(nc.vector.memset(share_parts[:, :, 3 * E:], 0.0))
            dve.wait_ge(logit_tok, B)
            steps(nc.vector.tensor_reduce(top[:, :], logit[:, :, :], AX.X, ALU.max))
            steps.settle()
            nc.vector.tensor_tensor(logit[:, :, :], logit[:, :, :], each(top, E), ALU.subtract).then_inc(shifted, 1)
            dve.wait_ge(exp_done, 1)
            steps(nc.vector.tensor_reduce(den[:, :], ex[:, :, :], AX.X, ALU.add))
            steps.settle()
            steps(nc.vector.reciprocal(rden[:, :], den[:, :]))
            steps.settle()
            steps(nc.vector.tensor_tensor(prob[:, :, 0:E], ex[:, :, :], each(rden, E), ALU.mult))
            steps.settle()
            for t in range(NT):
                steps(nc.vector.max(best[:, t, :], prob[:, t, 0:E]))
            steps.settle()
            steps(nc.vector.tensor_reduce(total[:, :], best[:, :, :], AX.X, ALU.add))
            steps.settle()
            steps(nc.vector.tensor_scalar(total_c[:, :], total[:, :], 1e-12, None, ALU.max))
            steps.settle()
            steps(nc.vector.reciprocal(rtotal[:, :], total_c[:, :]))
            steps.settle()
            steps(nc.vector.tensor_tensor(renorm[:, :, :], best[:, :, :], each(rtotal, TOPK), ALU.mult))
            steps.settle()
            for t in range(NT):
                steps(nc.vector.tensor_tensor_scan(cum[:, t, :], ones[:, :], renorm[:, t, :], 0.0,
                                                   ALU.mult, ALU.add))
            steps.settle()
            steps(nc.vector.tensor_scalar(active[:, :, 1:TOPK], cum[:, :, 0:TOPK - 1], KEEP, None, ALU.is_lt))
            steps.settle()
            steps(nc.vector.tensor_tensor(kept[:, :, :], best[:, :, :], active[:, :, :], ALU.mult))
            steps(nc.vector.tensor_scalar(inactive[:, :, :], active[:, :, :], -1.0, None, ALU.add))
            steps.settle()
            steps(nc.vector.tensor_reduce(mass[:, :], kept[:, :, :], AX.X, ALU.add))
            steps(nc.vector.tensor_tensor(key[:, :, :], kept[:, :, :], inactive[:, :, :], ALU.add))
            steps.settle()
            steps(nc.vector.tensor_scalar(mass_c[:, :], mass[:, :], 1e-12, None, ALU.max))
            for t in range(NT):
                steps(nc.vector.match_replace(rest[:, t, :], key[:, t, :], prob[:, t, :], 0.0))
            steps.settle()
            steps(nc.vector.reciprocal(rmass[:, :], mass_c[:, :]))
            steps(nc.vector.tensor_tensor(found[:, :, :], prob[:, :, 0:E], rest[:, :, 0:E], ALU.subtract))
            steps.settle()
            steps(nc.vector.tensor_tensor(share[:, :, :], found[:, :, :], each(rmass, E), ALU.mult))
            steps.settle()
            steps(nc.vector.tensor_copy(share_parts[:, :, 0:E], share[:, :, :]))
            steps.settle()
            steps(nc.vector.tensor_tensor(left1[:, :, :], share[:, :, :], share_parts[:, :, 0:E], ALU.subtract))
            steps.settle()
            steps(nc.vector.tensor_copy(share_parts[:, :, E:2 * E], left1[:, :, :]))
            steps.settle()
            steps(nc.vector.tensor_tensor(left2[:, :, :], left1[:, :, :], share_parts[:, :, E:2 * E], ALU.subtract))
            steps.settle()
            nc.vector.tensor_copy(share_parts[:, :, 2 * E:3 * E], left2[:, :, :]).then_inc(parts_ready, 1)


def mixture(nc, X, ps, name, xt, shares_t, spread, w_gu, w_d):
    LAG = 2
    RING = LAG + 1
    with ExitStack() as ctx:
        signal = ctx.enter_context(signals(nc))

        def sb(n, shape, dt=F32):
            return ctx.enter_context(nc.sbuf_tensor(f"{name}m_{n}", shape, dt))

        def sem(n):
            return signal(f"{name}m_{n}")

        act_g = sb("act_g", [P, 2, N])
        gated = sb("gated", [P, 2, N])
        hidden = sb("hidden", [P, RING, N])
        gate_ready, up_ready, share_ready = sem("gate_ready"), sem("up_ready"), sem("share_ready")
        silu_done, gated_done, hidden_done = sem("silu_done"), sem("gated_done"), sem("hidden_done")
        down_done, out_ready, out_added = sem("down_done"), sem("out_ready"), sem("out_added")
        bank_y = 6
        block = ctx.enter_context(nc.Block())

        @block.tensor
        def _(pe):
            with pe.Fori(0, B) as b:
                cols = bass.ds(b * N, N)
                x = [xt[:, k, cols] for k in range(KD)]
                pe.wait_ge(out_added, b)
                for i in range(HT + LAG):
                    if i < HT:
                        s = 3 * (i % 2)
                        if i >= 2:
                            pe.wait_ge(silu_done, HT * b + i - 1)
                        product(nc, ps[:, s, :], [w_gu[:, k, i * P:(i + 1) * P] for k in range(KD)], x,
                                True, True).then_inc(gate_ready, 1)
                        if i >= 2:
                            pe.wait_ge(gated_done, HT * b + i - 1)
                        o = E * INTER + i * P
                        product(nc, ps[:, s + 1, :], [w_gu[:, k, o:o + P] for k in range(KD)], x,
                                True, True).then_inc(up_ready, 1)
                        if i >= 2:
                            pe.wait_ge(hidden_done, HT * b + i - 1)
                        nc.tensor.matmul(ps[:, s + 2, :], spread[:, i, :], shares_t[:, cols],
                                         start=True, stop=True).then_inc(share_ready, 1)
                    if i >= LAG:
                        j = i - LAG
                        pe.wait_ge(hidden_done, HT * b + j + 1)
                        for t in range(TT):
                            ins = nc.tensor.matmul(ps[:, bank_y + t // 2, (t % 2) * D:(t % 2 + 1) * D],
                                                   hidden[:, j % RING, t * P:(t + 1) * P], w_d[:, j, :],
                                                   start=(j == 0 and t % 2 == 0), stop=(j == HT - 1),
                                                   skip_group_check=True)
                        ins.then_inc(out_ready if j == HT - 1 else down_done, 1)

        @block.scalar
        def _(act):
            with act.Fori(0, B) as b:
                for i in range(HT):
                    act.wait_ge(gate_ready, HT * b + i + 1)
                    if i >= 2:
                        act.wait_ge(gated_done, HT * b + i - 1)
                    else:
                        act.wait_ge(gated_done, HT * b)
                    nc.scalar.activation(act_g[:, i % 2, :], ps[:, 3 * (i % 2), :], ACT.Silu).then_inc(silu_done, 1)

        @block.vector
        def _(dve):
            with dve.Fori(0, B) as b:
                for i in range(HT):
                    s = 3 * (i % 2)
                    dve.wait_ge(silu_done, HT * b + i + 1)
                    dve.wait_ge(up_ready, HT * b + i + 1)
                    nc.vector.tensor_tensor(gated[:, i % 2, :], ps[:, s + 1, :], act_g[:, i % 2, :],
                                            ALU.mult).then_inc(gated_done, 1)
                    dve.wait_ge(gated_done, HT * b + i + 1)
                    dve.wait_ge(share_ready, HT * b + i + 1)
                    if i >= RING:
                        dve.wait_ge(down_done, (HT - 1) * b + i - RING + 1)
                    nc.vector.tensor_tensor(hidden[:, i % RING, :], ps[:, s + 2, :], gated[:, i % 2, :],
                                            ALU.mult).then_inc(hidden_done, 1)
                dve.wait_ge(out_ready, b + 1)
                for h in range(2):
                    x = X[:, bass.ds(b * TT + 2 * h, 2), :]
                    ins = nc.vector.tensor_tensor(x, x, ps[:, bank_y + h, :].rearrange("p (t n) -> p t n", t=2),
                                                  ALU.add)
                ins.then_inc(out_added, 1)


def attention(nc, X, ident, ps, d):
    PAIRS = H // 2
    SRC = 4 * HD
    UNITS = KV * TT * 2
    with ExitStack() as ctx:
        signal = ctx.enter_context(signals(nc))

        def sb(n, shape, dt=F32):
            return ctx.enter_context(nc.sbuf_tensor(f"b_{n}", shape, dt))

        def sem(n):
            return signal(f"b_{n}")

        w_qkv = Parts(sb("w_qkv_hi", [P, KD * QKV], F32R), sb("w_qkv_lo", [P, KD * QKV], F32R))
        split_weights(nc, "b_w", [(d["WqkvB"], w_qkv)])
        wqkv = Parts(*(w.rearrange("p (k n) -> p k n", k=KD) for w in (w_qkv.hi[:, :], w_qkv.lo[:, :])))
        w_out = sb("w_out", [P, KV, D])
        cos = sb("cos", [P, TT, HD])
        sin = sb("sin", [P, TT, HD])
        sum_rows = sb("sum_rows", [P, P])
        xt = Parts(sb("xt_hi", [P, KD, N], F32R), sb("xt_lo", [P, KD, N], F32R))
        work = sb("work", [P, NT * D])
        qk = sb("qk", [P, TT, D + KV * HD])
        k4 = sb("k4", [P, TT * KV, 3 * SRC])
        q_t = sb("q_t", [P, PAIRS, N], F32R)
        k_t = sb("k_t", [P, 2 * KV, N], F32R)
        v_pad = sb("v_pad", [P, TT, KV, PAD])
        ssq = sb("ssq", [P, 2, TT])
        mean_sq = sb("mean_sq", [P, 2, TT])
        rms = sb("rms", [P, 2, TT])
        rrms = sb("rrms", [P, 2, TT])
        xn = work[:, 0:TT * D].rearrange("p (t n) -> p t n", t=TT)
        W = TT * (D + KV * HD)
        term1 = work[:, 0:W].rearrange("p (t n) -> p t n", t=TT)
        term2 = work[:, W:2 * W].rearrange("p (t n) -> p t n", t=TT)
        q4 = work[:, :].rearrange("p (r c) -> p r c", c=SRC)
        probs = work[:, 0:4 * N].rearrange("p (u j n) -> p u j n", u=2, j=2)
        heads = work[:, 4 * N:8 * N].rearrange("p (g n) -> p g n", g=KV)
        enc = qk[:, :, :].rearrange("p t n -> p (t n)")[:, 0:N]
        rsum = qk[:, :, :].rearrange("p t n -> p (t n)")[:, N:2 * N]

        norm = Norm(nc, ctx, signal, "b_ln", xn)
        vec, batch_done, const_loaded = sem("vec"), sem("batch_done"), sem("const_loaded")
        zeroed, qkv_ready, squares_done, mean_ready, rms_ready = (sem("zeroed"), sem("qkv_ready"),
                                                                   sem("squares_done"), sem("mean_ready"),
                                                                   sem("rms_ready"))
        rrms_ready, qk_ready, v_ready = sem("rrms_ready"), sem("qk_ready"), sem("v_ready")
        rotated, q_hi, k_hi, q4_ready, k4_ready = (sem("rotated"), sem("q_hi"), sem("k_hi"),
                                                    sem("q4_ready"), sem("k4_ready"))
        q_turned, k_turned, q_parts, k_parts = sem("q_turned"), sem("k_turned"), sem("q_parts"), sem("k_parts")
        logits_ready, exp_done, pv_done = sem("logits_ready"), sem("exp_done"), sem("pv_done")
        enc_ready, enc_sb, sum_ready, rsum_ready, head_ready = (sem("enc_ready"), sem("enc_sb"), sem("sum_ready"),
                                                                 sem("rsum_ready"), sem("head_ready"))
        y_ready = sem("y_ready")
        VEC = LN_STEPS + 4
        block = ctx.enter_context(nc.Block())
        consts = [(w_out[:, :, :].rearrange("p g n -> p (g n)"), d["Wout"]),
                  (cos[:, :, :].rearrange("p t n -> p (t n)"), d["cos"]),
                  (sin[:, :, :].rearrange("p t n -> p (t n)"), d["sin"]), (sum_rows[:, :], d["sum_rows"])]

        @block.sync
        def _(sp):
            for dst, src in consts:
                sp.dma_start(dst, src).then_inc(const_loaded, 16)

        @block.tensor
        def _(pe):
            pe.wait_ge(const_loaded, 16 * len(consts))
            with pe.Fori(0, B) as b:
                pe.wait_ge(batch_done, b)
                norm.tensor(pe, b, ident, ps[:, 4:6, :])
                norm.wait_parts(pe, b)
                for t in range(TT):
                    product(nc, ps[:, t, 0:QKV], [xt[:, k, t * P:(t + 1) * P] for k in range(KD)],
                            [wqkv[:, k, :] for k in range(KD)], True, True).then_inc(qkv_ready, 1)
                pe.wait_ge(q4_ready, b + 1)
                pe.wait_ge(k4_ready, b + 1)
                for i in range(PAIRS):
                    if i >= 2:
                        pe.wait_ge(q_parts, PAIRS * b + i - 1)
                        pe.wait_ge(k_parts, PAIRS * b + i - 1)
                    for t in range(TT):
                        rows = q4[:, t * H + 2 * i:t * H + 2 * i + 2, :].rearrange("p r c -> p (r c)")
                        ins = nc.tensor.transpose(ps[:, 4 + i % 2, t * P:(t + 1) * P], rows, ident[:, :])
                    ins.then_inc(q_turned, 1)
                    g, low = i // 2, i % 2
                    for t in range(TT):
                        src = k4[:, t * KV + g, (1 - low) * SRC:(1 - low) * SRC + P]
                        ins = nc.tensor.transpose(ps[:, 6 + i % 2, t * P:(t + 1) * P], src, ident[:, :])
                    ins.then_inc(k_turned, 1)
                pe.wait_ge(v_ready, TT * (b + 1))
                pe.wait_ge(qk_ready, 2 * TT * (b + 1))
                pe.wait_ge(q_parts, PAIRS * (b + 1))
                pe.wait_ge(k_parts, PAIRS * (b + 1))

                def logits(u):
                    g, st, jp = u // (2 * TT), u // 2 % TT, u % 2
                    if u >= 3:
                        pe.wait_ge(exp_done, UNITS * b + u - 2)
                    for j in range(2):
                        ins = nc.tensor.matmul(ps[:, 2 * (u % 3) + j, :], k_t[:, 2 * g + j, st * P:(st + 1) * P],
                                               q_t[:, 2 * g + jp, :], start=True, stop=True)
                    ins.then_inc(logits_ready, 1)

                def values(u):
                    g, st, jp = u // (2 * TT), u // 2 % TT, u % 2
                    pe.wait_ge(exp_done, UNITS * b + u + 1)
                    if g >= 1 and st == 0 and jp == 0:
                        pe.wait_ge(enc_sb, KV * b + g)
                    for j in range(2 * jp, 2 * jp + 2):
                        ins = nc.tensor.matmul(ps[j * PAD:(j + 1) * PAD, 6, :], v_pad[:, st, g, :],
                                               probs[:, u % 2, j % 2, :], start=(st == 0), stop=(st == TT - 1),
                                               skip_group_check=True)
                    ins.then_inc(pv_done, 1)

                def sums(g):
                    pe.wait_ge(enc_sb, KV * b + g + 1)
                    if g >= 1:
                        pe.wait_ge(rsum_ready, KV * b + g)
                    nc.tensor.matmul(ps[:, 7, :], sum_rows[:, :], enc, start=True, stop=True).then_inc(sum_ready, 1)

                for u in range(UNITS + 2):
                    if u < UNITS:
                        logits(u)
                    if 1 <= u <= UNITS:
                        values(u - 1)
                    if u >= 2 * TT + 1 and (u - 1) % (2 * TT) == 0:
                        sums((u - 1) // (2 * TT) - 1)
                pe.wait_ge(head_ready, KV * (b + 1))
                for t in range(TT):
                    for g in range(KV):
                        ins = nc.tensor.matmul(ps[:, t // 2, (t % 2) * D:(t % 2 + 1) * D],
                                               heads[:, g, t * P:(t + 1) * P], w_out[:, g, :],
                                               start=(g == 0 and t % 2 == 0), stop=(g == KV - 1),
                                               skip_group_check=True)
                ins.then_inc(y_ready, 1)

        @block.scalar
        def _(act):
            with act.Fori(0, B) as b:
                act.wait_ge(batch_done, b)
                norm.scalar(act, b, xt, ps[:, 4:6, :])
                act.wait_ge(zeroed, 3)
                for t in range(TT):
                    act.wait_ge(qkv_ready, TT * b + t + 1)
                    for part, (o, n) in enumerate(((0, D), (D, KV * HD))):
                        nc.scalar.activation(qk[:, t, o:o + n], ps[:, t, o:o + n], ACT.Square,
                                             accum_out=ssq[:, part, t:t + 1]).then_inc(squares_done, 1)
                    nc.scalar.copy(v_pad[:, t, :, 0:HD],
                                   ps[:, t, D + KV * HD:QKV].rearrange("p (g e) -> p g e", e=HD)).then_inc(v_ready, 1)
                act.wait_ge(mean_ready, b + 1)
                nc.scalar.activation(rms[:, :, :], mean_sq[:, :, :], ACT.Sqrt).then_inc(rms_ready, 1)
                act.wait_ge(rrms_ready, b + 1)
                act.wait_ge(squares_done, 2 * TT * (b + 1))
                for t in range(TT):
                    for part, (o, n) in enumerate(((0, D), (D, KV * HD))):
                        nc.scalar.activation(qk[:, t, o:o + n], ps[:, t, o:o + n], ACT.Copy,
                                             scale=rrms[:, part, t:t + 1]).then_inc(qk_ready, 1)
                act.wait_ge(rotated, b + 1)
                q = qk[:, :, 0:D].rearrange("p t (h e) -> p t h e", e=HD)
                k = qk[:, :, D:D + KV * HD].rearrange("p t (g e) -> p t g e", e=HD)
                q4v = q4.rearrange("p (t h) c -> p t h c", t=TT)
                k4v = k4[:, :, :].rearrange("p (t g) c -> p t g c", t=TT)
                for c in (0, 1):
                    nc.scalar.copy(q4v[:, :, :, c * HD:(c + 1) * HD].bitcast(F32R), q).then_inc(q_hi, 1)
                for c in (0, 2):
                    nc.scalar.copy(k4v[:, :, :, SRC + c * HD:SRC + (c + 1) * HD].bitcast(F32R), k).then_inc(k_hi, 1)
                for i in range(PAIRS):
                    act.wait_ge(q_turned, PAIRS * b + i + 1)
                    nc.scalar.copy(q_t[:, i, :], ps[:, 4 + i % 2, :]).then_inc(q_parts, 1)
                for u in range(UNITS):
                    act.wait_ge(logits_ready, UNITS * b + u + 1)
                    if u >= 2:
                        act.wait_ge(pv_done, UNITS * b + u - 1)
                    nc.scalar.activation(probs[:, u % 2, :, :], ps[:, 2 * (u % 3):2 * (u % 3) + 2, :], ACT.Exp,
                                         scale=float(HD) ** -0.5).then_inc(exp_done, 1)

        @block.vector
        def _(dve):
            nc.vector.memset(k4[:, :, :], 0.0).then_inc(zeroed, 1)
            nc.vector.memset(v_pad[:, :, :, :], 0.0).then_inc(zeroed, 1)
            dve.wait_ge(zeroed, 2)
            nc.vector.memset(v_pad[:, :, :, HD:HD + 1], 1.0).then_inc(zeroed, 1)
            dve.wait_ge(const_loaded, 16 * len(consts))
            with dve.Fori(0, B) as b:
                steps = Steps(dve, vec, b * VEC)
                x = X[:, bass.ds(b * TT, TT), :]
                dve.wait_ge(batch_done, b)
                norm.vector(dve, steps, b, x, xt, ps[:, 4:6, :])
                dve.wait_ge(squares_done, 2 * TT * (b + 1))
                nc.vector.tensor_scalar(mean_sq[:, 0, :], ssq[:, 0, :], 1.0 / D, 1e-6, ALU.mult, ALU.add)
                nc.vector.tensor_scalar(mean_sq[:, 1, :], ssq[:, 1, :], 1.0 / (KV * HD), 1e-6, ALU.mult,
                                        ALU.add).then_inc(mean_ready, 1)
                dve.wait_ge(rms_ready, b + 1)
                nc.vector.reciprocal(rrms[:, :, :], rms[:, :, :]).then_inc(rrms_ready, 1)
                dve.wait_ge(qk_ready, 2 * TT * (b + 1))
                HEADS = H + KV
                half = HD // 2
                src = qk[:, :, :].rearrange("p t (h e) -> p t h e", e=HD)
                t1 = term1.rearrange("p t (h e) -> p t h e", e=HD)
                t2 = term2.rearrange("p t (h e) -> p t h e", e=HD)

                def table(v, o, n):
                    return v[:, :, None, o:o + n].broadcast_to([P, TT, HEADS, n])

                steps(nc.vector.tensor_tensor(t1, src, table(cos, 0, HD), ALU.mult))
                steps(nc.vector.tensor_tensor(t2[:, :, :, 0:half], src[:, :, :, half:HD], table(sin, 0, half),
                                              ALU.mult))
                steps(nc.vector.tensor_tensor(t2[:, :, :, half:HD], src[:, :, :, 0:half], table(sin, half, half),
                                              ALU.mult))
                steps.settle()
                nc.vector.tensor_tensor(qk[:, :, :], term1, term2, ALU.add).then_inc(rotated, 1)
                dve.wait_ge(rotated, b + 1)
                q = qk[:, :, 0:D].rearrange("p t (h e) -> p t h e", e=HD)
                k = qk[:, :, D:D + KV * HD].rearrange("p t (g e) -> p t g e", e=HD)
                q4v = q4.rearrange("p (t h) c -> p t h c", t=TT)
                k4v = k4[:, :, :].rearrange("p (t g) c -> p t g c", t=TT)
                dve.wait_ge(q_hi, 2 * (b + 1))
                for c in (2, 3):
                    ins = nc.vector.tensor_tensor(q4v[:, :, :, c * HD:(c + 1) * HD], q, q4v[:, :, :, 0:HD],
                                                  ALU.subtract)
                ins.then_inc(q4_ready, 1)
                dve.wait_ge(k_hi, 2 * (b + 1))
                for c in (1, 3):
                    ins = nc.vector.tensor_tensor(k4v[:, :, :, SRC + c * HD:SRC + (c + 1) * HD], k,
                                                  k4v[:, :, :, SRC:SRC + HD], ALU.subtract)
                ins.then_inc(k4_ready, 1)
                for i in range(PAIRS):
                    dve.wait_ge(k_turned, PAIRS * b + i + 1)
                    nc.vector.tensor_copy(k_t[:, i, :], ps[:, 6 + i % 2, :]).then_inc(k_parts, 1)
                for g in range(KV):
                    dve.wait_ge(pv_done, UNITS * b + 2 * TT * (g + 1))
                    if g >= 1:
                        dve.wait_ge(head_ready, KV * b + g)
                    nc.vector.tensor_copy(enc, ps[:, 6, :]).then_inc(enc_sb, 1)
                    dve.wait_ge(sum_ready, KV * b + g + 1)
                    nc.vector.reciprocal(rsum, ps[:, 7, :]).then_inc(rsum_ready, 1)
                    dve.wait_ge(rsum_ready, KV * b + g + 1)
                    nc.vector.tensor_tensor(heads[:, g, :], enc, rsum, ALU.mult).then_inc(head_ready, 1)
                dve.wait_ge(y_ready, b + 1)
                steps(nc.vector.tensor_tensor(x[:, 0:2, :], x[:, 0:2, :],
                                              ps[:, 0, :].rearrange("p (t n) -> p t n", t=2), ALU.add))
                nc.vector.tensor_tensor(x[:, 2:4, :], x[:, 2:4, :],
                                        ps[:, 1, :].rearrange("p (t n) -> p t n", t=2),
                                        ALU.add).then_inc(batch_done, 1)
                dve.wait_ge(batch_done, b + 1)
                assert steps.n == VEC


def program(nc, d, out):
    x_rows = d["x"].rearrange("b (t p) n -> p (b t) n", p=P)
    out_rows = out.rearrange("b (t p) n -> p (b t) n", p=P)
    with ExitStack() as ctx:
        signal = ctx.enter_context(signals(nc))
        X = ctx.enter_context(nc.sbuf_tensor("X", [P, NT, D], F32))
        ident = ctx.enter_context(nc.sbuf_tensor("ident", [P, P], F32))
        ps = ctx.enter_context(nc.psum_tensor("ps", [P, 8, N], F32))
        x_loaded = signal("x_loaded")
        stored = signal("stored")
        with nc.Block() as block:
            @block.sync
            def _(sp):
                sp.dma_start(ident[:, :], d["ident"]).then_inc(x_loaded, 16)
                sp.dma_start(X[:, :, :], x_rows).then_inc(x_loaded, 16)
                sp.wait_ge(x_loaded, 32)

        lightning(nc, X, ident, ps, d)
        w_gu = Parts(ctx.enter_context(nc.sbuf_tensor("w_gu_hi", [P, KD * 2 * E * INTER], F32R)),
                     ctx.enter_context(nc.sbuf_tensor("w_gu_lo", [P, KD * 2 * E * INTER], F32R)))
        split_weights(nc, "gu", [(d["Wgu"], w_gu)])
        wgu = Parts(*(w[:, :].rearrange("p (k n) -> p k n", k=KD) for w in (w_gu.hi, w_gu.lo)))
        experts(nc, X, ident, ps, d, "f", wgu)
        attention(nc, X, ident, ps, d)
        experts(nc, X, ident, ps, d, "g", wgu)
        with nc.Block() as block:
            @block.sync
            def _(sp):
                sp.dma_start(out_rows, X[:, :, :]).then_inc(stored, 16)
                sp.wait_ge(stored, 16)


def halves(w):
    return np.ascontiguousarray(w.reshape(KD, P, -1).transpose(1, 0, 2).reshape(P, -1))


def columns(w, n):
    out = np.zeros((w.shape[0], n), w.dtype)
    out[:, :w.shape[1]] = w
    return out


def constants():
    f = np.float32
    bf16_one = np.uint16(0x3F80)
    c = {"ident": np.eye(P, dtype=f), "ident_b": np.eye(P, dtype=np.uint16) * bf16_one}
    i = np.arange(P)
    c["gap"] = np.maximum(i[None, :] - i[:, None], 0).astype(f)
    c["causal"] = (i[None, :] >= i[:, None]).astype(f)
    c["ahead"] = np.broadcast_to((i + 1).astype(f), (P, P)).copy()
    c["left"] = (P - 1 - i).astype(f)[:, None].copy()
    c["head_rows"] = (i[:, None] // HD == np.arange(P // HD)[None, :]).astype(f)
    c["diagonal"] = np.repeat(c["head_rows"], PAD, axis=1)
    row = np.arange(HT * P) // INTER
    one = (np.arange(P)[:, None] % E == row[None, :]) & (np.arange(P)[:, None] < 3 * E)
    c["spread"] = one.astype(np.uint16) * bf16_one
    c["sum_rows"] = ((i[:, None] // PAD == i[None, :] // PAD) & (i[:, None] % PAD == HD)).astype(f)
    scale = f(10000.0) ** (np.arange(0, HD, 2, dtype=f) / f(HD))
    angle = np.arange(N, dtype=f)[:, None] * (f(1.0) / scale)[None, :]
    sin, cos = np.sin(angle), np.cos(angle)
    for name, v in (("sin", np.concatenate([-sin, sin], 1)), ("cos", np.concatenate([cos, cos], 1))):
        c[name] = v.reshape(TT, P, HD).transpose(1, 0, 2).reshape(P, -1).astype(f)
    return {k: np.ascontiguousarray(v) for k, v in c.items()}


def layout(v):
    a = {"x": v["L0_attn_a_x"]}
    p = "L0_attn_a_"
    a["Wqkv"] = halves(np.concatenate([v[p + "Wq"], v[p + "Wk"], v[p + "Wv"]], 1))
    a["Wo"] = halves(v[p + "Wo"])
    a["Wg1"] = halves(columns(v[p + "Wg1"], P))
    a["Wg2"] = columns(v[p + "Wg2"].T, P).T
    a["norm_w"] = np.broadcast_to(v[p + "norm_w"], (P, D))
    a["ld_heads"] = np.broadcast_to(v[p + "log_decay"], (P, H))
    a["ld_rows"] = np.repeat(v[p + "log_decay"], HD).reshape(KD, P).T
    p = "L0_attn_b_"
    a["WqkvB"] = halves(np.concatenate([v[p + "Wq"], v[p + "Wk"], v[p + "Wv"]], 1))
    w = v[p + "Wout"].reshape(KV, G, HD, D)
    out = np.zeros((G, PAD, KV, D), w.dtype)
    out[:, :HD] = w.transpose(1, 2, 0, 3)
    a["Wout"] = out.reshape(P, KV * D)
    p = "L0_ffn_"
    a["Wr"] = halves(columns(v[p + "gate_weight"].T, P))
    gu = v[p + "gate_up_proj"].reshape(E, 2, INTER, D).transpose(3, 1, 0, 2).reshape(D, -1)
    a["Wgu"] = halves(gu)
    a["Wdown"] = v[p + "down_proj"].transpose(0, 2, 1).reshape(E * INTER, D)
    return {k: np.ascontiguousarray(x) for k, x in a.items()}


def kernel(**inputs):
    import concourse.bacc as _bacc
    from concourse.bass_utils import run_bass_kernel_spmd as _run

    nc = _bacc.Bacc("TRN2", target_bir_lowering=False, num_devices=1)
    arrays = {**layout({k: np.asarray(v) for k, v in inputs.items()}), **constants()}
    d = {k: nc.dram_tensor(f"in_{k}", a.shape, mybir.dt.from_np(a.dtype), kind="ExternalInput").ap()
         for k, a in arrays.items()}
    out = nc.dram_tensor("out_0", (B, N, D), F32, kind="ExternalOutput").ap()
    program(nc, d, out)
    r = _run(nc, [{f"in_{k}": a for k, a in arrays.items()}], core_ids=[0])
    return r.results[0]["out_0"]
```

```python
from contextlib import ExitStack, contextmanager

import concourse.bass as bass
import numpy as np
from concourse import mybir

F32 = mybir.dt.float32
F32R = mybir.dt.float32r
BF16 = mybir.dt.bfloat16
U16 = mybir.dt.uint16
ALU = mybir.AluOpType
ACT = mybir.ActivationFunctionType
AX = mybir.AxisListType

P = 128
B, N, D = 4, 512, 256
TT = N // P
NT = B * TT
KD = D // P
H, HD = 16, 16
KV = 4
G = H // KV
PAD = 32
E, TOPK, KEEP = 32, 8, 0.8
INTER = 96
HT = E * INTER // P
QKV = D + 2 * KV * HD
AREA = 42 * 256
PASSES = (("hi", "hi"), ("hi", "lo"), ("lo", "hi"))


def chunks(n, step):
    return [(i, min(step, n - i)) for i in range(0, n, step)]


@contextmanager
def signals(nc):
    given = []

    def sem(name):
        given.append(nc.alloc_semaphore(name))
        return given[-1]

    yield sem
    nc.clear_and_free_semaphores(given)
    nc.all_engine_barrier()


class Area:

    def __init__(self, nc, ctx, name, columns):
        ctx.enter_context(nc.sbuf_tensor(name, [P, columns], F32))
        self.nc, self.name, self.end = nc, name, nc.sbuf_base
        self.start = self.end - 4 * columns


class Placer:
    def __init__(self, area, use):
        self.area, self.use, self.at = area, use, area.start

    def take(self, name, shape, dt):
        size = int(np.prod(shape[1:])) * (2 if dt == BF16 else 4)
        v = self.area.nc.alloc_sbuf_tensor_at(f"{self.use}_{name}", shape, dt, offset=self.at)
        self.at += (size + 31) // 32 * 32
        assert self.at <= self.area.end
        return v


def loaded_parts(nc, ctx, name, shape):
    hi = ctx.enter_context(nc.sbuf_tensor(f"{name}_hi", shape, F32R))
    area = Area(nc, ctx, f"{name}_area", int(np.prod(shape[1:])))
    return Parts(hi, Placer(area, name).take("lo", shape, F32R)), Placer(area, name).take("raw", shape, F32)


class Steps:

    def __init__(self, eng, sem, base=0):
        self.eng, self.sem, self.base, self.n = eng, sem, base, 0

    def __call__(self, ins):
        ins.then_inc(self.sem, 1)
        self.n += 1

    def settle(self):
        self.eng.wait_ge(self.sem, self.base + self.n)


class Parts:

    def __init__(self, hi, lo):
        self.hi, self.lo = hi, lo

    def __getitem__(self, i):
        return Parts(self.hi[i], self.lo[i])


def product(nc, out, stationary, moving, start, stop):
    pairs = [(s, m, sp, mp) for s, m in zip(stationary, moving) for sp, mp in PASSES]
    for i, (s, m, sp, mp) in enumerate(pairs):
        last = nc.tensor.matmul(out, s.hi if sp == "hi" else s.lo, m.hi if mp == "hi" else m.lo,
                                start=start and i == 0, stop=stop and i == len(pairs) - 1,
                                skip_group_check=True)
    return last


def lightning(nc, X, ident, ps, d, w_r, w_r_raw, routing, first_loads, x_loaded):
    HH = H // KD
    QUADS = H // 4
    UNITS = QUADS * TT
    HT2 = TT // 2
    W = HT2 * P
    STEPS_AHEAD = UNITS // 2
    DRAIN = 11
    with ExitStack() as ctx:
        signal = ctx.enter_context(signals(nc))

        def sb(n, shape, dt=F32):
            return ctx.enter_context(nc.sbuf_tensor(f"a_{n}", shape, dt))

        def sem(n):
            return signal(f"a_{n}")

        def parts(n, shape):
            return Parts(sb(n + "_hi", shape, F32R), sb(n + "_lo", shape, F32R))

        def weight(n, shape):
            return loaded_parts(nc, ctx, f"a_{n}", shape)

        w_qkv, w_qkv_raw = weight("w_qkv", [P, KD, 3 * D])
        w_o, w_o_raw = weight("w_o", [P, KD, D])
        w_g1, w_g1_raw = weight("w_g1", [P, KD, P])
        w_g2 = sb("w_g2", [P, D])
        norm_w = sb("norm_w", [P, D])
        ld_heads = sb("ld_heads", [P, H])
        ld_rows = sb("ld_rows", [P, KD])
        gap = sb("gap", [P, P])
        causal = sb("causal", [P, P])
        ahead = sb("ahead", [P, P])
        left = sb("left", [P, 1])
        head_rows = sb("head_rows", [P, HH])
        diagonal = sb("diagonal", [P, HH * PAD])
        decay = sb("decay", [P, H, P])
        q_decay = sb("q_decay", [P, KD, P])
        k_decay = sb("k_decay", [P, H])
        k_left = sb("k_left", [P, H])
        chunk_decay = sb("chunk_decay", [P, KD])
        xn = sb("xn", [P, HT2, D])
        xt = parts("xt", [P, KD, W])
        q_t = sb("q_t", [P, KD, N])
        k_t = sb("k_t", [P, KD, N])
        k_tok = sb("k_tok", [P, TT, D])
        v_pad = sb("v_pad", [P, TT, H, PAD])
        g1 = sb("g1", [P, W])
        gate = sb("gate", [P, TT, D])
        k_dec = sb("k_dec", [P, 2, D])
        q_dec = sb("q_dec", [P, 2, KD, P])
        q_mask = sb("q_mask", [P, 2, 4, P])
        weights = sb("weights", [P, 2, 4, P])
        state = sb("state", [P, 2, KD, HH * PAD])
        outer = sb("outer", [P, KD, HH * PAD])
        o_t = sb("o_t", [P, 2, N])
        og = sb("og", [P, 2, D])
        sq = sb("sq", [P, D])
        ss = sb("ss", [P, H])
        ms = sb("ms", [P, H])
        root = sb("root", [P, H])
        rrms = sb("rrms", [P, H])
        og_norm = sb("og_norm", [P, D])
        og_t = parts("og_t", [P, KD, P])

        norm = Norm(nc, sb, signal, "a_ln", xn, HT2)
        vec = sem("vec")
        early_loaded, const_loaded, late_loaded = sem("early_loaded"), sem("const_loaded"), sem("late_loaded")
        w_hi_done, w_lo_done = sem("w_hi_done"), sem("w_lo_done")
        k_left_done, decay_raw, decay_done = sem("k_left_done"), sem("decay_raw"), sem("decay_done")
        v_zero, root_set = sem("v_zero"), sem("root_set")
        q_ready, q_sb, k_ready, k_sb = sem("q_ready"), sem("q_sb"), sem("k_ready"), sem("k_sb")
        kv_ready, kv_sb = sem("kv_ready"), sem("kv_sb")
        g1_ready, g1_sb = sem("g1_ready"), sem("g1_sb")
        gate_ready, gate_sb = sem("gate_ready"), sem("gate_sb")
        dec_ready, mask_ready = sem("dec_ready"), sem("mask_ready")
        score_ready, weight_ready = sem("score_ready"), sem("weight_ready")
        outer_ready, outer_masked, state_ready = sem("outer_ready"), sem("outer_masked"), sem("state_ready")
        o_ready, o_sb, o_turned, og_ready = sem("o_ready"), sem("o_sb"), sem("o_turned"), sem("og_ready")
        sq_ready, ss_ready, ms_ready, rrms_ready = sem("sq_ready"), sem("ss_ready"), sem("ms_ready"), sem("rrms_ready")
        scaled, normed = sem("scaled"), sem("normed")
        og_turned, og_hi, og_lo = sem("og_turned"), sem("og_hi"), sem("og_lo")
        y_ready, y_added = sem("y_ready"), sem("y_added")

        front, route, bank_y, bank_turned = ps[:, 0, :], ps[:, 1, :], 2, 3
        bank_s, bank_o, bank_kv = 4, 6, 7
        ident_loaded = sem("ident_loaded")
        early = [(w_qkv, w_qkv_raw, d["Wqkv"]), (w_g1, w_g1_raw, d["Wg1"])]
        late = [(w_o, w_o_raw, d["Wo"]), (w_r, w_r_raw, d["Wr"])]
        consts = [(w_g2, d["Wg2"]), (norm_w, d["norm_w"]), (ld_heads, d["ld_heads"]), (ld_rows, d["ld_rows"]),
                  (gap, d["gap"]), (causal, d["causal"]), (ahead, d["ahead"]), (left, d["left"]),
                  (head_rows, d["head_rows"]), (diagonal, d["diagonal"])]
        block = ctx.enter_context(nc.Block())

        def some(count):
            return not isinstance(count, int) or count > 0

        def exists(chunk):
            return not isinstance(chunk, int) or 0 <= chunk < NT

        def first(b):
            return isinstance(b, int) and b == 0

        def last(b):
            return isinstance(b, int) and b == B - 1

        def batches(eng, body):
            body(0)
            with eng.Fori(1, B - 1) as b:
                body(b)
            body(B - 1)

        def route_slots(u):
            return range(u * HT // UNITS, (u + 1) * HT // UNITS)

        def next_half(u, b):
            nth = u // STEPS_AHEAD + 1
            return 2 * b + nth, nth % 2

        def is_next(u, b):
            return not (last(b) and u >= STEPS_AHEAD)

        def x_half(g, h, b):
            return X[:, bass.ds(b * TT + h * HT2, HT2), :]

        def split_loaded(eng, loads, loaded):
            eng.wait_ge(loaded, 16 * len(loads))
            for w, raw, _ in loads:
                nc.scalar.copy(w.hi[:, :, :], raw[:, :, :]).then_inc(w_hi_done, 1)

        def split_rest(eng, loads, before):
            for i, (w, raw, _) in enumerate(loads):
                eng.wait_ge(w_hi_done, before + i + 1)
                nc.vector.tensor_tensor(w.lo[:, :, :], raw[:, :, :], w.hi[:, :, :].bitcast(F32),
                                        ALU.subtract).then_inc(w_lo_done, 1)

        @block.sync
        def _(sp):
            first_loads(sp, 0)
            sp.dma_start(ident[:, :], d["ident"]).then_inc(ident_loaded, 16)
            for _, raw, src in early:
                sp.dma_start(raw[:, :, :], src.rearrange("p (k n) -> p k n", k=KD)).then_inc(early_loaded, 16)
            for dst, src in consts:
                sp.dma_start(dst[:, :], src).then_inc(const_loaded, 16)
            for _, raw, src in late:
                sp.dma_start(raw[:, :, :], src.rearrange("p (k n) -> p k n", k=KD)).then_inc(late_loaded, 16)
            routing.load_constants(sp)
            first_loads(sp, 1)

        @block.tensor
        def _(pe):
            def project(s, g):
                x = [xt[:, k, :] for k in range(KD)]
                if s == 1:
                    if some(g):
                        pe.wait_ge(kv_sb, HT2 * g)
                    for k in range(KD):
                        norm.turn(pe, g, k, ident, front[:, k * W:(k + 1) * W])
                if s in (2, 3):
                    if s == 2:
                        norm.wait_low(pe, g, KD - 1)
                        pe.wait_ge(w_lo_done, len(early))
                    else:
                        pe.wait_ge(q_sb, g + 1)
                    for m in range(KD):
                        o = (s - 2) * D + m * P
                        ins = product(nc, front[:, m * W:(m + 1) * W], [w_qkv[:, k, o:o + P] for k in range(KD)],
                                      x, True, True)
                    ins.then_inc(q_ready if s == 2 else k_ready, 1)
                if s == 4:
                    pe.wait_ge(k_sb, g + 1)
                    product(nc, front[:, 0:W], [w_g1[:, k, :] for k in range(KD)], x, True,
                            True).then_inc(g1_ready, 1)
                if s in (5, 7):
                    t = (s - 5) // 2
                    if t == 0:
                        pe.wait_ge(g1_sb, g + 1)
                    else:
                        pe.wait_ge(gate_sb, g + 1)
                    product(nc, front, [xt[:, k, t * P:(t + 1) * P] for k in range(KD)],
                            [w_qkv[:, k, D:3 * D] for k in range(KD)], True, True).then_inc(kv_ready, 1)
                if s == 6:
                    pe.wait_ge(kv_sb, HT2 * g + 1)
                    for t in range(HT2):
                        ins = nc.tensor.matmul(front[:, t * D:(t + 1) * D], g1[:, t * P:(t + 1) * P], w_g2[:, :],
                                               start=True, stop=True)
                    ins.then_inc(gate_ready, 1)

            def scores(i, b):
                n, q = i // QUADS, i % QUADS
                pe.wait_ge(mask_ready, UNITS * b + i + 1)
                if q == 0 and n % HT2 == 0:
                    pe.wait_ge(k_sb, 2 * b + n // HT2 + 1)
                if some(UNITS * b + i - 1):
                    pe.wait_ge(weight_ready, UNITS * b + i - 1)
                nc.tensor.matmul(ps[:, bank_s + q % 2, :], k_t[:, q // 2, n * P:(n + 1) * P],
                                 q_mask[:, q % 2, :, :], start=True, stop=True).then_inc(score_ready, 1)

            def outer_product(n, b):
                pe.wait_ge(dec_ready, 2 * (TT * b + n) + 1)
                pe.wait_ge(kv_sb, TT * b + n + 1)
                if some((TT - 1) * b + n):
                    pe.wait_ge(outer_masked, (TT - 1) * b + n)
                for m in range(KD):
                    ins = nc.tensor.matmul(ps[:, bank_kv, m * HH * PAD:(m + 1) * HH * PAD],
                                           k_dec[:, n % 2, m * P:(m + 1) * P],
                                           v_pad[:, n, m * HH:(m + 1) * HH, :], start=True, stop=True)
                ins.then_inc(outer_ready, 1)

            def output(i, b):
                n, q = i // QUADS, i % QUADS
                c = TT * b + n
                if q == 0:
                    pe.wait_ge(kv_sb, c + 1)
                    if some(c):
                        pe.wait_ge(o_sb, c)
                    if n == 1:
                        pe.wait_ge(outer_masked, (TT - 1) * b + 1)
                    if n >= 2:
                        pe.wait_ge(state_ready, (TT - 2) * b + n - 1)
                    if n >= 1:
                        pe.wait_ge(dec_ready, 2 * (c + 1))
                out = ps[:, bank_o, q * P:(q + 1) * P]
                if n >= 1:
                    nc.tensor.matmul(out, state[:, n % 2, q // 2, (q % 2) * P:(q % 2 + 1) * P],
                                     q_dec[:, n % 2, q // 2, :], start=(q == 0), stop=False,
                                     skip_group_check=True)
                pe.wait_ge(weight_ready, UNITS * b + i + 1)
                for j in range(4):
                    ins = nc.tensor.matmul(out[j * PAD:(j + 1) * PAD, :], v_pad[:, n, 4 * q + j, :],
                                           weights[:, q % 2, j, :], start=(q == 0 and n == 0), stop=True,
                                           skip_group_check=True)
                if q == QUADS - 1:
                    ins.then_inc(o_ready, 1)

            def finish(n, q, b):
                c = TT * b + n
                if q == 1 and exists(c - 3):
                    pe.wait_ge(og_hi, c - 2)
                    pe.wait_ge(og_lo, c - 2)
                    pe.wait_ge(w_lo_done, len(early + late))
                    product(nc, ps[:, bank_y, D:2 * D], [og_t[:, k, :] for k in range(KD)],
                            [w_o[:, k, :] for k in range(KD)], True, True).then_inc(y_ready, 1)
                if q == 1 and exists(c - 1):
                    pe.wait_ge(o_sb, c)
                    if some(c - 1):
                        pe.wait_ge(og_ready, c - 1)
                    for j in range(QUADS):
                        ins = nc.tensor.transpose(ps[:, bank_turned, j * P:(j + 1) * P],
                                                  o_t[:, (n - 1) % 2, j * P:(j + 1) * P], ident[:, :])
                    ins.then_inc(o_turned, 1)
                if q == 3 and exists(c - 2):
                    pe.wait_ge(normed, c - 1)
                    if some(c - 2):
                        pe.wait_ge(y_added, c - 2)
                    for k in range(KD):
                        ins = nc.tensor.transpose(ps[:, bank_y, k * P:(k + 1) * P],
                                                  og_norm[:, k * P:(k + 1) * P], ident[:, :])
                    ins.then_inc(og_turned, 1)

            def body(b):
                for u in range(UNITS):
                    n, q = u // QUADS, u % QUADS
                    scores(u, b)
                    if q == 1 and n < TT - 1:
                        outer_product(n, b)
                    if u >= 1:
                        output(u - 1, b)
                    elif not first(b):
                        output(UNITS - 1, b - 1)
                    finish(n, q, b)
                    if is_next(u, b):
                        g, h = next_half(u, b)
                        project(u % STEPS_AHEAD, g)
                    if last(b):
                        for slot in route_slots(u):
                            routing.tensor(pe, slot, 0, route)

            pe.wait_ge(ident_loaded, 16)
            for s in range(STEPS_AHEAD):
                if s == 6:
                    pe.wait_ge(const_loaded, 16 * len(consts))
                project(s, 0)
            batches(pe, body)
            output(UNITS - 1, B - 1)
            for u in range(UNITS, UNITS + DRAIN):
                finish(u // QUADS, u % QUADS, B - 1)

        @block.scalar
        def _(act):
            def project(s, g, h):
                cols = slice(h * W, (h + 1) * W)
                if s == 1:
                    act.wait_ge(norm.turned, KD * (g + 1))
                    nc.scalar.copy(xt.hi[:, :, :],
                                   front.rearrange("p (k n) -> p k n", k=KD)).then_inc(norm.hi_ready, KD)
                if s == 2:
                    act.wait_ge(q_ready, g + 1)
                    nc.scalar.activation(q_t[:, :, cols], front.rearrange("p (m n) -> p m n", m=KD),
                                         ACT.Silu).then_inc(q_sb, 1)
                if s == 3:
                    act.wait_ge(k_ready, g + 1)
                    nc.scalar.activation(k_t[:, :, cols], front.rearrange("p (m n) -> p m n", m=KD),
                                         ACT.Silu).then_inc(k_sb, 1)
                if s == 4:
                    act.wait_ge(g1_ready, g + 1)
                    nc.scalar.copy(g1[:, :], front[:, 0:W]).then_inc(g1_sb, 1)
                if s in (5, 7):
                    t = (s - 5) // 2
                    act.wait_ge(kv_ready, HT2 * g + t + 1)
                    nc.scalar.activation(k_tok[:, HT2 * h + t, :], front[:, 0:D], ACT.Silu)
                    nc.scalar.activation(v_pad[:, HT2 * h + t, :, 0:HD],
                                         front[:, D:2 * D].rearrange("p (h e) -> p h e", e=HD),
                                         ACT.Silu).then_inc(kv_sb, 1)
                if s == 6:
                    act.wait_ge(gate_ready, g + 1)
                    nc.scalar.activation(gate[:, HT2 * h:HT2 * (h + 1), :],
                                         front.rearrange("p (t n) -> p t n", t=HT2),
                                         ACT.Sigmoid).then_inc(gate_sb, 1)

            def finish(n, q, b):
                c = TT * b + n
                if q == 0 and exists(c - 1):
                    act.wait_ge(o_ready, c)
                    if some(c - 2):
                        act.wait_ge(o_turned, c - 2)
                    nc.scalar.copy(o_t[:, (n - 1) % 2, :], ps[:, bank_o, :]).then_inc(o_sb, 1)
                if q == 3 and exists(c - 2):
                    act.wait_ge(og_turned, c - 1)
                    if some(c - 2):
                        act.wait_ge(y_ready, c - 2)
                    nc.scalar.copy(og_t.hi[:, :, :],
                                   ps[:, bank_y, 0:D].rearrange("p (k n) -> p k n", k=KD)).then_inc(og_hi, 1)

            def body(b):
                for u in range(UNITS):
                    finish(u // QUADS, u % QUADS, b)
                    if is_next(u, b):
                        g, h = next_half(u, b)
                        project(u % STEPS_AHEAD, g, h)
                    if last(b):
                        for slot in route_slots(u):
                            routing.scalar(act, slot, 0, route)

            split_loaded(act, early, early_loaded)
            for s in range(STEPS_AHEAD):
                project(s, 0, 0)
                if s == 1:
                    act.wait_ge(const_loaded, 16 * len(consts))
                    for h in range(H):
                        ins = nc.scalar.activation(decay[:, h, :], gap[:, :], ACT.Exp, scale=ld_heads[:, h:h + 1])
                    ins.then_inc(decay_raw, 1)
                    for m in range(KD):
                        nc.scalar.activation(q_decay[:, m, :], ahead[:, :], ACT.Exp, scale=ld_rows[:, m:m + 1])
                    act.wait_ge(k_left_done, 1)
                    nc.scalar.activation(k_decay[:, :], k_left[:, :], ACT.Exp)
                    nc.scalar.activation(chunk_decay[:, :], ld_rows[:, :], ACT.Exp,
                                         scale=float(P)).then_inc(decay_raw, 1)
                    act.wait_ge(v_zero, 1)
            split_loaded(act, late, late_loaded)
            batches(act, body)
            for u in range(UNITS, UNITS + DRAIN):
                finish(u // QUADS, u % QUADS, B - 1)

        @block.gpsimd
        def _(pool):
            def mask(u, b):
                n, q = u // QUADS, u % QUADS
                if q == 0 and n % HT2 == 0:
                    pool.wait_ge(q_sb, 2 * b + n // HT2 + 1)
                if some(UNITS * b + u - 1):
                    pool.wait_ge(score_ready, UNITS * b + u - 1)
                src = q_t[:, q // 2, n * P:(n + 1) * P][:, None, :].broadcast_to([P, 4, P])
                rows = head_rows[:, (q % 2) * 4:(q % 2) * 4 + 4][:, :, None].broadcast_to([P, 4, P])
                nc.gpsimd.tensor_tensor(q_mask[:, q % 2, :, :], src, rows, ALU.mult).then_inc(mask_ready, 1)

            def finish(n, q, b):
                c = TT * b + n
                if q in (0, 1) and exists(c - 2):
                    heads = slice(q * HH, (q + 1) * HH)
                    pool.wait_ge(ms_ready, c - 1)
                    if some(c - 2):
                        pool.wait_ge(scaled, c - 2)
                    nc.gpsimd.tensor_tensor(rrms[:, heads], ms[:, heads], root[:, heads],
                                            ALU.pow).then_inc(rrms_ready, 1)
                if q == 2 and exists(c - 1):
                    pool.wait_ge(og_ready, c)
                    if some(c - 1):
                        pool.wait_ge(ss_ready, c - 1)
                    nc.gpsimd.tensor_tensor(sq[:, :], og[:, (n - 1) % 2, :], og[:, (n - 1) % 2, :],
                                            ALU.mult).then_inc(sq_ready, 1)

            def body(b):
                for u in range(UNITS):
                    if u + 1 < UNITS:
                        mask(u + 1, b)
                    elif not last(b):
                        mask(0, b + 1)
                    finish(u // QUADS, u % QUADS, b)
                    if u % STEPS_AHEAD == STEPS_AHEAD - 1 and not last(b):
                        norm.invert(pool, 2 * b + u // STEPS_AHEAD + 2)
                    if last(b) and u == 1:
                        routing.norm.invert(pool, 0)

            norm.exponent(pool)
            routing.exponent(pool)
            nc.gpsimd.memset(root[:, :], -0.5).then_inc(root_set, 1)
            pool.wait_ge(root_set, 1)
            norm.invert(pool, 0)
            norm.invert(pool, 1)
            pool.wait_ge(const_loaded, 16 * len(consts))
            mask(0, 0)
            batches(pool, body)
            for u in range(UNITS, UNITS + DRAIN):
                finish(u // QUADS, u % QUADS, B - 1)

        @block.vector
        def _(dve):
            def statistics(g, h, b):
                steps = Steps(dve, vec, g * norm.steps)
                norm.statistics(dve, steps, g, x_half(g, h, b))
                assert steps.n == norm.steps

            def project(s, g, h, b):
                if s == 0:
                    norm.scale(dve, g, x_half(g, h, b))
                if s == 1:
                    dve.wait_ge(norm.hi_ready, KD * (g + 1))
                    nc.vector.tensor_tensor(xt.lo[:, :, :], front.rearrange("p (k n) -> p k n", k=KD),
                                            xt.hi[:, :, :].bitcast(F32), ALU.subtract).then_inc(norm.lo_ready, KD)

            def decayed(n, b):
                c = TT * b + n
                dve.wait_ge(kv_sb, c + 1)
                dve.wait_ge(q_sb, 2 * b + n // HT2 + 1)
                if some(c - 1):
                    dve.wait_ge(o_ready, c - 1)
                nc.vector.tensor_tensor(k_dec[:, n % 2, :].rearrange("p (h e) -> p h e", e=HD),
                                        k_tok[:, n, :].rearrange("p (h e) -> p h e", e=HD),
                                        k_decay[:, :, None].broadcast_to([P, H, HD]),
                                        ALU.mult).then_inc(dec_ready, 1)
                nc.vector.tensor_tensor(q_dec[:, n % 2, :, :], q_t[:, :, n * P:(n + 1) * P], q_decay[:, :, :],
                                        ALU.mult).then_inc(dec_ready, 1)

            def weigh(u, b):
                q = u % QUADS
                dve.wait_ge(score_ready, UNITS * b + u + 1)
                nc.vector.tensor_tensor(weights[:, q % 2, :, :],
                                        ps[:, bank_s + q % 2, :].rearrange("p (j c) -> p j c", j=4),
                                        decay[:, 4 * q:4 * q + 4, :], ALU.mult).then_inc(weight_ready, 1)

            def own_blocks(n, b):
                dve.wait_ge(outer_ready, (TT - 1) * b + n + 1)
                if n == 0 and not first(b):
                    dve.wait_ge(o_ready, TT * b)
                    dve.wait_ge(state_ready, (TT - 2) * b)
                if n >= 1 and some((TT - 2) * b + n - 1):
                    dve.wait_ge(state_ready, (TT - 2) * b + n - 1)
                dst = state[:, 1, :, :] if n == 0 else outer[:, :, :]
                ins = nc.vector.tensor_tensor(dst, ps[:, bank_kv, :].rearrange("p (m c) -> p m c", m=KD),
                                              diagonal[:, None, :].broadcast_to([P, KD, HH * PAD]), ALU.mult)
                ins.then_inc(outer_masked, 1)

            def next_state(n, b):
                dve.wait_ge(outer_masked, (TT - 1) * b + n + 1)
                dve.wait_ge(o_ready, TT * b + n)
                if n >= 2:
                    dve.wait_ge(state_ready, (TT - 2) * b + n - 1)
                for m in range(KD):
                    ins = nc.vector.scalar_tensor_tensor(out=state[:, (n + 1) % 2, m, :], in0=state[:, n % 2, m, :],
                                                         scalar=chunk_decay[:, m:m + 1], in1=outer[:, m, :],
                                                         op0=ALU.mult, op1=ALU.add)
                ins.then_inc(state_ready, 1)

            def finish(n, q, b):
                c = TT * b + n
                if q == 0 and exists(c - 3):
                    dve.wait_ge(og_hi, c - 2)
                    nc.vector.tensor_tensor(og_t.lo[:, :, :], ps[:, bank_y, 0:D].rearrange("p (k n) -> p k n", k=KD),
                                            og_t.hi[:, :, :].bitcast(F32), ALU.subtract).then_inc(og_lo, 1)
                if q == 2 and exists(c - 3):
                    dve.wait_ge(y_ready, c - 2)
                    x = X[:, bass.ds(c - 3, 1), :]
                    nc.vector.tensor_tensor(x, x, ps[:, bank_y, D:2 * D][:, None, :], ALU.add).then_inc(y_added, 1)
                if q == 1 and exists(c - 1):
                    dve.wait_ge(o_turned, c)
                    dve.wait_ge(gate_sb, 2 * b + (n - 1) // HT2 + 1)
                    if some(c - 2):
                        dve.wait_ge(normed, c - 2)
                    src = ps[:, bank_turned, :].rearrange("p (h e) -> p h e", e=PAD)[:, :, 0:HD]
                    nc.vector.tensor_tensor(og[:, (n - 1) % 2, :].rearrange("p (h e) -> p h e", e=HD), src,
                                            gate[:, (n - 1) % TT, :].rearrange("p (h e) -> p h e", e=HD),
                                            ALU.mult).then_inc(og_ready, 1)
                if q == 2 and exists(c - 2):
                    rows = og[:, n % 2, :].rearrange("p (h e) -> p h e", e=HD)
                    dve.wait_ge(rrms_ready, 2 * (c - 1))
                    nc.vector.tensor_tensor(rows, rows, rrms[:, :, None].broadcast_to([P, H, HD]),
                                            ALU.mult).then_inc(scaled, 1)
                    dve.wait_ge(scaled, c - 1)
                    if some(c - 2):
                        dve.wait_ge(og_turned, c - 2)
                    nc.vector.tensor_tensor(og_norm[:, :], og[:, n % 2, :], norm_w[:, :], ALU.mult).then_inc(normed, 1)
                if q == 3 and exists(c - 1):
                    dve.wait_ge(sq_ready, c)
                    nc.vector.tensor_reduce(ss[:, :], sq[:, :].rearrange("p (h e) -> p h e", e=HD),
                                            AX.X, ALU.add).then_inc(ss_ready, 1)
                    dve.wait_ge(ss_ready, c)
                    if some(c - 1):
                        dve.wait_ge(rrms_ready, 2 * (c - 1))
                    nc.vector.tensor_scalar(ms[:, :], ss[:, :], 1.0 / HD, 1e-5, ALU.mult, ALU.add).then_inc(ms_ready, 1)

            def body(b):
                done = 0
                for u in range(UNITS):
                    n, q = u // QUADS, u % QUADS
                    if q == 0:
                        decayed(n, b)
                    weigh(u, b)
                    if q == 2 and n < TT - 1:
                        own_blocks(n, b)
                    if q == 3 and 1 <= n < TT - 1:
                        next_state(n, b)
                    finish(n, q, b)
                    if is_next(u, b):
                        g, h = next_half(u, b)
                        project(u % STEPS_AHEAD, g, h, b + (1 if h == 0 else 0))
                    if u % STEPS_AHEAD == STEPS_AHEAD - 1 and not last(b):
                        if first(b) and u < STEPS_AHEAD:
                            dve.wait_ge(x_loaded[1], 16)
                        h = u // STEPS_AHEAD
                        statistics(2 * b + h + 2, h, b + 1)
                    if last(b):
                        for slot in route_slots(u):
                            done = routing.vector(dve, slot, 0, route, done)

            nc.vector.memset(v_pad[:, :, :, :], 0.0).then_inc(v_zero, 1)
            routing.set_constants()
            dve.wait_ge(x_loaded[0], 16)
            statistics(0, 0, 0)
            norm.scale(dve, 0, x_half(0, 0, 0))
            split_rest(dve, early, 0)
            project(1, 0, 0, 0)
            statistics(1, 1, 0)
            dve.wait_ge(const_loaded, 16 * len(consts))
            nc.vector.tensor_scalar(k_left[:, :], ld_heads[:, :], left[:, 0:1], None,
                                    ALU.mult).then_inc(k_left_done, 1)
            dve.wait_ge(decay_raw, 2)
            nc.vector.tensor_tensor(decay[:, :, :], decay[:, :, :], causal[:, None, :].broadcast_to([P, H, P]),
                                    ALU.mult).then_inc(decay_done, 1)
            dve.wait_ge(decay_done, 1)
            split_rest(dve, late, len(early))
            batches(dve, body)
            for u in range(UNITS, UNITS + DRAIN):
                finish(u // QUADS, u % QUADS, B - 1)


class Norm:

    def __init__(self, nc, take, signal, name, xn, tiles=TT):
        def sb(n, shape):
            return take(f"{name}_{n}", shape, F32)

        def sem(n):
            return signal(f"{name}_{n}")

        self.nc, self.xn, self.tiles = nc, xn, tiles
        self.steps = 2 * tiles + 1
        self.stats = sb("stats", [P, tiles, 6])
        self.mean_var = sb("mean_var", [P, tiles, 2])
        self.eps = sb("eps", [P, tiles])
        self.var_eps = sb("var_eps", [P, tiles])
        self.root = sb("root", [P, tiles])
        self.rstd = sb("rstd", [P, tiles])
        self.root_ready = sem("root_ready")
        self.var_ready, self.rstd_ready = sem("var_ready"), sem("rstd_ready")
        self.xn_ready, self.turned = sem("xn_ready"), sem("turned")
        self.hi_ready, self.lo_ready = sem("hi_ready"), sem("lo_ready")

    def exponent(self, eng):
        self.nc.gpsimd.memset(self.root[:, :], -0.5).then_inc(self.root_ready, 1)
        eng.wait_ge(self.root_ready, 1)

    def statistics(self, eng, steps, f, x):
        nc = self.nc
        for t in range(self.tiles):
            steps(nc.vector.bn_stats(self.stats[:, t, :], x[:, t, :]))
        steps.settle()
        steps(nc.vector.memset(self.eps[:, :], 1e-5))
        for t in range(self.tiles):
            steps(nc.vector.bn_aggr(self.mean_var[:, t, :], self.stats[:, t, :]))
        steps.settle()
        nc.vector.tensor_tensor(self.var_eps[:, :], self.mean_var[:, :, 1], self.eps[:, :],
                                ALU.add).then_inc(self.var_ready, 1)

    def invert(self, eng, f):
        eng.wait_ge(self.var_ready, f + 1)
        self.nc.gpsimd.tensor_tensor(self.rstd[:, :], self.var_eps[:, :], self.root[:, :],
                                     ALU.pow).then_inc(self.rstd_ready, 1)

    def scale(self, eng, f, x):
        if not (isinstance(f, int) and f == 0):
            eng.wait_ge(self.turned, KD * f)
        eng.wait_ge(self.rstd_ready, f + 1)
        for t in range(self.tiles):
            self.nc.vector.tensor_scalar(self.xn[:, t, :], x[:, t, :], self.mean_var[:, t, 0:1],
                                         self.rstd[:, t:t + 1], ALU.subtract, ALU.mult).then_inc(self.xn_ready, 1)

    def turn(self, eng, f, k, ident, bank):
        eng.wait_ge(self.xn_ready, self.tiles * (f + 1))
        for t in range(self.tiles):
            ins = self.nc.tensor.transpose(bank[:, t * P:(t + 1) * P], self.xn[:, t, k * P:(k + 1) * P],
                                           ident[:, :])
        ins.then_inc(self.turned, 1)

    def high(self, eng, f, k, xt, bank):
        eng.wait_ge(self.turned, KD * f + k + 1)
        self.nc.scalar.copy(xt.hi[:, k, :], bank[:, 0:self.tiles * P]).then_inc(self.hi_ready, 1)

    def low(self, eng, f, k, xt, bank):
        eng.wait_ge(self.hi_ready, KD * f + k + 1)
        self.nc.vector.tensor_tensor(xt.lo[:, k, :], bank[:, 0:self.tiles * P], xt.hi[:, k, :].bitcast(F32),
                                     ALU.subtract).then_inc(self.lo_ready, 1)

    def wait_low(self, eng, f, k):
        eng.wait_ge(self.lo_ready, KD * f + k + 1)


class Routing:

    def __init__(self, nc, take, signal, name, X, ident, w_r, d):
        SENT = TOPK

        def sb(n, shape, dt=F32):
            return take(f"{name}_{n}", shape, dt)

        def sem(n):
            return signal(f"{name}_{n}")

        self.nc, self.X, self.ident, self.w_r, self.d = nc, X, ident, w_r, d
        self.xt = Parts(sb("xt_hi", [P, KD, 2 * N], F32R), sb("xt_lo", [P, KD, 2 * N], F32R))
        self.shares_t = sb("shares_t", [P, 2 * N], BF16)
        self.spread = sb("spread", [P, HT, P], BF16)
        self.ident_b = sb("ident_b", [P, P], BF16)
        self.xn = sb("xn", [P, TT, D])
        self.logit_t = sb("logit_t", [P, N])
        self.logit = sb("logit", [P, TT, E])
        self.top = sb("top", [P, TT])
        self.ex = sb("ex", [P, TT, E])
        self.den = sb("den", [P, TT])
        self.rden = sb("rden", [P, TT])
        self.prob = sb("prob", [P, TT, E + SENT])
        self.best = sb("best", [P, TT, TOPK])
        self.total = sb("total", [P, TT])
        self.total_c = sb("total_c", [P, TT])
        self.rtotal = sb("rtotal", [P, TT])
        self.renorm = sb("renorm", [P, TT, TOPK])
        self.ones = sb("ones", [P, TOPK])
        self.cum = sb("cum", [P, TT, TOPK])
        self.active = sb("active", [P, TT, TOPK])
        self.kept = sb("kept", [P, TT, TOPK])
        self.inactive = sb("inactive", [P, TT, TOPK])
        self.key = sb("key", [P, TT, TOPK])
        self.mass = sb("mass", [P, TT])
        self.mass_c = sb("mass_c", [P, TT])
        self.rmass = sb("rmass", [P, TT])
        self.rest = sb("rest", [P, TT, E + SENT])
        self.found = sb("found", [P, TT, E])
        self.share = sb("share", [P, TT, E])
        self.left1 = sb("left1", [P, TT, E])
        self.left2 = sb("left2", [P, TT, E])
        self.share_parts = sb("share_parts", [P, TT, P], BF16)

        self.norm = Norm(nc, take, signal, f"{name}_ln", self.xn)
        self.VEC = self.norm.steps + 22 + 3 * TT
        self.vec = sem("vec")
        self.const_loaded, self.const_set = sem("const_loaded"), sem("const_set")
        self.logit_ready, self.logit_sb = sem("logit_ready"), sem("logit_sb")
        self.logit_turned, self.logit_tok = sem("logit_turned"), sem("logit_tok")
        self.shifted, self.exp_done = sem("shifted"), sem("exp_done")
        self.parts_ready, self.parts_turned, self.parts_sb = sem("parts_ready"), sem("parts_turned"), sem("parts_sb")

    def parts(self, f):
        return self.xt[:, :, bass.ds((f % 2) * N, N)]

    def x(self, f):
        return self.X[:, bass.ds(f * TT, TT), :]

    def load_constants(self, sp):
        sp.dma_start(self.spread[:, :, :].bitcast(U16),
                     self.d["spread"].rearrange("p (t n) -> p t n", n=P)).then_inc(self.const_loaded, 16)
        sp.dma_start(self.ident_b[:, :].bitcast(U16), self.d["ident_b"]).then_inc(self.const_loaded, 16)

    def exponent(self, pool):
        self.norm.exponent(pool)

    CONSTANTS = 3

    def set_constants(self):
        nc = self.nc
        nc.vector.memset(self.prob[:, :, E:], -1.0).then_inc(self.const_set, 1)
        nc.vector.memset(self.active[:, :, 0:1], 1.0).then_inc(self.const_set, 1)
        nc.vector.memset(self.share_parts[:, :, 3 * E:], 0.0).then_inc(self.const_set, 1)

    def tensor(self, pe, slot, f, bank):
        nc = self.nc
        if slot == 3:
            if not (isinstance(f, int) and f == 0):
                pe.wait_ge(self.parts_sb, f)
            self.norm.turn(pe, f, 0, self.ident, bank)
        if slot == 5:
            self.norm.wait_low(pe, f, 0)
            self.norm.turn(pe, f, 1, self.ident, bank)
        if slot == 8:
            self.norm.wait_low(pe, f, 1)
            xt = self.parts(f)
            product(nc, bank, [self.w_r[:, k, :] for k in range(KD)], [xt[:, k, :] for k in range(KD)],
                    True, True).then_inc(self.logit_ready, 1)
        if slot == 10:
            pe.wait_ge(self.logit_sb, f + 1)
            for t in range(TT):
                ins = nc.tensor.transpose(bank[:, t * P:(t + 1) * P], self.logit_t[:, t * P:(t + 1) * P],
                                          self.ident[:, :])
            ins.then_inc(self.logit_turned, 1)
        if slot == 21:
            pe.wait_ge(self.parts_ready, f + 1)
            pe.wait_ge(self.const_loaded, 32)
            narrow = bank[:, 0:N // 2].bitcast(BF16)
            for t in range(TT):
                ins = nc.tensor.transpose(narrow[:, t * P:(t + 1) * P], self.share_parts[:, t, :],
                                          self.ident_b[:, :])
            ins.then_inc(self.parts_turned, 1)

    def scalar(self, act, slot, f, bank):
        nc = self.nc
        if slot == 3:
            self.norm.high(act, f, 0, self.parts(f), bank)
        if slot == 6:
            self.norm.high(act, f, 1, self.parts(f), bank)
        if slot == 9:
            act.wait_ge(self.logit_ready, f + 1)
            nc.scalar.copy(self.logit_t[:, :], bank).then_inc(self.logit_sb, 1)
        if slot == 11:
            act.wait_ge(self.logit_turned, f + 1)
            nc.scalar.copy(self.logit[:, :, :],
                           bank.rearrange("p (t e) -> p t e", e=P)[:, :, 0:E]).then_inc(self.logit_tok, 1)
        if slot == 13:
            act.wait_ge(self.shifted, f + 1)
            nc.scalar.activation(self.ex[:, :, :], self.found[:, :, :], ACT.Exp).then_inc(self.exp_done, 1)
        if slot == 22:
            act.wait_ge(self.parts_turned, f + 1)
            nc.scalar.copy(self.shares_t[:, bass.ds((f % 2) * N, N)],
                           bank[:, 0:N // 2].bitcast(BF16)).then_inc(self.parts_sb, 1)

    def vector(self, dve, slot, f, bank, done):
        nc = self.nc
        steps = Steps(dve, self.vec, f * self.VEC)
        steps.n = done

        def each(v, n):
            return v[:, :, None].broadcast_to([P, TT, n])

        if slot == 0:
            self.norm.statistics(dve, steps, f, self.x(f))
        if slot == 1:
            self.norm.scale(dve, f, self.x(f))
        if slot == 4:
            self.norm.low(dve, f, 0, self.parts(f), bank)
        if slot == 7:
            self.norm.low(dve, f, 1, self.parts(f), bank)
        if slot == 12:
            dve.wait_ge(self.logit_tok, f + 1)
            steps(nc.vector.tensor_reduce(self.top[:, :], self.logit[:, :, :], AX.X, ALU.max))
            steps.settle()
            nc.vector.tensor_tensor(self.found[:, :, :], self.logit[:, :, :], each(self.top, E),
                                    ALU.subtract).then_inc(self.shifted, 1)
        if slot == 14:
            dve.wait_ge(self.const_set, self.CONSTANTS)
            dve.wait_ge(self.exp_done, f + 1)
            steps(nc.vector.tensor_reduce(self.den[:, :], self.ex[:, :, :], AX.X, ALU.add))
            steps.settle()
            steps(nc.vector.reciprocal(self.rden[:, :], self.den[:, :]))
            steps.settle()
            steps(nc.vector.tensor_tensor(self.prob[:, :, 0:E], self.ex[:, :, :], each(self.rden, E), ALU.mult))
            steps.settle()
            steps(nc.vector.memset(self.ones[:, :], 1.0))
            for t in range(TT):
                steps(nc.vector.max(self.best[:, t, :], self.prob[:, t, 0:E]))
            steps.settle()
        if slot == 15:
            steps(nc.vector.tensor_reduce(self.total[:, :], self.best[:, :, :], AX.X, ALU.add))
            steps.settle()
            steps(nc.vector.tensor_scalar(self.total_c[:, :], self.total[:, :], 1e-12, None, ALU.max))
            steps.settle()
            steps(nc.vector.reciprocal(self.rtotal[:, :], self.total_c[:, :]))
            steps.settle()
            steps(nc.vector.tensor_tensor(self.renorm[:, :, :], self.best[:, :, :], each(self.rtotal, TOPK),
                                          ALU.mult))
            steps.settle()
        if slot == 16:
            for t in range(TT):
                steps(nc.vector.tensor_tensor_scan(self.cum[:, t, :], self.ones[:, :], self.renorm[:, t, :], 0.0,
                                                   ALU.mult, ALU.add))
            steps.settle()
            steps(nc.vector.tensor_scalar(self.active[:, :, 1:TOPK], self.cum[:, :, 0:TOPK - 1], KEEP, None,
                                          ALU.is_lt))
            steps.settle()
            steps(nc.vector.tensor_tensor(self.kept[:, :, :], self.best[:, :, :], self.active[:, :, :], ALU.mult))
            steps(nc.vector.tensor_scalar(self.inactive[:, :, :], self.active[:, :, :], -1.0, None, ALU.add))
            steps.settle()
        if slot == 17:
            steps(nc.vector.tensor_reduce(self.mass[:, :], self.kept[:, :, :], AX.X, ALU.add))
            steps(nc.vector.tensor_tensor(self.key[:, :, :], self.kept[:, :, :], self.inactive[:, :, :], ALU.add))
            steps.settle()
            steps(nc.vector.tensor_scalar(self.mass_c[:, :], self.mass[:, :], 1e-12, None, ALU.max))
            for t in range(TT):
                steps(nc.vector.match_replace(self.rest[:, t, :], self.key[:, t, :], self.prob[:, t, :], 0.0))
            steps.settle()
        if slot == 18:
            steps(nc.vector.reciprocal(self.rmass[:, :], self.mass_c[:, :]))
            steps(nc.vector.tensor_tensor(self.found[:, :, :], self.prob[:, :, 0:E], self.rest[:, :, 0:E],
                                          ALU.subtract))
            steps.settle()
            steps(nc.vector.tensor_tensor(self.share[:, :, :], self.found[:, :, :], each(self.rmass, E), ALU.mult))
            steps.settle()
        if slot == 19:
            if not (isinstance(f, int) and f == 0):
                dve.wait_ge(self.parts_turned, f)
            steps(nc.vector.tensor_copy(self.share_parts[:, :, 0:E], self.share[:, :, :]))
            steps.settle()
            steps(nc.vector.tensor_tensor(self.left1[:, :, :], self.share[:, :, :], self.share_parts[:, :, 0:E],
                                          ALU.subtract))
            steps.settle()
            steps(nc.vector.tensor_copy(self.share_parts[:, :, E:2 * E], self.left1[:, :, :]))
            steps.settle()
            steps(nc.vector.tensor_tensor(self.left2[:, :, :], self.left1[:, :, :],
                                          self.share_parts[:, :, E:2 * E], ALU.subtract))
            steps.settle()
            nc.vector.tensor_copy(self.share_parts[:, :, 2 * E:3 * E],
                                  self.left2[:, :, :]).then_inc(self.parts_ready, 1)
            assert steps.n == self.VEC, steps.n
        return steps.n


def experts(nc, X, ident, ps, d, name, routing, w_gu, gu_raw, gu_loaded):
    LAG = 2
    RING = LAG + 1
    AHEAD = 2
    LOADS = 4
    with ExitStack() as ctx:
        signal = ctx.enter_context(signals(nc))

        def sb(n, shape, dt=F32):
            return ctx.enter_context(nc.sbuf_tensor(f"{name}_{n}", shape, dt))

        def sem(n):
            return signal(f"{name}_{n}")

        w_d, w_d_raw = loaded_parts(nc, ctx, f"{name}_w_d", [P, HT, D])
        hidden = sb("hidden", [P, RING, N])
        h = Parts(sb("h_hi", [P, RING, N], F32R), sb("h_lo", [P, RING, N], F32R))
        gate_ready, up_ready, share_ready = sem("gate_ready"), sem("up_ready"), sem("share_ready")
        silu_done, gated_done, hidden_done = sem("silu_done"), sem("gated_done"), sem("hidden_done")
        h_hi_ready, h_lo_ready = sem("h_hi_ready"), sem("h_lo_ready")
        down_done, out_added = sem("down_done"), sem("out_added")
        down_loaded = [sem(f"down_loaded{i}") for i in range(LOADS)]
        w_hi_done, w_lo_done = sem("w_hi_done"), sem("w_lo_done")
        bank_share, bank_y, bank_route = 4, 5, ps[:, 7, :]

        split_at = {-1: [("gu", i) for i in range(AHEAD)] + [("down", 0)]}
        for i in range(HT):
            split_at[i] = [(matrix, tile) for matrix, tile in (("gu", i + AHEAD), ("down", i + 1)) if tile < HT]
        if gu_loaded is None:
            split_at = {slot: [p for p in pieces if p[0] == "down"] for slot, pieces in split_at.items()}
        order = [piece for slot in range(-1, HT) for piece in split_at[slot]]

        def piece_parts(matrix, tile):
            if matrix == "down":
                return Parts(w_d.hi[:, tile, :], w_d.lo[:, tile, :]), w_d_raw[:, tile, :]
            hi, lo, raw = (w[:, :, :].rearrange("p k (s n) -> p k s n", s=2)[:, :, :, tile * P:(tile + 1) * P]
                           for w in (w_gu.hi, w_gu.lo, gu_raw))
            return Parts(hi, lo), raw

        def wait_split(eng, matrix, tile):
            if (matrix, tile) in order:
                eng.wait_ge(w_hi_done, order.index((matrix, tile)) + 1)
                eng.wait_ge(w_lo_done, order.index((matrix, tile)) + 1)

        block = ctx.enter_context(nc.Block())

        def first(b):
            return isinstance(b, int) and b == 0

        def batches(eng, body):
            body(0, True)
            with eng.Fori(1, B - 1) as b:
                body(b, True)
            body(B - 1, False)

        @block.sync
        def _(sp):
            for i in range(LOADS):
                tiles = slice(i * HT // LOADS, (i + 1) * HT // LOADS)
                sp.dma_start(w_d_raw[:, tiles, :],
                             d["Wdown"].rearrange("p (t n) -> p t n", n=D)[:, tiles, :]).then_inc(down_loaded[i], 16)

        @block.gpsimd
        def _(pool):
            for i, piece in enumerate(order):
                w, raw = piece_parts(*piece)
                pool.wait_ge(w_hi_done, i + 1)
                nc.gpsimd.tensor_tensor(w.lo, raw, w.hi.bitcast(F32),
                                        ALU.subtract).then_inc(w_lo_done, 1)
                if piece == ("down", 1):
                    routing.norm.invert(pool, 1)
            with pool.Fori(2, B) as f:
                routing.norm.invert(pool, f)

        @block.tensor
        def _(pe):
            def down(tile, j, b):
                pe.wait_ge(h_lo_ready, tile + 1)
                if first(b):
                    wait_split(pe, "down", j)
                if j == 0 and not first(b):
                    pe.wait_ge(out_added, b)
                for t in range(TT):
                    ins = product(nc, ps[:, bank_y + t // 2, (t % 2) * D:(t % 2 + 1) * D],
                                  [h[:, j % RING, t * P:(t + 1) * P]], [w_d[:, j, :]],
                                  j == 0 and t % 2 == 0, j == HT - 1)
                ins.then_inc(down_done, 1)

            def body(b, route):
                xt = routing.parts(b)
                x = [xt[:, k, :] for k in range(KD)]
                shares = routing.shares_t[:, bass.ds((b % 2) * N, N)]
                pe.wait_ge(routing.parts_sb, b + 1)
                routing.norm.wait_low(pe, b, KD - 1)
                for i in range(HT):
                    tile = HT * b + i
                    ahead = i >= 2 or not first(b)
                    if first(b):
                        wait_split(pe, "gu", i)
                    if ahead:
                        pe.wait_ge(silu_done, tile - 1)
                    product(nc, ps[:, i % 2, :], [w_gu[:, k, i * P:(i + 1) * P] for k in range(KD)], x,
                            True, True).then_inc(gate_ready, 1)
                    if ahead:
                        pe.wait_ge(gated_done, tile - 1)
                    o = E * INTER + i * P
                    product(nc, ps[:, 2 + i % 2, :], [w_gu[:, k, o:o + P] for k in range(KD)], x,
                            True, True).then_inc(up_ready, 1)
                    if i >= 1 or not first(b):
                        pe.wait_ge(hidden_done, tile)
                    nc.tensor.matmul(ps[:, bank_share, :], routing.spread[:, i, :], shares,
                                     start=True, stop=True).then_inc(share_ready, 1)
                    if i >= LAG:
                        down(tile - LAG, i - LAG, b)
                    elif not first(b):
                        down(tile - LAG, HT + i - LAG, b - 1)
                    if route:
                        routing.tensor(pe, i, b + 1, bank_route)
                if first(b):
                    wait_split(pe, "down", HT - 1)

            batches(pe, body)
            for i in range(LAG):
                down(HT * B + i - LAG, HT + i - LAG, B - 1)

        @block.scalar
        def _(act):
            def split(slot):
                for matrix, tile in split_at[slot]:
                    if matrix == "gu" and tile == 0:
                        act.wait_ge(gu_loaded, 16)
                    if matrix == "down" and tile % (HT // LOADS) == 0:
                        act.wait_ge(down_loaded[tile // (HT // LOADS)], 16)
                    w, raw = piece_parts(matrix, tile)
                    nc.scalar.copy(w.hi, raw).then_inc(w_hi_done, 1)

            def high(tile, j):
                act.wait_ge(hidden_done, tile + 1)
                if j >= RING or not isinstance(tile, int) or tile >= RING:
                    act.wait_ge(down_done, tile - RING + 1)
                nc.scalar.copy(h.hi[:, j % RING, :], hidden[:, j % RING, :]).then_inc(h_hi_ready, 1)

            def body(b, route):
                for i in range(HT):
                    tile = HT * b + i
                    act.wait_ge(gate_ready, tile + 1)
                    if i >= RING or not first(b):
                        act.wait_ge(h_lo_ready, tile - RING + 1)
                    nc.scalar.activation(hidden[:, i % RING, :], ps[:, i % 2, :], ACT.Silu).then_inc(silu_done, 1)
                    if first(b):
                        split(i)
                    if i >= 1 or not first(b):
                        high(tile - 1, (i - 1) % HT)
                    if route:
                        routing.scalar(act, i, b + 1, bank_route)

            split(-1)
            batches(act, body)
            high(HT * B - 1, HT - 1)

        @block.vector
        def _(dve):
            def low(tile, j):
                dve.wait_ge(h_hi_ready, tile + 1)
                nc.vector.tensor_tensor(h.lo[:, j % RING, :], hidden[:, j % RING, :],
                                        h.hi[:, j % RING, :].bitcast(F32), ALU.subtract).then_inc(h_lo_ready, 1)

            def add_out(b):
                dve.wait_ge(down_done, HT * (b + 1))
                for y in range(2):
                    x = X[:, bass.ds(b * TT + 2 * y, 2), :]
                    ins = nc.vector.tensor_tensor(x, x, ps[:, bank_y + y, :].rearrange("p (t n) -> p t n", t=2),
                                                  ALU.add)
                ins.then_inc(out_added, 1)

            def body(b, route):
                done = 0
                for i in range(HT):
                    tile = HT * b + i
                    rows = hidden[:, i % RING, :]
                    dve.wait_ge(silu_done, tile + 1)
                    dve.wait_ge(up_ready, tile + 1)
                    nc.vector.tensor_tensor(rows, ps[:, 2 + i % 2, :], rows, ALU.mult).then_inc(gated_done, 1)
                    dve.wait_ge(gated_done, tile + 1)
                    dve.wait_ge(share_ready, tile + 1)
                    nc.vector.tensor_tensor(rows, ps[:, bank_share, :], rows, ALU.mult).then_inc(hidden_done, 1)
                    if i >= 1 or not first(b):
                        low(tile - 1, (i - 1) % HT)
                    if i == LAG - 1 and not first(b):
                        add_out(b - 1)
                    if route:
                        done = routing.vector(dve, i, b + 1, bank_route, done)

            batches(dve, body)
            low(HT * B - 1, HT - 1)
            add_out(B - 1)


def attention(nc, X, ident, ps, d, area, routing):
    PAIRS = H // 2
    SRC = 4 * HD
    GROUP = TT * 2
    UNITS = KV * GROUP
    ROT = D + KV * HD
    HEADS = H + KV
    LAG = 2
    RING = LAG + 1
    LATE = 6
    with ExitStack() as ctx:
        signal = ctx.enter_context(signals(nc))

        def sb(n, shape, dt=F32):
            return ctx.enter_context(nc.sbuf_tensor(f"b_{n}", shape, dt))

        def sem(n):
            return signal(f"b_{n}")

        w_qkv, w_qkv_raw = loaded_parts(nc, ctx, "b_w_qkv", [P, KD * QKV])
        wqkv = Parts(*(w.rearrange("p (k n) -> p k n", k=KD) for w in (w_qkv.hi[:, :], w_qkv.lo[:, :])))
        w_out, w_out_raw = loaded_parts(nc, ctx, "b_w_out", [P, KD, D])
        cos = sb("cos", [P, TT, HD])
        sin = sb("sin", [P, TT, HD])
        ahead = Placer(area, "b")
        xt = Parts(ahead.take("xt_hi", [P, KD, N], F32R), ahead.take("xt_lo", [P, KD, N], F32R))
        work = ahead.take("work", [P, TT * H * SRC], F32)
        raw = ahead.take("raw", [P, TT, QKV], F32)
        k4 = ahead.take("k4", [P, TT * KV, 3 * SRC], F32)
        q_t = sb("q_t", [P, PAIRS, N], F32R)
        k_t = sb("k_t", [P, 2 * KV, N], F32R)
        v_pad = sb("v_pad", [P, TT, KV, PAD])
        ssq = sb("ssq", [P, 2, TT])
        mean_sq = sb("mean_sq", [P, 2, TT])
        rrms = sb("rrms", [P, 2, TT])
        root = sb("root", [P, 2, TT])
        probs = sb("probs", [P, RING, 2, N])
        enc = sb("enc", [P, N])
        rsum = sb("rsum", [P, TT, G])
        heads = sb("heads", [P, TT, D])
        heads_t = Parts(sb("heads_t_hi", [P, KD, 2 * P], F32R), sb("heads_t_lo", [P, KD, 2 * P], F32R))
        xn = work[:, 0:TT * D].rearrange("p (t n) -> p t n", t=TT)
        term1 = work[:, 0:TT * ROT].rearrange("p (t n) -> p t n", t=TT)
        term2 = work[:, TT * ROT:2 * TT * ROT].rearrange("p (t n) -> p t n", t=TT)
        q4 = work[:, :].rearrange("p (r c) -> p r c", c=SRC)

        norm = Norm(nc, sb, signal, "ln", xn)
        vec, const_loaded, zeroed, root_set = sem("vec"), sem("const_loaded"), sem("zeroed"), sem("root_set")
        qkv_ready, qkv_sb, squares_done = sem("qkv_ready"), sem("qkv_sb"), sem("squares_done")
        mean_ready, rrms_ready, rotated = sem("mean_ready"), sem("rrms_ready"), sem("rotated")
        q_hi, k_hi, q4_ready, k4_ready = sem("q_hi"), sem("k_hi"), sem("q4_ready"), sem("k4_ready")
        q_turned, k_turned, q_parts, k_parts = sem("q_turned"), sem("k_turned"), sem("q_parts"), sem("k_parts")
        v_copied = sem("v_copied")
        logits_ready, exp_done, pv_done = sem("logits_ready"), sem("exp_done"), sem("pv_done")
        enc_sb, enc_turned, rsum_ready, head_ready = (sem("enc_sb"), sem("enc_turned"), sem("rsum_ready"),
                                                      sem("head_ready"))
        heads_turned, heads_hi, heads_lo = sem("heads_turned"), sem("heads_hi"), sem("heads_lo")
        y_ready, y_added = sem("y_ready"), sem("y_added")
        w_loaded, w_hi_done, w_lo_done = sem("w_loaded"), sem("w_hi_done"), sem("w_lo_done")
        VEC = norm.steps + 6
        FINISH = 10
        ROUTE = 5
        bank_pv, bank_out, bank_route = 6, 7, ps[:, 4, :]
        block = ctx.enter_context(nc.Block())
        consts = [(w_out_raw[:, :, :].rearrange("p k n -> p (k n)"), d["Wout"]),
                  (cos[:, :, :].rearrange("p t n -> p (t n)"), d["cos"]),
                  (sin[:, :, :].rearrange("p t n -> p (t n)"), d["sin"])]
        raw_q = raw[:, :, 0:D]
        raw_k = raw[:, :, D:ROT]
        q4v = q4.rearrange("p (t h) c -> p t h c", t=TT)
        k4v = k4[:, :, :].rearrange("p (t g) c -> p t g c", t=TT)

        def by_head(v):
            return v.rearrange("p t (h e) -> p t h e", e=HD)

        def first(b):
            return isinstance(b, int) and b == 0

        def last(b):
            return isinstance(b, int) and b == B - 1

        def x_of(f):
            return X[:, bass.ds(f * TT, TT), :]

        def wait_free(eng):
            eng.wait_ge(q_turned, PAIRS * B)
            eng.wait_ge(k_turned, PAIRS * B)
            eng.wait_ge(v_copied, KV * B)

        def batches(eng, body):
            body(0, True)
            with eng.Fori(1, B - 1) as b:
                body(b, True)
            body(B - 1, False)

        @block.sync
        def _(sp):
            sp.dma_start(w_qkv_raw[:, :], d["WqkvB"]).then_inc(w_loaded, 16)
            for dst, src in consts:
                sp.dma_start(dst, src).then_inc(const_loaded, 16)
            wait_free(sp)
            routing.load_constants(sp)

        @block.tensor
        def _(pe):
            def prepare(slot, f):
                if slot == 6:
                    if not first(f):
                        pe.wait_ge(q_parts, PAIRS * f)
                        pe.wait_ge(k_parts, PAIRS * f)
                    for k in range(KD):
                        norm.turn(pe, f, k, ident, ps[:, 4 + k, :])
                if 9 <= slot < 9 + TT:
                    t = slot - 9
                    if t == 0:
                        norm.wait_low(pe, f, KD - 1)
                        pe.wait_ge(w_lo_done, 1)
                    if t >= 2:
                        pe.wait_ge(qkv_sb, TT * f + t - 1)
                    product(nc, ps[:, 4 + t % 2, 0:QKV], [xt[:, k, t * P:(t + 1) * P] for k in range(KD)],
                            [wqkv[:, k, :] for k in range(KD)], True, True).then_inc(qkv_ready, 1)
                if 24 <= slot < 24 + LATE:
                    turn(f, slot - 24)

            def turn(f, i):
                if i == 0:
                    pe.wait_ge(qkv_sb, TT * (f + 1))
                    pe.wait_ge(q4_ready, f + 1)
                    pe.wait_ge(k4_ready, f + 1)
                else:
                    pe.wait_ge(q_parts, PAIRS * f + i)
                    pe.wait_ge(k_parts, PAIRS * f + i)
                for t in range(TT):
                    rows = q4[:, t * H + 2 * i:t * H + 2 * i + 2, :].rearrange("p r c -> p (r c)")
                    ins = nc.tensor.transpose(ps[:, 4, t * P:(t + 1) * P], rows, ident[:, :])
                ins.then_inc(q_turned, 1)
                g, low = i // 2, i % 2
                for t in range(TT):
                    src = k4[:, t * KV + g, (1 - low) * SRC:(1 - low) * SRC + P]
                    ins = nc.tensor.transpose(ps[:, 5, t * P:(t + 1) * P], src, ident[:, :])
                ins.then_inc(k_turned, 1)

            def logits(u, b):
                g, st, jp = u // GROUP, u // 2 % TT, u % 2
                if u % GROUP == 0:
                    pe.wait_ge(q_parts, PAIRS * b + 2 * g + 2)
                    pe.wait_ge(k_parts, PAIRS * b + 2 * g + 2)
                if u >= 2 or not first(b):
                    pe.wait_ge(exp_done, UNITS * b + u - 1)
                for j in range(2):
                    ins = nc.tensor.matmul(ps[:, 2 * (u % 2) + j, :], k_t[:, 2 * g + j, st * P:(st + 1) * P],
                                           q_t[:, 2 * g + jp, :], start=True, stop=True)
                ins.then_inc(logits_ready, 1)

            def values(u, b):
                g, st, jp = u // GROUP, u // 2 % TT, u % 2
                if u % GROUP == 0:
                    pe.wait_ge(v_copied, KV * b + g + 1)
                    if g >= 1 or not first(b):
                        pe.wait_ge(enc_sb, KV * b + g)
                pe.wait_ge(exp_done, UNITS * b + u + 1)
                for j in range(2 * jp, 2 * jp + 2):
                    ins = nc.tensor.matmul(ps[j * PAD:(j + 1) * PAD, bank_pv, :], v_pad[:, st, g, :],
                                           probs[:, u % RING, j % 2, :], start=(st == 0), stop=(st == TT - 1),
                                           skip_group_check=True)
                ins.then_inc(pv_done, 1)

            def turn_values(g, b):
                pe.wait_ge(enc_sb, KV * b + g + 1)
                if g >= 1:
                    pe.wait_ge(head_ready, KV * b + g)
                elif not first(b):
                    pe.wait_ge(y_added, 2 * b)
                for t in range(TT):
                    ins = nc.tensor.transpose(ps[:, bank_out, t * P:(t + 1) * P], enc[:, t * P:(t + 1) * P],
                                              ident[:, :])
                ins.then_inc(enc_turned, 1)

            def turn_heads(y, b):
                if y == 0:
                    pe.wait_ge(head_ready, KV * (b + 1))
                else:
                    pe.wait_ge(y_added, 2 * b + 1)
                for k in range(KD):
                    for t in range(2):
                        ins = nc.tensor.transpose(ps[:, bank_out, (2 * k + t) * P:(2 * k + t + 1) * P],
                                                  heads[:, 2 * y + t, k * P:(k + 1) * P], ident[:, :])
                ins.then_inc(heads_turned, 1)

            def project(y, b):
                pe.wait_ge(heads_lo, 2 * b + y + 1)
                if first(b) and y == 0:
                    pe.wait_ge(w_lo_done, 2)
                for t in range(2):
                    ins = product(nc, ps[:, bank_out, t * D:(t + 1) * D],
                                  [heads_t[:, k, t * P:(t + 1) * P] for k in range(KD)],
                                  [w_out[:, k, :] for k in range(KD)], True, True)
                ins.then_inc(y_ready, 1)

            def finish(slot, b):
                if slot == 3:
                    turn_values(KV - 1, b)
                if slot == 4:
                    turn_heads(0, b)
                if slot == 6:
                    project(0, b)
                if slot == 7:
                    turn_heads(1, b)
                if slot == 9:
                    project(1, b)

            def body(b, more):
                for u in range(UNITS):
                    logits(u, b)
                    if u >= LAG:
                        values(u - LAG, b)
                    elif not first(b):
                        values(UNITS + u - LAG, b - 1)
                    if u % GROUP == 3 and u > GROUP:
                        turn_values(u // GROUP - 1, b)
                    if u in (1, 3):
                        turn(b, LATE + u // 2)
                    if not first(b):
                        finish(u, b - 1)
                    if more:
                        prepare(u, b + 1)
                    if last(b) and u >= ROUTE:
                        if u == ROUTE:
                            pe.wait_ge(q_parts, PAIRS * B)
                        routing.tensor(pe, u - ROUTE, 0, bank_route)

            for slot in range(UNITS):
                prepare(slot, 0)
            batches(pe, body)
            for u in range(UNITS - LAG, UNITS):
                values(u, B - 1)
            for slot in range(FINISH):
                finish(slot, B - 1)

        @block.scalar
        def _(act):
            def prepare(slot, f):
                if slot == 7:
                    for k in range(KD):
                        norm.high(act, f, k, xt, ps[:, 4 + k, :])
                if 10 <= slot < 10 + TT:
                    t = slot - 10
                    if t == 0 and not first(f):
                        act.wait_ge(v_copied, KV * f)
                    act.wait_ge(qkv_ready, TT * f + t + 1)
                    nc.scalar.copy(raw[:, t, :], ps[:, 4 + t % 2, 0:QKV]).then_inc(qkv_sb, 1)
                if slot == 21:
                    act.wait_ge(rotated, f + 1)
                    nc.scalar.copy(q4v[:, :, :, 0:HD].bitcast(F32R), by_head(raw_q)).then_inc(q_hi, 1)
                if slot == 22:
                    nc.scalar.copy(q4v[:, :, :, HD:2 * HD].bitcast(F32R), by_head(raw_q)).then_inc(q_hi, 1)
                if slot == 23:
                    for c in (0, 2):
                        nc.scalar.copy(k4v[:, :, :, SRC + c * HD:SRC + (c + 1) * HD].bitcast(F32R),
                                       by_head(raw_k)).then_inc(k_hi, 1)
                if 25 <= slot < 25 + LATE:
                    q_out(f, slot - 25)

            def q_out(f, i):
                act.wait_ge(q_turned, PAIRS * f + i + 1)
                nc.scalar.copy(q_t[:, i, :], ps[:, 4, :]).then_inc(q_parts, 1)

            def finish(slot, b):
                if slot in (5, 8):
                    y = 0 if slot == 5 else 1
                    act.wait_ge(heads_turned, 2 * b + y + 1)
                    nc.scalar.copy(heads_t.hi[:, :, :],
                                   ps[:, bank_out, :].rearrange("p (k n) -> p k n", k=KD)).then_inc(heads_hi, 1)

            def body(b, more):
                for u in range(UNITS):
                    if not first(b):
                        finish(u, b - 1)
                    if u in (2, 4):
                        q_out(b, LATE + u // 2 - 1)
                    if more:
                        prepare(u, b + 1)
                    act.wait_ge(logits_ready, UNITS * b + u + 1)
                    if u >= RING:
                        act.wait_ge(pv_done, UNITS * b + u - RING + 1)
                    elif not first(b):
                        last_use = (UNITS - 1 - u) // RING * RING + u
                        act.wait_ge(pv_done, UNITS * (b - 1) + last_use + 1)
                    nc.scalar.activation(probs[:, u % RING, :, :], ps[:, 2 * (u % 2):2 * (u % 2) + 2, :], ACT.Exp,
                                         scale=float(HD) ** -0.5).then_inc(exp_done, 1)
                    if last(b) and u >= ROUTE:
                        routing.scalar(act, u - ROUTE, 0, bank_route)

            act.wait_ge(w_loaded, 16)
            nc.scalar.copy(w_qkv.hi[:, :], w_qkv_raw[:, :]).then_inc(w_hi_done, 1)
            act.wait_ge(const_loaded, 16 * len(consts))
            for slot in range(UNITS):
                if slot == 23:
                    act.wait_ge(zeroed, 3)
                prepare(slot, 0)
            nc.scalar.copy(w_out.hi[:, :, :], w_out_raw[:, :, :]).then_inc(w_hi_done, 1)
            batches(act, body)
            for slot in range(FINISH):
                finish(slot, B - 1)

        @block.gpsimd
        def _(pool):
            def prepare(f):
                if not first(f):
                    norm.invert(pool, f)
                for t in range(TT):
                    pool.wait_ge(qkv_sb, TT * f + t + 1)
                    nc.gpsimd.tensor_tensor(term2[:, t, :], raw[:, t, 0:ROT], raw[:, t, 0:ROT],
                                            ALU.mult).then_inc(squares_done, 1)
                pool.wait_ge(mean_ready, f + 1)
                nc.gpsimd.tensor_tensor(rrms[:, :, :], mean_sq[:, :, :], root[:, :, :],
                                        ALU.pow).then_inc(rrms_ready, 1)

            def body(b, more):
                if more:
                    prepare(b + 1)
                if last(b):
                    wait_free(pool)
                    routing.exponent(pool)
                    routing.norm.invert(pool, 0)

            norm.exponent(pool)
            nc.gpsimd.memset(root[:, :, :], -0.5).then_inc(root_set, 1)
            norm.invert(pool, 0)
            nc.gpsimd.memset(k4[:, :, :], 0.0).then_inc(zeroed, 1)
            nc.gpsimd.memset(v_pad[:, :, :, :], 0.0).then_inc(zeroed, 1)
            pool.wait_ge(zeroed, 2)
            nc.gpsimd.memset(v_pad[:, :, :, HD:HD + 1], 1.0).then_inc(zeroed, 1)
            pool.wait_ge(root_set, 1)
            prepare(0)
            batches(pool, body)

        @block.vector
        def _(dve):
            half = HD // 2

            def table(v, o, n):
                return v[:, :, None, o:o + n].broadcast_to([P, TT, HEADS, n])

            def prepare(slot, f, done):
                steps = Steps(dve, vec, f * VEC)
                steps.n = done
                rows, t1, t2 = by_head(raw[:, :, 0:ROT]), by_head(term1), by_head(term2)
                if slot == 0:
                    norm.statistics(dve, steps, f, x_of(f))
                if slot == 5:
                    if not first(f):
                        dve.wait_ge(q_turned, PAIRS * f)
                    norm.scale(dve, f, x_of(f))
                if slot == 8:
                    for k in range(KD):
                        norm.low(dve, f, k, xt, ps[:, 4 + k, :])
                if slot == 14:
                    dve.wait_ge(qkv_sb, TT * (f + 1))
                    if first(f):
                        dve.wait_ge(const_loaded, 16 * len(consts))
                    steps(nc.vector.tensor_tensor(t1, rows, table(cos, 0, HD), ALU.mult))
                if slot == 16:
                    dve.wait_ge(squares_done, TT * (f + 1))
                    steps(nc.vector.tensor_reduce(ssq[:, 0, :], term2[:, :, 0:D], AX.X, ALU.add))
                    steps(nc.vector.tensor_reduce(ssq[:, 1, :], term2[:, :, D:ROT], AX.X, ALU.add))
                    steps.settle()
                    nc.vector.tensor_scalar(mean_sq[:, 0, :], ssq[:, 0, :], 1.0 / D, 1e-6, ALU.mult, ALU.add)
                    nc.vector.tensor_scalar(mean_sq[:, 1, :], ssq[:, 1, :], 1.0 / (KV * HD), 1e-6, ALU.mult,
                                            ALU.add).then_inc(mean_ready, 1)
                if slot == 17:
                    steps(nc.vector.tensor_tensor(t2[:, :, :, 0:half], rows[:, :, :, half:HD], table(sin, 0, half),
                                                  ALU.mult))
                    steps(nc.vector.tensor_tensor(t2[:, :, :, half:HD], rows[:, :, :, 0:half],
                                                  table(sin, half, half), ALU.mult))
                    steps.settle()
                if slot == 18:
                    steps(nc.vector.tensor_tensor(raw[:, :, 0:ROT], term1, term2, ALU.add))
                    steps.settle()
                if slot == 19:
                    dve.wait_ge(rrms_ready, f + 1)
                    nc.vector.tensor_tensor(raw_q, raw_q, rrms[:, 0, :, None].broadcast_to([P, TT, D]), ALU.mult)
                    nc.vector.tensor_tensor(raw_k, raw_k, rrms[:, 1, :, None].broadcast_to([P, TT, KV * HD]),
                                            ALU.mult).then_inc(rotated, 1)
                if slot == 22:
                    dve.wait_ge(q_hi, 2 * f + 1)
                    dve.wait_ge(rotated, f + 1)
                    for c in (2, 3):
                        ins = nc.vector.tensor_tensor(q4v[:, :, :, c * HD:(c + 1) * HD], by_head(raw_q),
                                                      q4v[:, :, :, 0:HD], ALU.subtract)
                    ins.then_inc(q4_ready, 1)
                if slot == 23:
                    dve.wait_ge(q_hi, 2 * (f + 1))
                    dve.wait_ge(k_hi, 2 * (f + 1))
                    for c in (1, 3):
                        ins = nc.vector.tensor_tensor(k4v[:, :, :, SRC + c * HD:SRC + (c + 1) * HD], by_head(raw_k),
                                                      k4v[:, :, :, SRC:SRC + HD], ALU.subtract)
                    ins.then_inc(k4_ready, 1)
                    assert steps.n == VEC, steps.n
                if 25 <= slot < 25 + LATE:
                    k_out(f, slot - 25)
                if slot in (25, 26, 27):
                    copy_v(slot - 25)
                return steps.n

            def copy_v(g):
                o = ROT + g * HD
                nc.vector.tensor_copy(v_pad[:, :, g, 0:HD], raw[:, :, o:o + HD]).then_inc(v_copied, 1)

            def k_out(f, i):
                dve.wait_ge(k_turned, PAIRS * f + i + 1)
                nc.vector.tensor_copy(k_t[:, i, :], ps[:, 5, :]).then_inc(k_parts, 1)

            def encode(g, b):
                dve.wait_ge(pv_done, UNITS * b + GROUP * (g + 1))
                if g >= 1 or not first(b):
                    dve.wait_ge(enc_turned, KV * b + g)
                nc.vector.tensor_copy(enc[:, :], ps[:, bank_pv, :]).then_inc(enc_sb, 1)

            def normalise(g, b):
                dve.wait_ge(enc_turned, KV * b + g + 1)
                if g == 0 and not first(b):
                    dve.wait_ge(heads_turned, 2 * b)
                values = ps[:, bank_out, :].rearrange("p (t j e) -> p t j e", t=TT, j=G)
                nc.vector.reciprocal(rsum[:, :, :], values[:, :, :, HD]).then_inc(rsum_ready, 1)
                dve.wait_ge(rsum_ready, KV * b + g + 1)
                nc.vector.tensor_tensor(by_head(heads[:, :, :])[:, :, g * G:(g + 1) * G, :], values[:, :, :, 0:HD],
                                        rsum[:, :, :, None].broadcast_to([P, TT, G, HD]),
                                        ALU.mult).then_inc(head_ready, 1)

            def add_out(y, b):
                dve.wait_ge(y_ready, 2 * b + y + 1)
                x = X[:, bass.ds(b * TT + 2 * y, 2), :]
                nc.vector.tensor_tensor(x, x, ps[:, bank_out, :].rearrange("p (t n) -> p t n", t=2),
                                        ALU.add).then_inc(y_added, 1)

            def finish(slot, b):
                if slot == 1:
                    encode(KV - 1, b)
                if slot == 3:
                    normalise(KV - 1, b)
                if slot in (5, 8):
                    y = 0 if slot == 5 else 1
                    dve.wait_ge(heads_hi, 2 * b + y + 1)
                    nc.vector.tensor_tensor(heads_t.lo[:, :, :],
                                            ps[:, bank_out, :].rearrange("p (k n) -> p k n", k=KD),
                                            heads_t.hi[:, :, :].bitcast(F32), ALU.subtract).then_inc(heads_lo, 1)
                if slot == 6:
                    add_out(0, b)
                if slot == 9:
                    add_out(1, b)

            def body(b, more):
                done = 0
                for u in range(UNITS):
                    if u % GROUP == 1 and u > GROUP:
                        encode(u // GROUP - 1, b)
                    if u % GROUP == 4 and u > GROUP:
                        normalise(u // GROUP - 1, b)
                    if not first(b):
                        finish(u, b - 1)
                    if u == 1:
                        copy_v(KV - 1)
                    if u in (2, 4):
                        k_out(b, LATE + u // 2 - 1)
                    if more:
                        done = prepare(u, b + 1, done)
                    if last(b) and u >= ROUTE:
                        if u == ROUTE:
                            wait_free(dve)
                            routing.set_constants()
                        done = routing.vector(dve, u - ROUTE, 0, bank_route, done)

            done = 0
            for slot in range(UNITS):
                if slot == 23:
                    dve.wait_ge(zeroed, 3)
                done = prepare(slot, 0, done)
                if slot == 0:
                    dve.wait_ge(w_hi_done, 1)
                    nc.vector.tensor_tensor(w_qkv.lo[:, :], w_qkv_raw[:, :], w_qkv.hi[:, :].bitcast(F32),
                                            ALU.subtract).then_inc(w_lo_done, 1)
            dve.wait_ge(w_hi_done, 2)
            nc.vector.tensor_tensor(w_out.lo[:, :, :], w_out_raw[:, :, :], w_out.hi[:, :, :].bitcast(F32),
                                    ALU.subtract).then_inc(w_lo_done, 1)
            batches(dve, body)
            for slot in range(FINISH):
                finish(slot, B - 1)


def program(nc, d, out):
    x_rows = d["x"].rearrange("b (t p) n -> p (b t) n", p=P)
    out_rows = out.rearrange("b (t p) n -> p (b t) n", p=P)
    with ExitStack() as ctx:
        signal = ctx.enter_context(signals(nc))

        def sb(n, shape, dt=F32):
            return ctx.enter_context(nc.sbuf_tensor(n, shape, dt))

        X = sb("X", [P, NT, D])
        ident = sb("ident", [P, P])
        ps = ctx.enter_context(nc.psum_tensor("ps", [P, 8, N], F32))
        gu_shape = [P, KD, 2 * E * INTER]
        gu_area = Area(nc, ctx, "gu_area", KD * 2 * E * INTER)
        gu_raw = Placer(gu_area, "w_gu").take("raw", gu_shape, F32)
        w_r, w_r_raw = loaded_parts(nc, ctx, "w_r", [P, KD, P])
        area = Area(nc, ctx, "area", AREA)
        x_loaded = [signal(f"x_loaded{i}") for i in range(2)]
        gu_loaded, stored = signal("gu_loaded"), signal("stored")

        def first_loads(sp, part):
            if part == 0:
                sp.dma_start(X[:, 0:TT, :], x_rows[:, 0:TT, :]).then_inc(x_loaded[0], 16)
                return
            sp.dma_start(X[:, TT:NT, :], x_rows[:, TT:NT, :]).then_inc(x_loaded[1], 16)
            sp.dma_start(gu_raw[:, :, :],
                         d["Wgu"].rearrange("p (k n) -> p k n", k=KD)).then_inc(gu_loaded, 16)

        with signals(nc) as of_routing:
            routing = Routing(nc, Placer(area, "f").take, of_routing, "f_route", X, ident, w_r, d)
            lightning(nc, X, ident, ps, d, w_r, w_r_raw, routing, first_loads, x_loaded)
            w_gu = Parts(sb("w_gu_hi", gu_shape, F32R), Placer(gu_area, "w_gu").take("lo", gu_shape, F32R))
            experts(nc, X, ident, ps, d, "f", routing, w_gu, gu_raw, gu_loaded)
        with signals(nc) as of_routing:
            routing = Routing(nc, Placer(area, "g").take, of_routing, "g_route", X, ident, w_r, d)
            attention(nc, X, ident, ps, d, area, routing)
            experts(nc, X, ident, ps, d, "g", routing, w_gu, None, None)
        with nc.Block() as block:
            @block.sync
            def _(sp):
                sp.dma_start(out_rows, X[:, :, :]).then_inc(stored, 16)
                sp.wait_ge(stored, 16)


def halves(w):
    return np.ascontiguousarray(w.reshape(KD, P, -1).transpose(1, 0, 2).reshape(P, -1))


def columns(w, n):
    out = np.zeros((w.shape[0], n), w.dtype)
    out[:, :w.shape[1]] = w
    return out


def constants():
    f = np.float32
    bf16_one = np.uint16(0x3F80)
    c = {"ident": np.eye(P, dtype=f), "ident_b": np.eye(P, dtype=np.uint16) * bf16_one}
    i = np.arange(P)
    c["gap"] = np.maximum(i[None, :] - i[:, None], 0).astype(f)
    c["causal"] = (i[None, :] >= i[:, None]).astype(f)
    c["ahead"] = np.broadcast_to((i + 1).astype(f), (P, P)).copy()
    c["left"] = (P - 1 - i).astype(f)[:, None].copy()
    c["head_rows"] = (i[:, None] // HD == np.arange(P // HD)[None, :]).astype(f)
    c["diagonal"] = np.repeat(c["head_rows"], PAD, axis=1)
    row = np.arange(HT * P) // INTER
    one = (np.arange(P)[:, None] % E == row[None, :]) & (np.arange(P)[:, None] < 3 * E)
    c["spread"] = one.astype(np.uint16) * bf16_one
    scale = f(10000.0) ** (np.arange(0, HD, 2, dtype=f) / f(HD))
    angle = np.arange(N, dtype=f)[:, None] * (f(1.0) / scale)[None, :]
    sin, cos = np.sin(angle), np.cos(angle)
    for name, v in (("sin", np.concatenate([-sin, sin], 1)), ("cos", np.concatenate([cos, cos], 1))):
        c[name] = v.reshape(TT, P, HD).transpose(1, 0, 2).reshape(P, -1).astype(f)
    return {k: np.ascontiguousarray(v) for k, v in c.items()}


def layout(v):
    a = {"x": v["L0_attn_a_x"]}
    p = "L0_attn_a_"
    a["Wqkv"] = halves(np.concatenate([v[p + "Wq"], v[p + "Wk"], v[p + "Wv"]], 1))
    a["Wo"] = halves(v[p + "Wo"])
    a["Wg1"] = halves(columns(v[p + "Wg1"], P))
    a["Wg2"] = columns(v[p + "Wg2"].T, P).T
    a["norm_w"] = np.broadcast_to(v[p + "norm_w"], (P, D))
    a["ld_heads"] = np.broadcast_to(v[p + "log_decay"], (P, H))
    a["ld_rows"] = np.repeat(v[p + "log_decay"], HD).reshape(KD, P).T
    p = "L0_attn_b_"
    a["WqkvB"] = halves(np.concatenate([v[p + "Wq"], v[p + "Wk"], v[p + "Wv"]], 1))
    a["Wout"] = halves(v[p + "Wout"])
    p = "L0_ffn_"
    a["Wr"] = halves(columns(v[p + "gate_weight"].T, P))
    gu = v[p + "gate_up_proj"].reshape(E, 2, INTER, D).transpose(3, 1, 0, 2).reshape(D, -1)
    a["Wgu"] = halves(gu)
    down = v[p + "down_proj"].transpose(0, 2, 1).reshape(HT, P, D)
    a["Wdown"] = down.transpose(1, 0, 2).reshape(P, -1)
    return {k: np.ascontiguousarray(x) for k, x in a.items()}


def kernel(**inputs):
    import concourse.bacc as _bacc
    from concourse.bass_utils import run_bass_kernel_spmd as _run

    nc = _bacc.Bacc("TRN2", target_bir_lowering=False, num_devices=1, dynamic_dma_scratch_size=256)
    arrays = {**layout({k: np.asarray(v) for k, v in inputs.items()}), **constants()}
    d = {k: nc.dram_tensor(f"in_{k}", a.shape, mybir.dt.from_np(a.dtype), kind="ExternalInput").ap()
         for k, a in arrays.items()}
    out = nc.dram_tensor("out_0", (B, N, D), F32, kind="ExternalOutput").ap()
    program(nc, d, out)
    r = _run(nc, [{f"in_{k}": a for k, a in arrays.items()}], core_ids=[0])
    return r.results[0]["out_0"]
```

```python
from contextlib import ExitStack, contextmanager

import concourse.bass as bass
import numpy as np
from concourse import mybir

F32 = mybir.dt.float32
F32R = mybir.dt.float32r
ALU = mybir.AluOpType
ACT = mybir.ActivationFunctionType
AX = mybir.AxisListType

P = 128
B, N, D = 4, 512, 256
TT = N // P
NT = B * TT
KD = D // P
H, HD = 16, 16
KV = 4
G = H // KV
PAD = 32
E, TOPK, KEEP = 32, 8, 0.8
INTER = 96
HT = E * INTER // P
QKV = D + 2 * KV * HD
AREA = 2 * KD * N + 4 * TT * H * HD + TT * QKV + 3 * 4 * TT * KV * HD
PASSES = (("hi", "hi"), ("hi", "lo"), ("lo", "hi"))


@contextmanager
def signals(nc):
    given = []

    def sem(name):
        given.append(nc.alloc_semaphore(name))
        return given[-1]

    yield sem
    nc.clear_and_free_semaphores(given)
    nc.all_engine_barrier()


class Area:

    def __init__(self, nc, ctx, name, columns):
        ctx.enter_context(nc.sbuf_tensor(name, [P, columns], F32))
        self.nc, self.name, self.end = nc, name, nc.sbuf_base
        self.start = self.end - 4 * columns


class Placer:

    def __init__(self, area, use):
        self.area, self.use, self.at = area, use, area.start

    def take(self, name, shape, dt):
        size = int(np.prod(shape[1:])) * 4
        v = self.area.nc.alloc_sbuf_tensor_at(f"{self.use}_{name}", shape, dt, offset=self.at)
        self.at += (size + 31) // 32 * 32
        assert self.at <= self.area.end
        return v


def loaded_parts(nc, ctx, name, shape):
    hi = ctx.enter_context(nc.sbuf_tensor(f"{name}_hi", shape, F32R))
    area = Area(nc, ctx, f"{name}_area", int(np.prod(shape[1:])))
    return Parts(hi, Placer(area, name).take("lo", shape, F32R)), Placer(area, name).take("raw", shape, F32)


class Steps:

    def __init__(self, eng, sem, base=0):
        self.eng, self.sem, self.base, self.n = eng, sem, base, 0

    def __call__(self, ins):
        ins.then_inc(self.sem, 1)
        self.n += 1

    def settle(self):
        self.eng.wait_ge(self.sem, self.base + self.n)


class Parts:

    def __init__(self, hi, lo):
        self.hi, self.lo = hi, lo

    def __getitem__(self, i):
        return Parts(self.hi[i], self.lo[i])


def product(nc, out, stationary, moving, start, stop):
    pairs = [(s, m, sp, mp) for s, m in zip(stationary, moving) for sp, mp in PASSES]
    for i, (s, m, sp, mp) in enumerate(pairs):
        last = nc.tensor.matmul(out, s.hi if sp == "hi" else s.lo, m.hi if mp == "hi" else m.lo,
                                start=start and i == 0, stop=stop and i == len(pairs) - 1,
                                skip_group_check=True)
    return last


def lightning(nc, X, ident, ps, d, w_r, w_r_raw, routing, first_loads, x_loaded):
    HH = H // KD
    QUADS = H // 4
    UNITS = QUADS * TT
    HT2 = TT // 2
    W = HT2 * P
    STEPS_AHEAD = UNITS // 2
    DRAIN = 11
    with ExitStack() as ctx:
        signal = ctx.enter_context(signals(nc))

        def sb(n, shape, dt=F32):
            return ctx.enter_context(nc.sbuf_tensor(f"a_{n}", shape, dt))

        def sem(n):
            return signal(f"a_{n}")

        def parts(n, shape):
            return Parts(sb(n + "_hi", shape, F32R), sb(n + "_lo", shape, F32R))

        def weight(n, shape):
            return loaded_parts(nc, ctx, f"a_{n}", shape)

        w_qkv, w_qkv_raw = weight("w_qkv", [P, KD, 3 * D])
        w_o, w_o_raw = weight("w_o", [P, KD, D])
        w_g1, w_g1_raw = weight("w_g1", [P, KD, P])
        w_g2 = sb("w_g2", [P, D])
        norm_w = sb("norm_w", [P, D])
        ld_heads = sb("ld_heads", [P, H])
        ld_rows = sb("ld_rows", [P, KD])
        gap = sb("gap", [P, P])
        causal = sb("causal", [P, P])
        ahead = sb("ahead", [P, P])
        left = sb("left", [P, 1])
        head_rows = sb("head_rows", [P, HH])
        diagonal = sb("diagonal", [P, HH * PAD])
        decay = sb("decay", [P, H, P])
        q_decay = sb("q_decay", [P, KD, P])
        k_decay = sb("k_decay", [P, H])
        k_left = sb("k_left", [P, H])
        chunk_decay = sb("chunk_decay", [P, KD])
        xn = sb("xn", [P, HT2, D])
        xt = parts("xt", [P, KD, W])
        q_t = sb("q_t", [P, KD, N])
        k_t = sb("k_t", [P, KD, N])
        k_tok = sb("k_tok", [P, TT, D])
        v_pad = sb("v_pad", [P, TT, H, PAD])
        g1 = sb("g1", [P, W])
        gate = sb("gate", [P, TT, D])
        k_dec = sb("k_dec", [P, 2, D])
        q_dec = sb("q_dec", [P, 2, KD, P])
        q_mask = sb("q_mask", [P, 2, 4, P])
        weights = sb("weights", [P, 2, 4, P])
        state = sb("state", [P, 2, KD, HH * PAD])
        outer = sb("outer", [P, KD, HH * PAD])
        o_t = sb("o_t", [P, 2, N])
        og = sb("og", [P, 2, D])
        sq = sb("sq", [P, D])
        ss = sb("ss", [P, H])
        ms = sb("ms", [P, H])
        root = sb("root", [P, H])
        rrms = sb("rrms", [P, H])
        og_norm = sb("og_norm", [P, D])
        og_t = parts("og_t", [P, KD, P])

        norm = Norm(nc, sb, signal, "a_ln", xn, HT2)
        vec = sem("vec")
        early_loaded, const_loaded, late_loaded = sem("early_loaded"), sem("const_loaded"), sem("late_loaded")
        w_hi_done, w_lo_done = sem("w_hi_done"), sem("w_lo_done")
        k_left_done, decay_raw, decay_done = sem("k_left_done"), sem("decay_raw"), sem("decay_done")
        v_zero, root_set = sem("v_zero"), sem("root_set")
        q_ready, q_sb, k_ready, k_sb = sem("q_ready"), sem("q_sb"), sem("k_ready"), sem("k_sb")
        kv_ready, kv_sb = sem("kv_ready"), sem("kv_sb")
        g1_ready, g1_sb = sem("g1_ready"), sem("g1_sb")
        gate_ready, gate_sb = sem("gate_ready"), sem("gate_sb")
        dec_ready, mask_ready = sem("dec_ready"), sem("mask_ready")
        score_ready, weight_ready = sem("score_ready"), sem("weight_ready")
        outer_ready, outer_masked, state_ready = sem("outer_ready"), sem("outer_masked"), sem("state_ready")
        o_ready, o_sb, o_turned, og_ready = sem("o_ready"), sem("o_sb"), sem("o_turned"), sem("og_ready")
        sq_ready, ss_ready, ms_ready, rrms_ready = sem("sq_ready"), sem("ss_ready"), sem("ms_ready"), sem("rrms_ready")
        scaled, normed = sem("scaled"), sem("normed")
        og_turned, og_hi, og_lo = sem("og_turned"), sem("og_hi"), sem("og_lo")
        y_ready, y_added = sem("y_ready"), sem("y_added")

        bank_front, route, bank_y, bank_turned = 0, ps[:, 1, :], 2, 3
        bank_s, bank_o, bank_kv = 4, 6, 7
        ident_loaded = sem("ident_loaded")
        early = [(w_qkv, w_qkv_raw, d["Wqkv"]), (w_g1, w_g1_raw, d["Wg1"])]
        late = [(w_o, w_o_raw, d["Wo"]), (w_r, w_r_raw, d["Wr"])]
        consts = [(w_g2, d["Wg2"]), (norm_w, d["norm_w"]), (ld_heads, d["ld_heads"]), (ld_rows, d["ld_rows"]),
                  (gap, d["gap"]), (causal, d["causal"]), (ahead, d["ahead"]), (left, d["left"]),
                  (head_rows, d["head_rows"]), (diagonal, d["diagonal"])]
        block = ctx.enter_context(nc.Block())

        def some(count):
            return not isinstance(count, int) or count > 0

        def exists(chunk):
            return not isinstance(chunk, int) or 0 <= chunk < NT

        def first(b):
            return isinstance(b, int) and b == 0

        def last(b):
            return isinstance(b, int) and b == B - 1

        def batches(eng, body):
            body(0)
            with eng.Fori(1, B - 1) as b:
                body(b)
            body(B - 1)

        def route_slots(u):
            return range(u * HT // UNITS, (u + 1) * HT // UNITS)

        def next_half(u, b):
            nth = u // STEPS_AHEAD + 1
            return 2 * b + nth, nth % 2

        def front_of(s, g):
            if isinstance(g, int) and g == 0:
                return ps[:, (bank_front, bank_y, bank_turned)[(s - 1) % 3], :]
            return ps[:, bank_front, :]

        def is_next(u, b):
            return not (last(b) and u >= STEPS_AHEAD)

        def x_half(g, h, b):
            return X[:, bass.ds(b * TT + h * HT2, HT2), :]

        def split_loaded(eng, loads, loaded):
            eng.wait_ge(loaded, 16 * len(loads))
            for w, raw, _ in loads:
                nc.scalar.copy(w.hi[:, :, :], raw[:, :, :]).then_inc(w_hi_done, 1)

        def split_rest(eng, loads, before):
            for i, (w, raw, _) in enumerate(loads):
                eng.wait_ge(w_hi_done, before + i + 1)
                nc.vector.tensor_tensor(w.lo[:, :, :], raw[:, :, :], w.hi[:, :, :].bitcast(F32),
                                        ALU.subtract).then_inc(w_lo_done, 1)

        @block.sync
        def _(sp):
            first_loads(sp, 0)
            sp.dma_start(ident[:, :], d["ident"]).then_inc(ident_loaded, 16)
            for _, raw, src in early:
                sp.dma_start(raw[:, :, :], src.rearrange("p (k n) -> p k n", k=KD)).then_inc(early_loaded, 16)
            for dst, src in consts:
                sp.dma_start(dst[:, :], src).then_inc(const_loaded, 16)
            for _, raw, src in late:
                sp.dma_start(raw[:, :, :], src.rearrange("p (k n) -> p k n", k=KD)).then_inc(late_loaded, 16)
            first_loads(sp, 1)
            routing.store(sp, 0)

        @block.tensor
        def _(pe):
            def project(s, g):
                x = [xt[:, k, :] for k in range(KD)]
                front, alone = front_of(s, g), isinstance(g, int) and g == 0
                if s == 1:
                    if some(g):
                        pe.wait_ge(kv_sb, HT2 * g)
                    for k in range(KD):
                        norm.turn(pe, g, k, ident, front[:, k * W:(k + 1) * W])
                if s in (2, 3):
                    if s == 2:
                        norm.wait_low(pe, g, KD - 1)
                        pe.wait_ge(w_lo_done, len(early))
                    elif not alone:
                        pe.wait_ge(q_sb, g + 1)
                    for m in range(KD):
                        o = (s - 2) * D + m * P
                        ins = product(nc, front[:, m * W:(m + 1) * W], [w_qkv[:, k, o:o + P] for k in range(KD)],
                                      x, True, True)
                    ins.then_inc(q_ready if s == 2 else k_ready, 1)
                if s == 4:
                    if not alone:
                        pe.wait_ge(k_sb, g + 1)
                    product(nc, front[:, 0:W], [w_g1[:, k, :] for k in range(KD)], x, True,
                            True).then_inc(g1_ready, 1)
                if s in (5, 7):
                    t = (s - 5) // 2
                    if alone:
                        pe.wait_ge(q_sb if t == 0 else g1_sb, 1)
                    else:
                        pe.wait_ge(g1_sb if t == 0 else gate_sb, g + 1)
                    product(nc, front, [xt[:, k, t * P:(t + 1) * P] for k in range(KD)],
                            [w_qkv[:, k, D:3 * D] for k in range(KD)], True, True).then_inc(kv_ready, 1)
                if s == 6:
                    pe.wait_ge(g1_sb, g + 1)
                    if alone:
                        pe.wait_ge(k_sb, 1)
                    else:
                        pe.wait_ge(kv_sb, HT2 * g + 1)
                    for t in range(HT2):
                        ins = nc.tensor.matmul(front[:, t * D:(t + 1) * D], g1[:, t * P:(t + 1) * P], w_g2[:, :],
                                               start=True, stop=True)
                    ins.then_inc(gate_ready, 1)

            def scores(i, b):
                n, q = i // QUADS, i % QUADS
                pe.wait_ge(mask_ready, UNITS * b + i + 1)
                if q == 0 and n % HT2 == 0:
                    pe.wait_ge(k_sb, 2 * b + n // HT2 + 1)
                if some(UNITS * b + i - 1):
                    pe.wait_ge(weight_ready, UNITS * b + i - 1)
                nc.tensor.matmul(ps[:, bank_s + q % 2, :], k_t[:, q // 2, n * P:(n + 1) * P],
                                 q_mask[:, q % 2, :, :], start=True, stop=True).then_inc(score_ready, 1)

            def outer_product(n, b):
                pe.wait_ge(dec_ready, 2 * (TT * b + n) + 1)
                pe.wait_ge(kv_sb, TT * b + n + 1)
                if some((TT - 1) * b + n):
                    pe.wait_ge(outer_masked, (TT - 1) * b + n)
                for m in range(KD):
                    ins = nc.tensor.matmul(ps[:, bank_kv, m * HH * PAD:(m + 1) * HH * PAD],
                                           k_dec[:, n % 2, m * P:(m + 1) * P],
                                           v_pad[:, n, m * HH:(m + 1) * HH, :], start=True, stop=True)
                ins.then_inc(outer_ready, 1)

            def output(i, b):
                n, q = i // QUADS, i % QUADS
                c = TT * b + n
                if q == 0:
                    pe.wait_ge(kv_sb, c + 1)
                    if some(c):
                        pe.wait_ge(o_sb, c)
                    if n == 1:
                        pe.wait_ge(outer_masked, (TT - 1) * b + 1)
                    if n >= 2:
                        pe.wait_ge(state_ready, (TT - 2) * b + n - 1)
                    if n >= 1:
                        pe.wait_ge(dec_ready, 2 * (c + 1))
                out = ps[:, bank_o, q * P:(q + 1) * P]
                if n >= 1:
                    nc.tensor.matmul(out, state[:, n % 2, q // 2, (q % 2) * P:(q % 2 + 1) * P],
                                     q_dec[:, n % 2, q // 2, :], start=(q == 0), stop=False,
                                     skip_group_check=True)
                pe.wait_ge(weight_ready, UNITS * b + i + 1)
                for j in range(4):
                    ins = nc.tensor.matmul(out[j * PAD:(j + 1) * PAD, :], v_pad[:, n, 4 * q + j, :],
                                           weights[:, q % 2, j, :], start=(q == 0 and n == 0), stop=True,
                                           skip_group_check=True)
                if q == QUADS - 1:
                    ins.then_inc(o_ready, 1)

            def finish(n, q, b):
                c = TT * b + n
                if q == 1 and exists(c - 3):
                    pe.wait_ge(og_hi, c - 2)
                    pe.wait_ge(og_lo, c - 2)
                    pe.wait_ge(w_lo_done, len(early + late))
                    product(nc, ps[:, bank_y, D:2 * D], [og_t[:, k, :] for k in range(KD)],
                            [w_o[:, k, :] for k in range(KD)], True, True).then_inc(y_ready, 1)
                if q == 1 and exists(c - 1):
                    pe.wait_ge(o_sb, c)
                    if some(c - 1):
                        pe.wait_ge(og_ready, c - 1)
                    for j in range(QUADS):
                        ins = nc.tensor.transpose(ps[:, bank_turned, j * P:(j + 1) * P],
                                                  o_t[:, (n - 1) % 2, j * P:(j + 1) * P], ident[:, :])
                    ins.then_inc(o_turned, 1)
                if q == 3 and exists(c - 2):
                    pe.wait_ge(normed, c - 1)
                    if some(c - 2):
                        pe.wait_ge(y_added, c - 2)
                    for k in range(KD):
                        ins = nc.tensor.transpose(ps[:, bank_y, k * P:(k + 1) * P],
                                                  og_norm[:, k * P:(k + 1) * P], ident[:, :])
                    ins.then_inc(og_turned, 1)

            def body(b):
                for u in range(UNITS):
                    n, q = u // QUADS, u % QUADS
                    scores(u, b)
                    if q == 1 and n < TT - 1:
                        outer_product(n, b)
                    if u >= 1:
                        output(u - 1, b)
                    elif not first(b):
                        output(UNITS - 1, b - 1)
                    finish(n, q, b)
                    if is_next(u, b):
                        g, h = next_half(u, b)
                        project(u % STEPS_AHEAD, g)
                    if last(b):
                        for slot in route_slots(u):
                            routing.tensor(pe, slot, 0, route)

            pe.wait_ge(ident_loaded, 16)
            for s in range(STEPS_AHEAD):
                if s == 6:
                    pe.wait_ge(const_loaded, 16 * len(consts))
                project(s, 0)
            batches(pe, body)
            output(UNITS - 1, B - 1)
            for u in range(UNITS, UNITS + DRAIN):
                finish(u // QUADS, u % QUADS, B - 1)

        @block.scalar
        def _(act):
            def project(s, g, h):
                front, cols = front_of(s, g), slice(h * W, (h + 1) * W)
                if s == 1:
                    act.wait_ge(norm.turned, KD * (g + 1))
                    nc.scalar.copy(xt.hi[:, :, :],
                                   front.rearrange("p (k n) -> p k n", k=KD)).then_inc(norm.hi_ready, KD)
                if s == 2:
                    act.wait_ge(q_ready, g + 1)
                    nc.scalar.activation(q_t[:, :, cols], front.rearrange("p (m n) -> p m n", m=KD),
                                         ACT.Silu).then_inc(q_sb, 1)
                if s == 3:
                    act.wait_ge(k_ready, g + 1)
                    nc.scalar.activation(k_t[:, :, cols], front.rearrange("p (m n) -> p m n", m=KD),
                                         ACT.Silu).then_inc(k_sb, 1)
                if s == 4:
                    act.wait_ge(g1_ready, g + 1)
                    nc.scalar.copy(g1[:, :], front[:, 0:W]).then_inc(g1_sb, 1)
                if s in (5, 7):
                    t = (s - 5) // 2
                    act.wait_ge(kv_ready, HT2 * g + t + 1)
                    nc.scalar.activation(k_tok[:, HT2 * h + t, :], front[:, 0:D], ACT.Silu)
                    nc.scalar.activation(v_pad[:, HT2 * h + t, :, 0:HD],
                                         front[:, D:2 * D].rearrange("p (h e) -> p h e", e=HD),
                                         ACT.Silu).then_inc(kv_sb, 1)
                if s == 6:
                    act.wait_ge(gate_ready, g + 1)
                    nc.scalar.activation(gate[:, HT2 * h:HT2 * (h + 1), :],
                                         front.rearrange("p (t n) -> p t n", t=HT2),
                                         ACT.Sigmoid).then_inc(gate_sb, 1)

            def finish(n, q, b):
                c = TT * b + n
                if q == 0 and exists(c - 1):
                    act.wait_ge(o_ready, c)
                    if some(c - 2):
                        act.wait_ge(o_turned, c - 2)
                    nc.scalar.copy(o_t[:, (n - 1) % 2, :], ps[:, bank_o, :]).then_inc(o_sb, 1)
                if q == 3 and exists(c - 2):
                    act.wait_ge(og_turned, c - 1)
                    if some(c - 2):
                        act.wait_ge(y_ready, c - 2)
                    nc.scalar.copy(og_t.hi[:, :, :],
                                   ps[:, bank_y, 0:D].rearrange("p (k n) -> p k n", k=KD)).then_inc(og_hi, 1)

            def body(b):
                for u in range(UNITS):
                    finish(u // QUADS, u % QUADS, b)
                    if is_next(u, b):
                        g, h = next_half(u, b)
                        project(u % STEPS_AHEAD, g, h)
                    if last(b):
                        for slot in route_slots(u):
                            routing.scalar(act, slot, 0, route)

            split_loaded(act, early, early_loaded)
            for s in range(STEPS_AHEAD):
                project(s, 0, 0)
                if s == 1:
                    act.wait_ge(const_loaded, 16 * len(consts))
                    for h in range(H):
                        ins = nc.scalar.activation(decay[:, h, :], gap[:, :], ACT.Exp, scale=ld_heads[:, h:h + 1])
                    ins.then_inc(decay_raw, 1)
                    for m in range(KD):
                        nc.scalar.activation(q_decay[:, m, :], ahead[:, :], ACT.Exp, scale=ld_rows[:, m:m + 1])
                    act.wait_ge(k_left_done, 1)
                    nc.scalar.activation(k_decay[:, :], k_left[:, :], ACT.Exp)
                    nc.scalar.activation(chunk_decay[:, :], ld_rows[:, :], ACT.Exp,
                                         scale=float(P)).then_inc(decay_raw, 1)
                    act.wait_ge(v_zero, 1)
            split_loaded(act, late, late_loaded)
            batches(act, body)
            for u in range(UNITS, UNITS + DRAIN):
                finish(u // QUADS, u % QUADS, B - 1)

        @block.gpsimd
        def _(pool):
            def mask(u, b):
                n, q = u // QUADS, u % QUADS
                if q == 0 and n % HT2 == 0:
                    pool.wait_ge(q_sb, 2 * b + n // HT2 + 1)
                if some(UNITS * b + u - 1):
                    pool.wait_ge(score_ready, UNITS * b + u - 1)
                src = q_t[:, q // 2, n * P:(n + 1) * P][:, None, :].broadcast_to([P, 4, P])
                rows = head_rows[:, (q % 2) * 4:(q % 2) * 4 + 4][:, :, None].broadcast_to([P, 4, P])
                nc.gpsimd.tensor_tensor(q_mask[:, q % 2, :, :], src, rows, ALU.mult).then_inc(mask_ready, 1)

            def finish(n, q, b):
                c = TT * b + n
                if q in (0, 1) and exists(c - 2):
                    heads = slice(q * HH, (q + 1) * HH)
                    pool.wait_ge(ms_ready, c - 1)
                    if some(c - 2):
                        pool.wait_ge(scaled, c - 2)
                    nc.gpsimd.tensor_tensor(rrms[:, heads], ms[:, heads], root[:, heads],
                                            ALU.pow).then_inc(rrms_ready, 1)
                if q == 2 and exists(c - 1):
                    pool.wait_ge(og_ready, c)
                    if some(c - 1):
                        pool.wait_ge(ss_ready, c - 1)
                    nc.gpsimd.tensor_tensor(sq[:, :], og[:, (n - 1) % 2, :], og[:, (n - 1) % 2, :],
                                            ALU.mult).then_inc(sq_ready, 1)

            def body(b):
                for u in range(UNITS):
                    if u + 1 < UNITS:
                        mask(u + 1, b)
                    elif not last(b):
                        mask(0, b + 1)
                    finish(u // QUADS, u % QUADS, b)
                    if u % STEPS_AHEAD == STEPS_AHEAD - 1 and not last(b):
                        norm.invert(pool, 2 * b + u // STEPS_AHEAD + 2)
                    if last(b) and u == 1:
                        routing.norm.invert(pool, 0)

            norm.exponent(pool)
            routing.exponent(pool)
            nc.gpsimd.memset(root[:, :], -0.5).then_inc(root_set, 1)
            pool.wait_ge(root_set, 1)
            norm.invert(pool, 0)
            norm.invert(pool, 1)
            pool.wait_ge(const_loaded, 16 * len(consts))
            mask(0, 0)
            batches(pool, body)
            for u in range(UNITS, UNITS + DRAIN):
                finish(u // QUADS, u % QUADS, B - 1)

        @block.vector
        def _(dve):
            def statistics(g, h, b):
                steps = Steps(dve, vec, g * norm.steps)
                norm.statistics(dve, steps, g, x_half(g, h, b))
                assert steps.n == norm.steps

            def project(s, g, h, b):
                if s == 0:
                    norm.scale(dve, g, x_half(g, h, b))
                if s == 1:
                    dve.wait_ge(norm.hi_ready, KD * (g + 1))
                    nc.vector.tensor_tensor(xt.lo[:, :, :], front_of(s, g).rearrange("p (k n) -> p k n", k=KD),
                                            xt.hi[:, :, :].bitcast(F32), ALU.subtract).then_inc(norm.lo_ready, KD)

            def decayed(n, b):
                c = TT * b + n
                dve.wait_ge(kv_sb, c + 1)
                dve.wait_ge(q_sb, 2 * b + n // HT2 + 1)
                if some(c - 1):
                    dve.wait_ge(o_ready, c - 1)
                nc.vector.tensor_tensor(k_dec[:, n % 2, :].rearrange("p (h e) -> p h e", e=HD),
                                        k_tok[:, n, :].rearrange("p (h e) -> p h e", e=HD),
                                        k_decay[:, :, None].broadcast_to([P, H, HD]),
                                        ALU.mult).then_inc(dec_ready, 1)
                nc.vector.tensor_tensor(q_dec[:, n % 2, :, :], q_t[:, :, n * P:(n + 1) * P], q_decay[:, :, :],
                                        ALU.mult).then_inc(dec_ready, 1)

            def weigh(u, b):
                q = u % QUADS
                dve.wait_ge(score_ready, UNITS * b + u + 1)
                nc.vector.tensor_tensor(weights[:, q % 2, :, :],
                                        ps[:, bank_s + q % 2, :].rearrange("p (j c) -> p j c", j=4),
                                        decay[:, 4 * q:4 * q + 4, :], ALU.mult).then_inc(weight_ready, 1)

            def own_blocks(n, b):
                dve.wait_ge(outer_ready, (TT - 1) * b + n + 1)
                if n == 0 and not first(b):
                    dve.wait_ge(o_ready, TT * b)
                    dve.wait_ge(state_ready, (TT - 2) * b)
                if n >= 1 and some((TT - 2) * b + n - 1):
                    dve.wait_ge(state_ready, (TT - 2) * b + n - 1)
                dst = state[:, 1, :, :] if n == 0 else outer[:, :, :]
                ins = nc.vector.tensor_tensor(dst, ps[:, bank_kv, :].rearrange("p (m c) -> p m c", m=KD),
                                              diagonal[:, None, :].broadcast_to([P, KD, HH * PAD]), ALU.mult)
                ins.then_inc(outer_masked, 1)

            def next_state(n, b):
                dve.wait_ge(outer_masked, (TT - 1) * b + n + 1)
                dve.wait_ge(o_ready, TT * b + n)
                if n >= 2:
                    dve.wait_ge(state_ready, (TT - 2) * b + n - 1)
                for m in range(KD):
                    ins = nc.vector.scalar_tensor_tensor(out=state[:, (n + 1) % 2, m, :], in0=state[:, n % 2, m, :],
                                                         scalar=chunk_decay[:, m:m + 1], in1=outer[:, m, :],
                                                         op0=ALU.mult, op1=ALU.add)
                ins.then_inc(state_ready, 1)

            def finish(n, q, b):
                c = TT * b + n
                if q == 0 and exists(c - 3):
                    dve.wait_ge(og_hi, c - 2)
                    nc.vector.tensor_tensor(og_t.lo[:, :, :], ps[:, bank_y, 0:D].rearrange("p (k n) -> p k n", k=KD),
                                            og_t.hi[:, :, :].bitcast(F32), ALU.subtract).then_inc(og_lo, 1)
                if q == 2 and exists(c - 3):
                    dve.wait_ge(y_ready, c - 2)
                    x = X[:, bass.ds(c - 3, 1), :]
                    nc.vector.tensor_tensor(x, x, ps[:, bank_y, D:2 * D][:, None, :], ALU.add).then_inc(y_added, 1)
                if q == 1 and exists(c - 1):
                    dve.wait_ge(o_turned, c)
                    dve.wait_ge(gate_sb, 2 * b + (n - 1) // HT2 + 1)
                    if some(c - 2):
                        dve.wait_ge(normed, c - 2)
                    src = ps[:, bank_turned, :].rearrange("p (h e) -> p h e", e=PAD)[:, :, 0:HD]
                    nc.vector.tensor_tensor(og[:, (n - 1) % 2, :].rearrange("p (h e) -> p h e", e=HD), src,
                                            gate[:, (n - 1) % TT, :].rearrange("p (h e) -> p h e", e=HD),
                                            ALU.mult).then_inc(og_ready, 1)
                if q == 2 and exists(c - 2):
                    rows = og[:, n % 2, :].rearrange("p (h e) -> p h e", e=HD)
                    dve.wait_ge(rrms_ready, 2 * (c - 1))
                    nc.vector.tensor_tensor(rows, rows, rrms[:, :, None].broadcast_to([P, H, HD]),
                                            ALU.mult).then_inc(scaled, 1)
                    dve.wait_ge(scaled, c - 1)
                    if some(c - 2):
                        dve.wait_ge(og_turned, c - 2)
                    nc.vector.tensor_tensor(og_norm[:, :], og[:, n % 2, :], norm_w[:, :], ALU.mult).then_inc(normed, 1)
                if q == 3 and exists(c - 1):
                    dve.wait_ge(sq_ready, c)
                    nc.vector.tensor_reduce(ss[:, :], sq[:, :].rearrange("p (h e) -> p h e", e=HD),
                                            AX.X, ALU.add).then_inc(ss_ready, 1)
                    dve.wait_ge(ss_ready, c)
                    if some(c - 1):
                        dve.wait_ge(rrms_ready, 2 * (c - 1))
                    nc.vector.tensor_scalar(ms[:, :], ss[:, :], 1.0 / HD, 1e-5, ALU.mult, ALU.add).then_inc(ms_ready, 1)

            def body(b):
                done = 0
                for u in range(UNITS):
                    n, q = u // QUADS, u % QUADS
                    if q == 0:
                        decayed(n, b)
                    weigh(u, b)
                    if q == 2 and n < TT - 1:
                        own_blocks(n, b)
                    if q == 3 and 1 <= n < TT - 1:
                        next_state(n, b)
                    finish(n, q, b)
                    if is_next(u, b):
                        g, h = next_half(u, b)
                        project(u % STEPS_AHEAD, g, h, b + (1 if h == 0 else 0))
                    if u % STEPS_AHEAD == STEPS_AHEAD - 1 and not last(b):
                        if first(b) and u < STEPS_AHEAD:
                            dve.wait_ge(x_loaded[1], 16)
                        h = u // STEPS_AHEAD
                        statistics(2 * b + h + 2, h, b + 1)
                    if last(b):
                        for slot in route_slots(u):
                            done = routing.vector(dve, slot, 0, route, done)

            nc.vector.memset(v_pad[:, :, :, :], 0.0).then_inc(v_zero, 1)
            routing.set_constants()
            dve.wait_ge(x_loaded[0], 16)
            statistics(0, 0, 0)
            norm.scale(dve, 0, x_half(0, 0, 0))
            split_rest(dve, early, 0)
            project(1, 0, 0, 0)
            statistics(1, 1, 0)
            dve.wait_ge(const_loaded, 16 * len(consts))
            nc.vector.tensor_scalar(k_left[:, :], ld_heads[:, :], left[:, 0:1], None,
                                    ALU.mult).then_inc(k_left_done, 1)
            dve.wait_ge(decay_raw, 2)
            nc.vector.tensor_tensor(decay[:, :, :], decay[:, :, :], causal[:, None, :].broadcast_to([P, H, P]),
                                    ALU.mult).then_inc(decay_done, 1)
            dve.wait_ge(decay_done, 1)
            split_rest(dve, late, len(early))
            batches(dve, body)
            for u in range(UNITS, UNITS + DRAIN):
                finish(u // QUADS, u % QUADS, B - 1)


class Norm:

    def __init__(self, nc, take, signal, name, xn, tiles=TT):
        def sb(n, shape):
            return take(f"{name}_{n}", shape, F32)

        def sem(n):
            return signal(f"{name}_{n}")

        self.nc, self.xn, self.tiles = nc, xn, tiles
        self.steps = 2 * tiles + 1
        self.stats = sb("stats", [P, tiles, 6])
        self.mean_var = sb("mean_var", [P, tiles, 2])
        self.eps = sb("eps", [P, tiles])
        self.var_eps = sb("var_eps", [P, tiles])
        self.root = sb("root", [P, tiles])
        self.rstd = sb("rstd", [P, tiles])
        self.root_ready = sem("root_ready")
        self.var_ready, self.rstd_ready = sem("var_ready"), sem("rstd_ready")
        self.xn_ready, self.turned = sem("xn_ready"), sem("turned")
        self.hi_ready, self.lo_ready = sem("hi_ready"), sem("lo_ready")

    def exponent(self, eng):
        self.nc.gpsimd.memset(self.root[:, :], -0.5).then_inc(self.root_ready, 1)
        eng.wait_ge(self.root_ready, 1)

    def statistics(self, eng, steps, f, x):
        nc = self.nc
        for t in range(self.tiles):
            steps(nc.vector.bn_stats(self.stats[:, t, :], x[:, t, :]))
        steps.settle()
        steps(nc.vector.memset(self.eps[:, :], 1e-5))
        for t in range(self.tiles):
            steps(nc.vector.bn_aggr(self.mean_var[:, t, :], self.stats[:, t, :]))
        steps.settle()
        nc.vector.tensor_tensor(self.var_eps[:, :], self.mean_var[:, :, 1], self.eps[:, :],
                                ALU.add).then_inc(self.var_ready, 1)

    def invert(self, eng, f):
        eng.wait_ge(self.var_ready, f + 1)
        self.nc.gpsimd.tensor_tensor(self.rstd[:, :], self.var_eps[:, :], self.root[:, :],
                                     ALU.pow).then_inc(self.rstd_ready, 1)

    def scale(self, eng, f, x):
        if not (isinstance(f, int) and f == 0):
            eng.wait_ge(self.turned, KD * f)
        eng.wait_ge(self.rstd_ready, f + 1)
        for t in range(self.tiles):
            self.nc.vector.tensor_scalar(self.xn[:, t, :], x[:, t, :], self.mean_var[:, t, 0:1],
                                         self.rstd[:, t:t + 1], ALU.subtract, ALU.mult).then_inc(self.xn_ready, 1)

    def turn(self, eng, f, k, ident, bank):
        eng.wait_ge(self.xn_ready, self.tiles * (f + 1))
        for t in range(self.tiles):
            ins = self.nc.tensor.transpose(bank[:, t * P:(t + 1) * P], self.xn[:, t, k * P:(k + 1) * P],
                                           ident[:, :])
        ins.then_inc(self.turned, 1)

    def high(self, eng, f, k, xt, bank):
        eng.wait_ge(self.turned, KD * f + k + 1)
        self.nc.scalar.copy(xt.hi[:, k, :], bank[:, 0:self.tiles * P]).then_inc(self.hi_ready, 1)

    def low(self, eng, f, k, xt, bank):
        eng.wait_ge(self.hi_ready, KD * f + k + 1)
        self.nc.vector.tensor_tensor(xt.lo[:, k, :], bank[:, 0:self.tiles * P], xt.hi[:, k, :].bitcast(F32),
                                     ALU.subtract).then_inc(self.lo_ready, 1)

    def wait_low(self, eng, f, k):
        eng.wait_ge(self.lo_ready, KD * f + k + 1)


class Routing:

    RING = 3

    def __init__(self, nc, take, signal, name, X, ident, w_r, shares_dram):
        SENT = TOPK

        def sb(n, shape, dt=F32):
            return take(f"{name}_{n}", shape, dt)

        def sem(n):
            return signal(f"{name}_{n}")

        self.nc, self.X, self.ident, self.w_r, self.shares_dram = nc, X, ident, w_r, shares_dram
        self.xt = Parts(sb("xt_hi", [P, KD, 2 * N], F32R), sb("xt_lo", [P, KD, 2 * N], F32R))
        self.shares_t = sb("shares_t", [P, N])
        self.share_rows = sb("share_rows", [P, self.RING, N])
        self.xn = sb("xn", [P, TT, D])
        self.logit_t = sb("logit_t", [P, N])
        self.logit = sb("logit", [P, TT, E])
        self.top = sb("top", [P, TT])
        self.ex = sb("ex", [P, TT, E])
        self.den = sb("den", [P, TT])
        self.rden = sb("rden", [P, TT])
        self.prob = sb("prob", [P, TT, E + SENT])
        self.best = sb("best", [P, TT, TOPK])
        self.total = sb("total", [P, TT])
        self.total_c = sb("total_c", [P, TT])
        self.rtotal = sb("rtotal", [P, TT])
        self.renorm = sb("renorm", [P, TT, TOPK])
        self.ones = sb("ones", [P, TOPK])
        self.cum = sb("cum", [P, TT, TOPK])
        self.active = sb("active", [P, TT, TOPK])
        self.kept = sb("kept", [P, TT, TOPK])
        self.inactive = sb("inactive", [P, TT, TOPK])
        self.key = sb("key", [P, TT, TOPK])
        self.mass = sb("mass", [P, TT])
        self.mass_c = sb("mass_c", [P, TT])
        self.rmass = sb("rmass", [P, TT])
        self.rest = sb("rest", [P, TT, E + SENT])
        self.found = sb("found", [P, TT, E])
        self.share = sb("share", [P, TT, P])

        self.norm = Norm(nc, take, signal, f"{name}_ln", self.xn)
        self.VEC = self.norm.steps + 17 + 3 * TT
        self.vec = sem("vec")
        self.const_set = sem("const_set")
        self.logit_ready, self.logit_sb = sem("logit_ready"), sem("logit_sb")
        self.logit_turned, self.logit_tok = sem("logit_turned"), sem("logit_tok")
        self.shifted, self.exp_done = sem("shifted"), sem("exp_done")
        self.share_ready, self.share_turned, self.shares_sb = sem("share_ready"), sem("share_turned"), sem("shares_sb")
        self.shares_stored = sem("shares_stored")
        self.rows_loaded = [sem(f"rows_loaded{i}") for i in range(self.RING)]

    def parts(self, f):
        return self.xt[:, :, bass.ds((f % 2) * N, N)]

    def x(self, f):
        return self.X[:, bass.ds(f * TT, TT), :]

    def store(self, sp, f):
        sp.wait_ge(self.shares_sb, f + 1)
        sp.dma_start(self.shares_dram[bass.ds(f % 2, 1), :, :].rearrange("o e n -> (o e) n"),
                     self.shares_t[0:E, :]).then_inc(self.shares_stored, 16)

    def load_rows(self, sp, i, f):
        for e in range(i * P // INTER, ((i + 1) * P - 1) // INTER + 1):
            top, end = max(e * INTER - i * P, 0), min((e + 1) * INTER - i * P, P)
            src = self.shares_dram[bass.ds(f % 2, 1), e, :].broadcast_to([end - top, N])
            sp.dma_start(self.share_rows[top:end, i % self.RING, :], src).then_inc(self.rows_loaded[i % self.RING], 16)

    def wait_rows(self, eng, i, f):
        eng.wait_ge(self.rows_loaded[i % self.RING], 2 * 16 * (HT // self.RING * f + i // self.RING + 1))

    def exponent(self, pool):
        self.norm.exponent(pool)

    CONSTANTS = 3

    def set_constants(self):
        nc = self.nc
        nc.vector.memset(self.prob[:, :, E:], -1.0).then_inc(self.const_set, 1)
        nc.vector.memset(self.active[:, :, 0:1], 1.0).then_inc(self.const_set, 1)
        nc.vector.memset(self.share[:, :, E:], 0.0).then_inc(self.const_set, 1)

    def tensor(self, pe, slot, f, bank):
        nc = self.nc
        if slot == 3:
            if not (isinstance(f, int) and f == 0):
                pe.wait_ge(self.shares_sb, f)
            self.norm.turn(pe, f, 0, self.ident, bank)
        if slot == 5:
            self.norm.wait_low(pe, f, 0)
            self.norm.turn(pe, f, 1, self.ident, bank)
        if slot == 8:
            self.norm.wait_low(pe, f, 1)
            xt = self.parts(f)
            product(nc, bank, [self.w_r[:, k, :] for k in range(KD)], [xt[:, k, :] for k in range(KD)],
                    True, True).then_inc(self.logit_ready, 1)
        if slot == 10:
            pe.wait_ge(self.logit_sb, f + 1)
            for t in range(TT):
                ins = nc.tensor.transpose(bank[:, t * P:(t + 1) * P], self.logit_t[:, t * P:(t + 1) * P],
                                          self.ident[:, :])
            ins.then_inc(self.logit_turned, 1)
        if slot == 20:
            pe.wait_ge(self.share_ready, f + 1)
            for t in range(TT):
                ins = nc.tensor.transpose(bank[:, t * P:(t + 1) * P], self.share[:, t, :], self.ident[:, :])
            ins.then_inc(self.share_turned, 1)

    def scalar(self, act, slot, f, bank):
        nc = self.nc
        if slot == 3:
            self.norm.high(act, f, 0, self.parts(f), bank)
        if slot == 6:
            self.norm.high(act, f, 1, self.parts(f), bank)
        if slot == 9:
            act.wait_ge(self.logit_ready, f + 1)
            nc.scalar.copy(self.logit_t[:, :], bank).then_inc(self.logit_sb, 1)
        if slot == 11:
            act.wait_ge(self.logit_turned, f + 1)
            nc.scalar.copy(self.logit[:, :, :],
                           bank.rearrange("p (t e) -> p t e", e=P)[:, :, 0:E]).then_inc(self.logit_tok, 1)
        if slot == 13:
            act.wait_ge(self.shifted, f + 1)
            nc.scalar.activation(self.ex[:, :, :], self.found[:, :, :], ACT.Exp).then_inc(self.exp_done, 1)
        if slot == 21:
            act.wait_ge(self.share_turned, f + 1)
            if not (isinstance(f, int) and f == 0):
                act.wait_ge(self.shares_stored, 16 * f)
            nc.scalar.copy(self.shares_t[:, :], bank).then_inc(self.shares_sb, 1)

    def vector(self, dve, slot, f, bank, done):
        nc = self.nc
        steps = Steps(dve, self.vec, f * self.VEC)
        steps.n = done

        def each(v, n):
            return v[:, :, None].broadcast_to([P, TT, n])

        if slot == 0:
            self.norm.statistics(dve, steps, f, self.x(f))
        if slot == 1:
            self.norm.scale(dve, f, self.x(f))
        if slot == 4:
            self.norm.low(dve, f, 0, self.parts(f), bank)
        if slot == 7:
            self.norm.low(dve, f, 1, self.parts(f), bank)
        if slot == 12:
            dve.wait_ge(self.logit_tok, f + 1)
            steps(nc.vector.tensor_reduce(self.top[:, :], self.logit[:, :, :], AX.X, ALU.max))
            steps.settle()
            nc.vector.tensor_tensor(self.found[:, :, :], self.logit[:, :, :], each(self.top, E),
                                    ALU.subtract).then_inc(self.shifted, 1)
        if slot == 14:
            dve.wait_ge(self.const_set, self.CONSTANTS)
            dve.wait_ge(self.exp_done, f + 1)
            steps(nc.vector.tensor_reduce(self.den[:, :], self.ex[:, :, :], AX.X, ALU.add))
            steps.settle()
            steps(nc.vector.reciprocal(self.rden[:, :], self.den[:, :]))
            steps.settle()
            steps(nc.vector.tensor_tensor(self.prob[:, :, 0:E], self.ex[:, :, :], each(self.rden, E), ALU.mult))
            steps.settle()
            steps(nc.vector.memset(self.ones[:, :], 1.0))
            for t in range(TT):
                steps(nc.vector.max(self.best[:, t, :], self.prob[:, t, 0:E]))
            steps.settle()
        if slot == 15:
            steps(nc.vector.tensor_reduce(self.total[:, :], self.best[:, :, :], AX.X, ALU.add))
            steps.settle()
            steps(nc.vector.tensor_scalar(self.total_c[:, :], self.total[:, :], 1e-12, None, ALU.max))
            steps.settle()
            steps(nc.vector.reciprocal(self.rtotal[:, :], self.total_c[:, :]))
            steps.settle()
            steps(nc.vector.tensor_tensor(self.renorm[:, :, :], self.best[:, :, :], each(self.rtotal, TOPK),
                                          ALU.mult))
            steps.settle()
        if slot == 16:
            for t in range(TT):
                steps(nc.vector.tensor_tensor_scan(self.cum[:, t, :], self.ones[:, :], self.renorm[:, t, :], 0.0,
                                                   ALU.mult, ALU.add))
            steps.settle()
            steps(nc.vector.tensor_scalar(self.active[:, :, 1:TOPK], self.cum[:, :, 0:TOPK - 1], KEEP, None,
                                          ALU.is_lt))
            steps.settle()
            steps(nc.vector.tensor_tensor(self.kept[:, :, :], self.best[:, :, :], self.active[:, :, :], ALU.mult))
            steps(nc.vector.tensor_scalar(self.inactive[:, :, :], self.active[:, :, :], -1.0, None, ALU.add))
            steps.settle()
        if slot == 17:
            steps(nc.vector.tensor_reduce(self.mass[:, :], self.kept[:, :, :], AX.X, ALU.add))
            steps(nc.vector.tensor_tensor(self.key[:, :, :], self.kept[:, :, :], self.inactive[:, :, :], ALU.add))
            steps.settle()
            steps(nc.vector.tensor_scalar(self.mass_c[:, :], self.mass[:, :], 1e-12, None, ALU.max))
            for t in range(TT):
                steps(nc.vector.match_replace(self.rest[:, t, :], self.key[:, t, :], self.prob[:, t, :], 0.0))
            steps.settle()
        if slot == 18:
            steps(nc.vector.reciprocal(self.rmass[:, :], self.mass_c[:, :]))
            steps(nc.vector.tensor_tensor(self.found[:, :, :], self.prob[:, :, 0:E], self.rest[:, :, 0:E],
                                          ALU.subtract))
            steps.settle()
            if not (isinstance(f, int) and f == 0):
                dve.wait_ge(self.share_turned, f)
            nc.vector.tensor_tensor(self.share[:, :, 0:E], self.found[:, :, :], each(self.rmass, E),
                                    ALU.mult).then_inc(self.share_ready, 1)
            assert steps.n == self.VEC, steps.n
        return steps.n


def experts(nc, X, ident, ps, d, name, routing, w_gu, gu_raw, gu_loaded, out_rows=None):
    LAG = 2
    RING = LAG + 1
    AHEAD = 2
    LOADS = 8
    with ExitStack() as ctx:
        signal = ctx.enter_context(signals(nc))

        def sb(n, shape, dt=F32):
            return ctx.enter_context(nc.sbuf_tensor(f"{name}_{n}", shape, dt))

        def sem(n):
            return signal(f"{name}_{n}")

        w_d, w_d_raw = loaded_parts(nc, ctx, f"{name}_w_d", [P, HT, D])
        hidden = sb("hidden", [P, RING, N])
        h = Parts(sb("h_hi", [P, RING, N], F32R), sb("h_lo", [P, RING, N], F32R))
        gate_ready, up_ready = sem("gate_ready"), sem("up_ready")
        silu_done, gated_done, hidden_done = sem("silu_done"), sem("gated_done"), sem("hidden_done")
        h_hi_ready, h_lo_ready = sem("h_hi_ready"), sem("h_lo_ready")
        down_done, out_added, out_stored = sem("down_done"), sem("out_added"), sem("out_stored")
        down_loaded = [sem(f"down_loaded{i}") for i in range(LOADS)]
        w_hi_done, w_lo_done = sem("w_hi_done"), sem("w_lo_done")
        bank_y, bank_route = 5, ps[:, 7, :]

        split_at = {-1: [("gu", i) for i in range(AHEAD)] + [("down", 0)]}
        for i in range(HT):
            split_at[i] = [(matrix, tile) for matrix, tile in (("gu", i + AHEAD), ("down", i + 1)) if tile < HT]
        if gu_loaded is None:
            split_at = {slot: [p for p in pieces if p[0] == "down"] for slot, pieces in split_at.items()}
        order = [piece for slot in range(-1, HT) for piece in split_at[slot]]

        def piece_parts(matrix, tile):
            if matrix == "down":
                return Parts(w_d.hi[:, tile, :], w_d.lo[:, tile, :]), w_d_raw[:, tile, :]
            hi, lo, raw = (w[:, :, :].rearrange("p k (s n) -> p k s n", s=2)[:, :, :, tile * P:(tile + 1) * P]
                           for w in (w_gu.hi, w_gu.lo, gu_raw))
            return Parts(hi, lo), raw

        def wait_split(eng, matrix, tile):
            if (matrix, tile) in order:
                eng.wait_ge(w_hi_done, order.index((matrix, tile)) + 1)
                eng.wait_ge(w_lo_done, order.index((matrix, tile)) + 1)

        block = ctx.enter_context(nc.Block())

        def first(b):
            return isinstance(b, int) and b == 0

        def batches(eng, body):
            body(0, True)
            with eng.Fori(1, B - 1) as b:
                body(b, True)
            body(B - 1, False)

        @block.sync
        def _(sp):
            def body(b, route):
                for i in range(HT):
                    if i == 0:
                        sp.wait_ge(routing.shares_stored, 16 * (b + 1))
                    if i >= routing.RING or not first(b):
                        sp.wait_ge(hidden_done, HT * b + i - routing.RING + 1)
                    routing.load_rows(sp, i, b)
                    if first(b) and i == 0:
                        load_down(0)
                    if first(b) and i == routing.RING - 1:
                        for part in range(1, LOADS):
                            load_down(part)
                    if i == LAG and not first(b):
                        store_out(b - 1)
                    if route and i == HT - 1:
                        routing.store(sp, b + 1)

            def load_down(part):
                tiles = slice(part * HT // LOADS, (part + 1) * HT // LOADS)
                src = d["Wdown"].rearrange("p (t n) -> p t n", n=D)[:, tiles, :]
                sp.dma_start(w_d_raw[:, tiles, :], src).then_inc(down_loaded[part], 16)

            def store_out(b):
                if out_rows is not None:
                    sp.wait_ge(out_added, b + 1)
                    rows = bass.ds(b * TT, TT)
                    sp.dma_start(out_rows[:, rows, :], X[:, rows, :]).then_inc(out_stored, 16)

            batches(sp, body)
            store_out(B - 1)
            if out_rows is not None:
                sp.wait_ge(out_stored, 16 * B)

        @block.gpsimd
        def _(pool):
            for i, piece in enumerate(order):
                w, raw = piece_parts(*piece)
                pool.wait_ge(w_hi_done, i + 1)
                nc.gpsimd.tensor_tensor(w.lo, raw, w.hi.bitcast(F32),
                                        ALU.subtract).then_inc(w_lo_done, 1)
                if piece == ("down", 1):
                    routing.norm.invert(pool, 1)
            with pool.Fori(2, B) as f:
                routing.norm.invert(pool, f)

        @block.tensor
        def _(pe):
            def down(tile, j, b):
                pe.wait_ge(h_lo_ready, tile + 1)
                if first(b):
                    wait_split(pe, "down", j)
                if j == 0 and not first(b):
                    pe.wait_ge(out_added, b)
                for t in range(TT):
                    ins = product(nc, ps[:, bank_y + t // 2, (t % 2) * D:(t % 2 + 1) * D],
                                  [h[:, j % RING, t * P:(t + 1) * P]], [w_d[:, j, :]],
                                  j == 0 and t % 2 == 0, j == HT - 1)
                ins.then_inc(down_done, 1)

            def body(b, route):
                xt = routing.parts(b)
                x = [xt[:, k, :] for k in range(KD)]
                routing.norm.wait_low(pe, b, KD - 1)
                for i in range(HT):
                    tile = HT * b + i
                    ahead = i >= 2 or not first(b)
                    if first(b):
                        wait_split(pe, "gu", i)
                    if ahead:
                        pe.wait_ge(silu_done, tile - 1)
                    product(nc, ps[:, i % 2, :], [w_gu[:, k, i * P:(i + 1) * P] for k in range(KD)], x,
                            True, True).then_inc(gate_ready, 1)
                    if ahead:
                        pe.wait_ge(gated_done, tile - 1)
                    o = E * INTER + i * P
                    product(nc, ps[:, 2 + i % 2, :], [w_gu[:, k, o:o + P] for k in range(KD)], x,
                            True, True).then_inc(up_ready, 1)
                    if i >= LAG:
                        down(tile - LAG, i - LAG, b)
                    elif not first(b):
                        down(tile - LAG, HT + i - LAG, b - 1)
                    if route:
                        routing.tensor(pe, i, b + 1, bank_route)
                if first(b):
                    wait_split(pe, "down", HT - 1)

            batches(pe, body)
            for i in range(LAG):
                down(HT * B + i - LAG, HT + i - LAG, B - 1)

        @block.scalar
        def _(act):
            def split(slot):
                for matrix, tile in split_at[slot]:
                    if matrix == "gu" and tile == 0:
                        act.wait_ge(gu_loaded, 16)
                    if matrix == "down" and tile % (HT // LOADS) == 0:
                        act.wait_ge(down_loaded[tile // (HT // LOADS)], 16)
                    w, raw = piece_parts(matrix, tile)
                    nc.scalar.copy(w.hi, raw).then_inc(w_hi_done, 1)

            def high(tile, j):
                act.wait_ge(hidden_done, tile + 1)
                if j >= RING or not isinstance(tile, int) or tile >= RING:
                    act.wait_ge(down_done, tile - RING + 1)
                nc.scalar.copy(h.hi[:, j % RING, :], hidden[:, j % RING, :]).then_inc(h_hi_ready, 1)

            def body(b, route):
                for i in range(HT):
                    tile = HT * b + i
                    act.wait_ge(gate_ready, tile + 1)
                    if i >= RING or not first(b):
                        act.wait_ge(h_lo_ready, tile - RING + 1)
                    nc.scalar.activation(hidden[:, i % RING, :], ps[:, i % 2, :], ACT.Silu).then_inc(silu_done, 1)
                    if first(b):
                        split(i)
                    if i >= 1 or not first(b):
                        high(tile - 1, (i - 1) % HT)
                    if route:
                        routing.scalar(act, i, b + 1, bank_route)

            split(-1)
            batches(act, body)
            high(HT * B - 1, HT - 1)

        @block.vector
        def _(dve):
            def low(tile, j):
                dve.wait_ge(h_hi_ready, tile + 1)
                nc.vector.tensor_tensor(h.lo[:, j % RING, :], hidden[:, j % RING, :],
                                        h.hi[:, j % RING, :].bitcast(F32), ALU.subtract).then_inc(h_lo_ready, 1)

            def add_out(b):
                dve.wait_ge(down_done, HT * (b + 1))
                for y in range(2):
                    x = X[:, bass.ds(b * TT + 2 * y, 2), :]
                    ins = nc.vector.tensor_tensor(x, x, ps[:, bank_y + y, :].rearrange("p (t n) -> p t n", t=2),
                                                  ALU.add)
                ins.then_inc(out_added, 1)

            def body(b, route):
                done = 0
                for i in range(HT):
                    tile = HT * b + i
                    rows = hidden[:, i % RING, :]
                    if i >= 1 or not first(b):
                        low(tile - 1, (i - 1) % HT)
                    dve.wait_ge(silu_done, tile + 1)
                    dve.wait_ge(up_ready, tile + 1)
                    nc.vector.tensor_tensor(rows, ps[:, 2 + i % 2, :], rows, ALU.mult).then_inc(gated_done, 1)
                    dve.wait_ge(gated_done, tile + 1)
                    routing.wait_rows(dve, i, b)
                    nc.vector.tensor_tensor(rows, routing.share_rows[:, i % routing.RING, :], rows,
                                            ALU.mult).then_inc(hidden_done, 1)
                    if i == LAG - 1 and not first(b):
                        add_out(b - 1)
                    if route:
                        done = routing.vector(dve, i, b + 1, bank_route, done)

            batches(dve, body)
            low(HT * B - 1, HT - 1)
            add_out(B - 1)


def attention(nc, X, ident, ps, d, area, routing):
    PAIRS = H // 2
    SRC = 4 * HD
    GROUP = TT * 2
    UNITS = KV * GROUP
    ROT = D + KV * HD
    HEADS = H + KV
    LAG = 2
    RING = LAG + 1
    LATE = 6
    with ExitStack() as ctx:
        signal = ctx.enter_context(signals(nc))

        def sb(n, shape, dt=F32):
            return ctx.enter_context(nc.sbuf_tensor(f"b_{n}", shape, dt))

        def sem(n):
            return signal(f"b_{n}")

        w_qkv, w_qkv_raw = loaded_parts(nc, ctx, "b_w_qkv", [P, KD * QKV])
        wqkv = Parts(*(w.rearrange("p (k n) -> p k n", k=KD) for w in (w_qkv.hi[:, :], w_qkv.lo[:, :])))
        w_out, w_out_raw = loaded_parts(nc, ctx, "b_w_out", [P, KD, D])
        cos = sb("cos", [P, TT, HD])
        sin = sb("sin", [P, TT, HD])
        ahead = Placer(area, "b")
        xt = Parts(ahead.take("xt_hi", [P, KD, N], F32R), ahead.take("xt_lo", [P, KD, N], F32R))
        work = ahead.take("work", [P, TT * H * SRC], F32)
        raw = ahead.take("raw", [P, TT, QKV], F32)
        k_stack = ahead.take("k_stack", [P, TT * KV, 3 * SRC], F32)
        q_t = sb("q_t", [P, PAIRS, N], F32R)
        k_t = sb("k_t", [P, 2 * KV, N], F32R)
        v_pad = sb("v_pad", [P, TT, KV, PAD])
        ssq = sb("ssq", [P, 2, TT])
        mean_sq = sb("mean_sq", [P, 2, TT])
        rrms = sb("rrms", [P, 2, TT])
        root = sb("root", [P, 2, TT])
        probs = sb("probs", [P, RING, 2, N])
        enc = sb("enc", [P, N])
        rsum = sb("rsum", [P, TT, G])
        heads = sb("heads", [P, TT, D])
        heads_t = Parts(sb("heads_t_hi", [P, KD, 2 * P], F32R), sb("heads_t_lo", [P, KD, 2 * P], F32R))
        xn = work[:, 0:TT * D].rearrange("p (t n) -> p t n", t=TT)
        term1 = work[:, 0:TT * ROT].rearrange("p (t n) -> p t n", t=TT)
        term2 = work[:, TT * ROT:2 * TT * ROT].rearrange("p (t n) -> p t n", t=TT)
        squares = work[:, 2 * TT * ROT:3 * TT * ROT].rearrange("p (t n) -> p t n", t=TT)
        q_stack = work[:, :].rearrange("p (r c) -> p r c", c=SRC)

        norm = Norm(nc, sb, signal, "ln", xn)
        vec, const_loaded, zeroed, root_set = sem("vec"), sem("const_loaded"), sem("zeroed"), sem("root_set")
        qkv_ready, qkv_sb, squares_done = sem("qkv_ready"), sem("qkv_sb"), sem("squares_done")
        mean_ready, rrms_ready, rotated = sem("mean_ready"), sem("rrms_ready"), sem("rotated")
        q_hi, k_hi, q_stacked, k_stacked = sem("q_hi"), sem("k_hi"), sem("q_stacked"), sem("k_stacked")
        q_turned, k_turned, q_parts, k_parts = sem("q_turned"), sem("k_turned"), sem("q_parts"), sem("k_parts")
        v_copied = sem("v_copied")
        logits_ready, exp_done, values_done = sem("logits_ready"), sem("exp_done"), sem("values_done")
        enc_sb, enc_turned, rsum_ready, head_ready = (sem("enc_sb"), sem("enc_turned"), sem("rsum_ready"),
                                                      sem("head_ready"))
        heads_turned, heads_hi, heads_lo = sem("heads_turned"), sem("heads_hi"), sem("heads_lo")
        y_ready, y_added = sem("y_ready"), sem("y_added")
        w_loaded, w_hi_done, w_lo_done = sem("w_loaded"), sem("w_hi_done"), sem("w_lo_done")
        VEC = norm.steps + 6 * TT
        FINISH = 10
        ROUTE = 5
        bank_values, bank_out, bank_route = 6, 7, ps[:, 4, :]
        block = ctx.enter_context(nc.Block())
        consts = [(w_out_raw[:, :, :].rearrange("p k n -> p (k n)"), d["Wout"]),
                  (cos[:, :, :].rearrange("p t n -> p (t n)"), d["cos"]),
                  (sin[:, :, :].rearrange("p t n -> p (t n)"), d["sin"])]
        raw_q = raw[:, :, 0:D]
        raw_k = raw[:, :, D:ROT]
        q_rows = q_stack.rearrange("p (t h) c -> p t h c", t=TT)
        k_rows = k_stack[:, :, :].rearrange("p (t g) c -> p t g c", t=TT)

        def by_head(v):
            return v.rearrange("p t (h e) -> p t h e", e=HD)

        def first(b):
            return isinstance(b, int) and b == 0

        def last(b):
            return isinstance(b, int) and b == B - 1

        def x_of(f):
            return X[:, bass.ds(f * TT, TT), :]

        def turn_bank(f, i):
            return 0 if first(f) and i < LATE and i % 2 == 1 else 4

        def heads_bank(y, b):
            return ps[:, y if last(b) else bank_out, :]

        def project_bank(y, b):
            return ps[:, 2 + y if last(b) else bank_out, :]

        def wait_free(eng):
            eng.wait_ge(q_turned, PAIRS * B)
            eng.wait_ge(k_turned, PAIRS * B)
            eng.wait_ge(v_copied, KV * B)

        def batches(eng, body):
            body(0, True)
            with eng.Fori(1, B - 1) as b:
                body(b, True)
            body(B - 1, False)

        @block.sync
        def _(sp):
            sp.dma_start(w_qkv_raw[:, :], d["WqkvB"]).then_inc(w_loaded, 16)
            for dst, src in consts:
                sp.dma_start(dst, src).then_inc(const_loaded, 16)
            routing.store(sp, 0)

        @block.tensor
        def _(pe):
            def prepare(slot, f):
                if slot == 6:
                    if not first(f):
                        pe.wait_ge(q_parts, PAIRS * f)
                        pe.wait_ge(k_parts, PAIRS * f)
                    for k in range(KD):
                        norm.turn(pe, f, k, ident, ps[:, 4 + k, :])
                if 9 <= slot < 9 + TT:
                    t = slot - 9
                    if t == 0:
                        norm.wait_low(pe, f, KD - 1)
                        pe.wait_ge(w_lo_done, 1)
                    if t >= 2:
                        pe.wait_ge(qkv_sb, TT * f + t - 1)
                    product(nc, ps[:, 4 + t % 2, 0:QKV], [xt[:, k, t * P:(t + 1) * P] for k in range(KD)],
                            [wqkv[:, k, :] for k in range(KD)], True, True).then_inc(qkv_ready, 1)
                if 24 <= slot < 24 + LATE:
                    turn(f, slot - 24)

            def turn(f, i):
                if i == 0:
                    pe.wait_ge(qkv_sb, TT * (f + 1))
                    pe.wait_ge(q_stacked, f + 1)
                    pe.wait_ge(k_stacked, f + 1)
                elif turn_bank(f, i) == turn_bank(f, i - 1):
                    pe.wait_ge(q_parts, PAIRS * f + i)
                    pe.wait_ge(k_parts, PAIRS * f + i)
                elif i >= 2:
                    pe.wait_ge(q_parts, i - 1)
                    pe.wait_ge(k_parts, i - 1)
                for t in range(TT):
                    rows = q_stack[:, t * H + 2 * i:t * H + 2 * i + 2, :].rearrange("p r c -> p (r c)")
                    ins = nc.tensor.transpose(ps[:, turn_bank(f, i), t * P:(t + 1) * P], rows, ident[:, :])
                ins.then_inc(q_turned, 1)
                g, low = i // 2, i % 2
                for t in range(TT):
                    src = k_stack[:, t * KV + g, (1 - low) * SRC:(1 - low) * SRC + P]
                    ins = nc.tensor.transpose(ps[:, turn_bank(f, i) + 1, t * P:(t + 1) * P], src, ident[:, :])
                ins.then_inc(k_turned, 1)

            def logits(u, b):
                g, st, jp = u // GROUP, u // 2 % TT, u % 2
                if u % GROUP == 0:
                    pe.wait_ge(q_parts, PAIRS * b + 2 * g + 2)
                    pe.wait_ge(k_parts, PAIRS * b + 2 * g + 2)
                if u < 2 and first(b):
                    pe.wait_ge(q_parts, LATE)
                    pe.wait_ge(k_parts, LATE)
                if u >= 2 or not first(b):
                    pe.wait_ge(exp_done, UNITS * b + u - 1)
                for j in range(2):
                    ins = nc.tensor.matmul(ps[:, 2 * (u % 2) + j, :], k_t[:, 2 * g + j, st * P:(st + 1) * P],
                                           q_t[:, 2 * g + jp, :], start=True, stop=True)
                ins.then_inc(logits_ready, 1)

            def values(u, b):
                g, st, jp = u // GROUP, u // 2 % TT, u % 2
                if u % GROUP == 0:
                    pe.wait_ge(v_copied, KV * b + g + 1)
                    if g >= 1 or not first(b):
                        pe.wait_ge(enc_sb, KV * b + g)
                pe.wait_ge(exp_done, UNITS * b + u + 1)
                for j in range(2 * jp, 2 * jp + 2):
                    ins = nc.tensor.matmul(ps[j * PAD:(j + 1) * PAD, bank_values, :], v_pad[:, st, g, :],
                                           probs[:, u % RING, j % 2, :], start=(st == 0), stop=(st == TT - 1),
                                           skip_group_check=True)
                ins.then_inc(values_done, 1)

            def turn_values(g, b):
                pe.wait_ge(enc_sb, KV * b + g + 1)
                if g >= 1:
                    pe.wait_ge(head_ready, KV * b + g)
                elif not first(b):
                    pe.wait_ge(y_added, 2 * b)
                for t in range(TT):
                    ins = nc.tensor.transpose(ps[:, bank_out, t * P:(t + 1) * P], enc[:, t * P:(t + 1) * P],
                                              ident[:, :])
                ins.then_inc(enc_turned, 1)

            def turn_heads(y, b):
                if y == 0:
                    pe.wait_ge(head_ready, KV * (b + 1))
                if last(b):
                    pe.wait_ge(exp_done, UNITS * B)
                elif y == 1:
                    pe.wait_ge(y_added, 2 * b + 1)
                for k in range(KD):
                    for t in range(2):
                        ins = nc.tensor.transpose(heads_bank(y, b)[:, (2 * k + t) * P:(2 * k + t + 1) * P],
                                                  heads[:, 2 * y + t, k * P:(k + 1) * P], ident[:, :])
                ins.then_inc(heads_turned, 1)

            def project(y, b):
                pe.wait_ge(heads_lo, 2 * b + y + 1)
                if first(b) and y == 0:
                    pe.wait_ge(w_lo_done, 2)
                for t in range(2):
                    ins = product(nc, project_bank(y, b)[:, t * D:(t + 1) * D],
                                  [heads_t[:, k, t * P:(t + 1) * P] for k in range(KD)],
                                  [w_out[:, k, :] for k in range(KD)], True, True)
                ins.then_inc(y_ready, 1)

            def finish(slot, b):
                if slot == 3:
                    turn_values(KV - 1, b)
                if slot == 4:
                    turn_heads(0, b)
                if slot == (5 if last(b) else 7):
                    turn_heads(1, b)
                if slot == 6:
                    project(0, b)
                if slot == 9:
                    project(1, b)

            def body(b, more):
                for u in range(UNITS):
                    logits(u, b)
                    if u >= LAG:
                        values(u - LAG, b)
                    elif not first(b):
                        values(UNITS + u - LAG, b - 1)
                    if u % GROUP == 3 and u > GROUP:
                        turn_values(u // GROUP - 1, b)
                    if u in (1, 3):
                        turn(b, LATE + u // 2)
                    if not first(b):
                        finish(u, b - 1)
                    if more:
                        prepare(u, b + 1)
                    if last(b) and u >= ROUTE:
                        if u == ROUTE:
                            pe.wait_ge(q_parts, PAIRS * B)
                        routing.tensor(pe, u - ROUTE, 0, bank_route)

            for slot in range(UNITS):
                prepare(slot, 0)
            batches(pe, body)
            for u in range(UNITS - LAG, UNITS):
                values(u, B - 1)
            for slot in range(FINISH):
                finish(slot, B - 1)

        @block.scalar
        def _(act):
            def prepare(slot, f):
                if slot == 7:
                    for k in range(KD):
                        norm.high(act, f, k, xt, ps[:, 4 + k, :])
                if 10 <= slot < 10 + TT:
                    t = slot - 10
                    if t == 0 and not first(f):
                        act.wait_ge(v_copied, KV * f)
                    act.wait_ge(qkv_ready, TT * f + t + 1)
                    nc.scalar.copy(raw[:, t, :], ps[:, 4 + t % 2, 0:QKV]).then_inc(qkv_sb, 1)
                if slot == 20:
                    act.wait_ge(rotated, f + 1)
                    nc.scalar.copy(q_rows[:, :, :, 0:HD].bitcast(F32R), by_head(raw_q)).then_inc(q_hi, 1)
                if slot == 21:
                    nc.scalar.copy(q_rows[:, :, :, HD:2 * HD].bitcast(F32R), by_head(raw_q)).then_inc(q_hi, 1)
                if slot == 22:
                    for c in (0, 2):
                        nc.scalar.copy(k_rows[:, :, :, SRC + c * HD:SRC + (c + 1) * HD].bitcast(F32R),
                                       by_head(raw_k)).then_inc(k_hi, 1)
                if 25 <= slot < 25 + LATE:
                    q_out(f, slot - 25)

            def q_out(f, i):
                act.wait_ge(q_turned, PAIRS * f + i + 1)
                nc.scalar.copy(q_t[:, i, :], ps[:, turn_bank(f, i), :]).then_inc(q_parts, 1)

            def finish(slot, b):
                if slot in (5, 8):
                    y = 0 if slot == 5 else 1
                    act.wait_ge(heads_turned, 2 * b + y + 1)
                    if y == 1:
                        act.wait_ge(y_ready, 2 * b + 1)
                    nc.scalar.copy(heads_t.hi[:, :, :],
                                   heads_bank(y, b).rearrange("p (k n) -> p k n", k=KD)).then_inc(heads_hi, 1)

            def body(b, more):
                for u in range(UNITS):
                    if not first(b):
                        finish(u, b - 1)
                    if u in (2, 4):
                        q_out(b, LATE + u // 2 - 1)
                    if more:
                        prepare(u, b + 1)
                    act.wait_ge(logits_ready, UNITS * b + u + 1)
                    if u >= RING:
                        act.wait_ge(values_done, UNITS * b + u - RING + 1)
                    elif not first(b):
                        last_use = (UNITS - 1 - u) // RING * RING + u
                        act.wait_ge(values_done, UNITS * (b - 1) + last_use + 1)
                    nc.scalar.activation(probs[:, u % RING, :, :], ps[:, 2 * (u % 2):2 * (u % 2) + 2, :], ACT.Exp,
                                         scale=float(HD) ** -0.5).then_inc(exp_done, 1)
                    if last(b) and u >= ROUTE:
                        routing.scalar(act, u - ROUTE, 0, bank_route)

            act.wait_ge(w_loaded, 16)
            nc.scalar.copy(w_qkv.hi[:, :], w_qkv_raw[:, :]).then_inc(w_hi_done, 1)
            act.wait_ge(const_loaded, 16 * len(consts))
            for slot in range(UNITS):
                if slot == 22:
                    act.wait_ge(zeroed, 3)
                prepare(slot, 0)
            nc.scalar.copy(w_out.hi[:, :, :], w_out_raw[:, :, :]).then_inc(w_hi_done, 1)
            batches(act, body)
            for slot in range(FINISH):
                finish(slot, B - 1)

        @block.gpsimd
        def _(pool):
            def prepare(f):
                if not first(f):
                    norm.invert(pool, f)
                for t in range(TT):
                    pool.wait_ge(qkv_sb, TT * f + t + 1)
                    nc.gpsimd.tensor_tensor(squares[:, t, :], raw[:, t, 0:ROT], raw[:, t, 0:ROT],
                                            ALU.mult).then_inc(squares_done, 1)
                pool.wait_ge(mean_ready, f + 1)
                nc.gpsimd.tensor_tensor(rrms[:, :, :], mean_sq[:, :, :], root[:, :, :],
                                        ALU.pow).then_inc(rrms_ready, 1)

            def body(b, more):
                if more:
                    prepare(b + 1)
                if last(b):
                    wait_free(pool)
                    routing.exponent(pool)
                    routing.norm.invert(pool, 0)

            norm.exponent(pool)
            nc.gpsimd.memset(root[:, :, :], -0.5).then_inc(root_set, 1)
            norm.invert(pool, 0)
            nc.gpsimd.memset(k_stack[:, :, :], 0.0).then_inc(zeroed, 1)
            nc.gpsimd.memset(v_pad[:, :, :, :], 0.0).then_inc(zeroed, 1)
            pool.wait_ge(zeroed, 2)
            nc.gpsimd.memset(v_pad[:, :, :, HD:HD + 1], 1.0).then_inc(zeroed, 1)
            pool.wait_ge(root_set, 1)
            prepare(0)
            batches(pool, body)

        @block.vector
        def _(dve):
            half = HD // 2

            def rotate(t, f, steps):
                def table(v, o, n):
                    return v[:, t, None, o:o + n].broadcast_to([P, HEADS, n])

                rows, cos_term, sin_term = (v[:, t, 0:ROT].rearrange("p (h e) -> p h e", e=HD)
                                            for v in (raw, term1, term2))
                if first(f) and t == 0:
                    dve.wait_ge(const_loaded, 16 * len(consts))
                dve.wait_ge(qkv_sb, TT * f + t + 1)
                if t > 0 or not first(f):
                    steps.settle()
                steps(nc.vector.tensor_tensor(cos_term, rows, table(cos, 0, HD), ALU.mult))
                steps(nc.vector.tensor_tensor(sin_term[:, :, 0:half], rows[:, :, half:HD], table(sin, 0, half),
                                              ALU.mult))
                steps(nc.vector.tensor_tensor(sin_term[:, :, half:HD], rows[:, :, 0:half], table(sin, half, half),
                                              ALU.mult))
                steps.settle()

            def prepare(slot, f, done):
                steps = Steps(dve, vec, f * VEC)
                steps.n = done
                if slot == 0:
                    norm.statistics(dve, steps, f, x_of(f))
                if slot == 5:
                    if not first(f):
                        dve.wait_ge(q_turned, PAIRS * f)
                    norm.scale(dve, f, x_of(f))
                if slot == 8:
                    for k in range(KD):
                        norm.low(dve, f, k, xt, ps[:, 4 + k, :])
                if 11 <= slot < 11 + TT:
                    rotate(slot - 11, f, steps)
                if 12 <= slot < 12 + TT:
                    t = slot - 12
                    dve.wait_ge(squares_done, TT * f + t + 1)
                    steps(nc.vector.tensor_reduce(ssq[:, 0, t:t + 1], squares[:, t, 0:D], AX.X, ALU.add))
                    steps(nc.vector.tensor_reduce(ssq[:, 1, t:t + 1], squares[:, t, D:ROT], AX.X, ALU.add))
                    steps(nc.vector.tensor_tensor(raw[:, t, 0:ROT], term1[:, t, :], term2[:, t, :], ALU.add))
                if slot == 15:
                    steps.settle()
                    nc.vector.tensor_scalar(mean_sq[:, 0, :], ssq[:, 0, :], 1.0 / D, 1e-6, ALU.mult, ALU.add)
                    nc.vector.tensor_scalar(mean_sq[:, 1, :], ssq[:, 1, :], 1.0 / (KV * HD), 1e-6, ALU.mult,
                                            ALU.add).then_inc(mean_ready, 1)
                if slot == 17:
                    dve.wait_ge(rrms_ready, f + 1)
                    nc.vector.tensor_tensor(raw_q, raw_q, rrms[:, 0, :, None].broadcast_to([P, TT, D]), ALU.mult)
                    nc.vector.tensor_tensor(raw_k, raw_k, rrms[:, 1, :, None].broadcast_to([P, TT, KV * HD]),
                                            ALU.mult).then_inc(rotated, 1)
                if slot == 22:
                    dve.wait_ge(q_hi, 2 * f + 1)
                    dve.wait_ge(rotated, f + 1)
                    for c in (2, 3):
                        ins = nc.vector.tensor_tensor(q_rows[:, :, :, c * HD:(c + 1) * HD], by_head(raw_q),
                                                      q_rows[:, :, :, 0:HD], ALU.subtract)
                    ins.then_inc(q_stacked, 1)
                if slot == 23:
                    dve.wait_ge(q_hi, 2 * (f + 1))
                    dve.wait_ge(k_hi, 2 * (f + 1))
                    for c in (1, 3):
                        ins = nc.vector.tensor_tensor(k_rows[:, :, :, SRC + c * HD:SRC + (c + 1) * HD], by_head(raw_k),
                                                      k_rows[:, :, :, SRC:SRC + HD], ALU.subtract)
                    ins.then_inc(k_stacked, 1)
                    assert steps.n == VEC, steps.n
                if 25 <= slot < 25 + LATE:
                    k_out(f, slot - 25)
                if slot in (25, 26, 27):
                    copy_v(slot - 25)
                return steps.n

            def copy_v(g):
                o = ROT + g * HD
                nc.vector.tensor_copy(v_pad[:, :, g, 0:HD], raw[:, :, o:o + HD]).then_inc(v_copied, 1)

            def k_out(f, i):
                dve.wait_ge(k_turned, PAIRS * f + i + 1)
                nc.vector.tensor_copy(k_t[:, i, :], ps[:, turn_bank(f, i) + 1, :]).then_inc(k_parts, 1)

            def encode(g, b):
                dve.wait_ge(values_done, UNITS * b + GROUP * (g + 1))
                if g >= 1 or not first(b):
                    dve.wait_ge(enc_turned, KV * b + g)
                nc.vector.tensor_copy(enc[:, :], ps[:, bank_values, :]).then_inc(enc_sb, 1)

            def normalise(g, b):
                dve.wait_ge(enc_turned, KV * b + g + 1)
                if g == 0 and not first(b):
                    dve.wait_ge(heads_turned, 2 * b)
                values = ps[:, bank_out, :].rearrange("p (t j e) -> p t j e", t=TT, j=G)
                nc.vector.reciprocal(rsum[:, :, :], values[:, :, :, HD]).then_inc(rsum_ready, 1)
                dve.wait_ge(rsum_ready, KV * b + g + 1)
                nc.vector.tensor_tensor(by_head(heads[:, :, :])[:, :, g * G:(g + 1) * G, :], values[:, :, :, 0:HD],
                                        rsum[:, :, :, None].broadcast_to([P, TT, G, HD]),
                                        ALU.mult).then_inc(head_ready, 1)

            def add_out(y, b):
                dve.wait_ge(y_ready, 2 * b + y + 1)
                x = X[:, bass.ds(b * TT + 2 * y, 2), :]
                nc.vector.tensor_tensor(x, x, project_bank(y, b).rearrange("p (t n) -> p t n", t=2),
                                        ALU.add).then_inc(y_added, 1)

            def finish(slot, b):
                if slot == 1:
                    encode(KV - 1, b)
                if slot == 3:
                    normalise(KV - 1, b)
                if slot in (5, 8):
                    y = 0 if slot == 5 else 1
                    dve.wait_ge(heads_hi, 2 * b + y + 1)
                    nc.vector.tensor_tensor(heads_t.lo[:, :, :],
                                            heads_bank(y, b).rearrange("p (k n) -> p k n", k=KD),
                                            heads_t.hi[:, :, :].bitcast(F32), ALU.subtract).then_inc(heads_lo, 1)
                if slot == 6:
                    add_out(0, b)
                if slot == 9:
                    add_out(1, b)

            def body(b, more):
                done = 0
                for u in range(UNITS):
                    if u % GROUP == 1 and u > GROUP:
                        encode(u // GROUP - 1, b)
                    if u % GROUP == 4 and u > GROUP:
                        normalise(u // GROUP - 1, b)
                    if not first(b):
                        finish(u, b - 1)
                    if u == 1:
                        copy_v(KV - 1)
                    if u in (2, 4):
                        k_out(b, LATE + u // 2 - 1)
                    if more:
                        done = prepare(u, b + 1, done)
                    if last(b) and u >= ROUTE:
                        if u == ROUTE:
                            wait_free(dve)
                            routing.set_constants()
                        done = routing.vector(dve, u - ROUTE, 0, bank_route, done)

            done = 0
            for slot in range(UNITS):
                if slot == 23:
                    dve.wait_ge(zeroed, 3)
                done = prepare(slot, 0, done)
                if slot == 5:
                    dve.wait_ge(w_hi_done, 1)
                    nc.vector.tensor_tensor(w_qkv.lo[:, :], w_qkv_raw[:, :], w_qkv.hi[:, :].bitcast(F32),
                                            ALU.subtract).then_inc(w_lo_done, 1)
            dve.wait_ge(w_hi_done, 2)
            nc.vector.tensor_tensor(w_out.lo[:, :, :], w_out_raw[:, :, :], w_out.hi[:, :, :].bitcast(F32),
                                    ALU.subtract).then_inc(w_lo_done, 1)
            batches(dve, body)
            for slot in range(FINISH):
                finish(slot, B - 1)


def program(nc, d, out):
    x_rows = d["x"].rearrange("b (t p) n -> p (b t) n", p=P)
    out_rows = out.rearrange("b (t p) n -> p (b t) n", p=P)
    with ExitStack() as ctx:
        signal = ctx.enter_context(signals(nc))

        def sb(n, shape, dt=F32):
            return ctx.enter_context(nc.sbuf_tensor(n, shape, dt))

        X = sb("X", [P, NT, D])
        ident = sb("ident", [P, P])
        ps = ctx.enter_context(nc.psum_tensor("ps", [P, 8, N], F32))
        gu_shape = [P, KD, 2 * E * INTER]
        gu_area = Area(nc, ctx, "gu_area", KD * 2 * E * INTER)
        gu_raw = Placer(gu_area, "w_gu").take("raw", gu_shape, F32)
        w_r, w_r_raw = loaded_parts(nc, ctx, "w_r", [P, KD, P])
        area = Area(nc, ctx, "area", AREA)
        x_loaded = [signal(f"x_loaded{i}") for i in range(2)]
        shares_dram = nc.dram_tensor("shares", (2, E, N), F32, kind="Internal").ap()
        gu_loaded = signal("gu_loaded")

        def first_loads(sp, part):
            if part == 0:
                sp.dma_start(X[:, 0:TT, :], x_rows[:, 0:TT, :]).then_inc(x_loaded[0], 16)
                return
            sp.dma_start(X[:, TT:NT, :], x_rows[:, TT:NT, :]).then_inc(x_loaded[1], 16)
            sp.dma_start(gu_raw[:, :, :],
                         d["Wgu"].rearrange("p (k n) -> p k n", k=KD)).then_inc(gu_loaded, 16)

        with signals(nc) as of_routing:
            routing = Routing(nc, Placer(area, "f").take, of_routing, "f_route", X, ident, w_r, shares_dram)
            lightning(nc, X, ident, ps, d, w_r, w_r_raw, routing, first_loads, x_loaded)
            w_gu = Parts(sb("w_gu_hi", gu_shape, F32R), Placer(gu_area, "w_gu").take("lo", gu_shape, F32R))
            experts(nc, X, ident, ps, d, "f", routing, w_gu, gu_raw, gu_loaded)
        with signals(nc) as of_routing:
            routing = Routing(nc, Placer(area, "g").take, of_routing, "g_route", X, ident, w_r, shares_dram)
            attention(nc, X, ident, ps, d, area, routing)
            experts(nc, X, ident, ps, d, "g", routing, w_gu, None, None, out_rows)


def halves(w):
    return np.ascontiguousarray(w.reshape(KD, P, -1).transpose(1, 0, 2).reshape(P, -1))


def columns(w, n):
    out = np.zeros((w.shape[0], n), w.dtype)
    out[:, :w.shape[1]] = w
    return out


def constants():
    f = np.float32
    c = {"ident": np.eye(P, dtype=f)}
    i = np.arange(P)
    c["gap"] = np.maximum(i[None, :] - i[:, None], 0).astype(f)
    c["causal"] = (i[None, :] >= i[:, None]).astype(f)
    c["ahead"] = np.broadcast_to((i + 1).astype(f), (P, P)).copy()
    c["left"] = (P - 1 - i).astype(f)[:, None].copy()
    c["head_rows"] = (i[:, None] // HD == np.arange(P // HD)[None, :]).astype(f)
    c["diagonal"] = np.repeat(c["head_rows"], PAD, axis=1)
    scale = f(10000.0) ** (np.arange(0, HD, 2, dtype=f) / f(HD))
    angle = np.arange(N, dtype=f)[:, None] * (f(1.0) / scale)[None, :]
    sin, cos = np.sin(angle), np.cos(angle)
    for name, v in (("sin", np.concatenate([-sin, sin], 1)), ("cos", np.concatenate([cos, cos], 1))):
        c[name] = v.reshape(TT, P, HD).transpose(1, 0, 2).reshape(P, -1).astype(f)
    return {k: np.ascontiguousarray(v) for k, v in c.items()}


def layout(v):
    a = {"x": v["L0_attn_a_x"]}
    p = "L0_attn_a_"
    a["Wqkv"] = halves(np.concatenate([v[p + "Wq"], v[p + "Wk"], v[p + "Wv"]], 1))
    a["Wo"] = halves(v[p + "Wo"])
    a["Wg1"] = halves(columns(v[p + "Wg1"], P))
    a["Wg2"] = columns(v[p + "Wg2"].T, P).T
    a["norm_w"] = np.broadcast_to(v[p + "norm_w"], (P, D))
    a["ld_heads"] = np.broadcast_to(v[p + "log_decay"], (P, H))
    a["ld_rows"] = np.repeat(v[p + "log_decay"], HD).reshape(KD, P).T
    p = "L0_attn_b_"
    a["WqkvB"] = halves(np.concatenate([v[p + "Wq"], v[p + "Wk"], v[p + "Wv"]], 1))
    a["Wout"] = halves(v[p + "Wout"])
    p = "L0_ffn_"
    a["Wr"] = halves(columns(v[p + "gate_weight"].T, P))
    gu = v[p + "gate_up_proj"].reshape(E, 2, INTER, D).transpose(3, 1, 0, 2).reshape(D, -1)
    a["Wgu"] = halves(gu)
    down = v[p + "down_proj"].transpose(0, 2, 1).reshape(HT, P, D)
    a["Wdown"] = down.transpose(1, 0, 2).reshape(P, -1)
    return {k: np.ascontiguousarray(x) for k, x in a.items()}


def kernel(**inputs):
    import concourse.bacc as _bacc
    from concourse.bass_utils import run_bass_kernel_spmd as _run

    nc = _bacc.Bacc("TRN2", target_bir_lowering=False, num_devices=1, dynamic_dma_scratch_size=256)
    arrays = {**layout({k: np.asarray(v) for k, v in inputs.items()}), **constants()}
    d = {k: nc.dram_tensor(f"in_{k}", a.shape, mybir.dt.from_np(a.dtype), kind="ExternalInput").ap()
         for k, a in arrays.items()}
    out = nc.dram_tensor("out_0", (B, N, D), F32, kind="ExternalOutput").ap()
    program(nc, d, out)
    r = _run(nc, [{f"in_{k}": a for k, a in arrays.items()}], core_ids=[0])
    return r.results[0]["out_0"]
```
